# Optimizing a Trainium2 kernel written in Bass

```python
import numpy as np
import jax
import jax.numpy as jnp

def _softmax(x, axis=-1):
    return jax.nn.softmax(x, axis=axis)

def _gelu(x):
    return jax.nn.gelu(x, approximate=True)

def _silu(x):
    return jax.nn.silu(x)

def _sigmoid(x):
    return jax.nn.sigmoid(x)

def _layernorm(x, axis=-1, eps=1e-05):
    m = jnp.mean(x, axis=axis, keepdims=True)
    v = jnp.var(x, axis=axis, keepdims=True)
    return (x - m) / jnp.sqrt(v + eps)

def _scatter_add(tgt, idx, src, axis=0):
    return tgt.at[idx].add(src)

def _segment_sum(src, seg, n):
    return jax.ops.segment_sum(src, seg, n)
kernel_name = 'mk_flamingo_gated_d4_seqx_r4_a2a067'

def setup_inputs(seed: int=0):
    np.random.seed(seed)
    _w = jnp.asarray

    def _rec_inputs():
        import jax
        import jax.numpy as jnp
        _rk = jax.random.key(seed)
        x = -0.0002928 + 1 * jax.random.normal(jax.random.fold_in(_rk, 1), (16, 128, 256), jnp.float32)
        _lenS = 128 - jax.random.randint(jax.random.fold_in(_rk, 7), (16,), 0, max(1, 128 // 4) + 1, jnp.int32)
        _lenS2 = 128 - jax.random.randint(jax.random.fold_in(_rk, 8), (16,), 0, max(1, 128 // 4) + 1, jnp.int32)
        _ctx_1024P = jax.random.normal(jax.random.fold_in(_rk, 11), (16, 16, 256), jnp.float32)
        _ctx_1024c = jax.random.dirichlet(jax.random.fold_in(_rk, 511), 0.3 * jnp.ones((16,), jnp.float32), (16, 128))
        _ctx_1024t = jnp.einsum('bsk,bkd->bsd', _ctx_1024c, _ctx_1024P)
        _ctx_1024t = _ctx_1024t * jax.lax.rsqrt(jnp.mean(jnp.square(_ctx_1024t)) + 1e-12) * 0.953939
        ctx_1024 = -1.39393e-06 + 0.999914 * (_ctx_1024t + 0.3 * jax.random.normal(jax.random.fold_in(_rk, 611), (16, 128, 256), jnp.float32))
        fside_Bx1xSxS2_0 = -1.47943e-05 + 1.00017 * jax.random.normal(jax.random.fold_in(_rk, 12), (16, 1, 128, 128), jnp.float32)
        _validS = jnp.arange(128)[None, :] < _lenS[:, None]
        _validS2 = jnp.arange(128)[None, :] < _lenS2[:, None]
        _causal = jnp.tril(jnp.ones((128, 128), dtype=bool))
        mask_BxSxS2_bk0 = jnp.logical_not(jnp.broadcast_to(_validS2[:, None, :], (16, 128, 128)))
        mask_BxS2_bk0 = jnp.logical_not(jnp.broadcast_to(_validS2[:, :], (16, 128)))
        _g = jax.random.normal(jax.random.fold_in(_rk, 9001), (2, 4), jnp.float32)
        _g = jnp.sign(_g) * jnp.maximum(jnp.abs(_g), 1.0) + (_g == 0) * 1.0
        g_xattn = _g[0]
        g_ffn = _g[1]
        return (x, ctx_1024, fside_Bx1xSxS2_0, mask_BxSxS2_bk0, mask_BxS2_bk0, g_xattn, g_ffn)
    x, ctx_1024, fside_Bx1xSxS2_0, mask_BxSxS2_bk0, mask_BxS2_bk0, g_xattn, g_ffn = _rec_inputs()

    def _L0_xattn_setup():
        import jax, jax.numpy as jnp
        import numpy as np
        D_MODEL = 256
        NHEAD = 16
        D_HEAD = D_MODEL // NHEAD
        key = jax.random.key(seed)
        ks = jax.random.split(key, 11)
        B, Nq, Nk = (2, 512, 512)
        s = 1.0 / np.sqrt(D_MODEL)
        inp = {'q': jax.random.normal(ks[0], (B, Nq, D_MODEL), jnp.float32), 'k': jax.random.normal(ks[1], (B, Nk, D_MODEL), jnp.float32), 'v': jax.random.normal(ks[2], (B, Nk, D_MODEL), jnp.float32), 'Wq': jax.random.normal(ks[3], (D_MODEL, D_MODEL), jnp.float32) * s, 'bq': jnp.zeros((D_MODEL,), jnp.float32), 'Wk': jax.random.normal(ks[4], (D_MODEL, D_MODEL), jnp.float32) * s, 'bk': jnp.zeros((D_MODEL,), jnp.float32), 'Wv': jax.random.normal(ks[5], (D_MODEL, D_MODEL), jnp.float32) * s, 'bv': jnp.zeros((D_MODEL,), jnp.float32), 'Wo': jax.random.normal(ks[6], (D_MODEL, D_MODEL), jnp.float32) * s, 'bo': jnp.zeros((D_MODEL,), jnp.float32)}
        return inp
    _L0_xattn_all = _L0_xattn_setup()
    _L0_xattn_in = {k: v for k, v in _L0_xattn_all.items() if k in ('Wq', 'bq', 'Wk', 'bk', 'Wv', 'bv', 'Wo', 'bo')}
    del _L0_xattn_all

    def _L0_ffn_setup():
        import jax, jax.numpy as jnp
        import numpy as np
        S, B, H, I, E = (128, 2, 256, 704, 8)
        key = jax.random.key(seed)
        ks = jax.random.split(key, 5)
        return {'hidden_states': jax.random.normal(ks[0], (S, B, H), dtype=jnp.float32), 'router_w': jax.random.normal(ks[1], (E, H), dtype=jnp.float32) * 0.02, 'gate_w': jax.random.normal(ks[2], (E, I, H), dtype=jnp.float32) * 0.02, 'up_w': jax.random.normal(ks[3], (E, I, H), dtype=jnp.float32) * 0.02, 'down_w': jax.random.normal(ks[4], (E, H, I), dtype=jnp.float32) * 0.02}
    _L0_ffn_all = _L0_ffn_setup()
    _L0_ffn_in = {k: v for k, v in _L0_ffn_all.items() if k in ('router_w', 'gate_w', 'up_w', 'down_w')}
    del _L0_ffn_all

    def _L1_xattn_setup():
        import jax, jax.numpy as jnp
        import numpy as np
        HIDDEN = 256
        HEADS = 16
        HEAD_DIM = HIDDEN // HEADS
        B, S = (4, 512)
        key = jax.random.key(seed)
        ks = jax.random.split(key, 12)
        d = {'query': jax.random.normal(ks[0], (B, S, HIDDEN), jnp.float32), 'key': jax.random.normal(ks[1], (B, S, HIDDEN), jnp.float32), 'value': jax.random.normal(ks[2], (B, S, HIDDEN), jnp.float32), 'relative_time': jax.random.normal(ks[3], (B, 1, S, S), jnp.float32), 'attn_mask': jnp.broadcast_to(jnp.tril(jnp.ones((S, S), bool)), (B, S, S))}
        scale = 1.0 / np.sqrt(HIDDEN)
        for i, name in enumerate(['q', 'k', 'v', 'out']):
            d[f'W{name}'] = jax.random.normal(ks[4 + 2 * i], (HIDDEN, HIDDEN), jnp.float32) * scale
            d[f'b{name}'] = jax.random.normal(ks[5 + 2 * i], (HIDDEN,), jnp.float32) * 0.01
        return d
    _L1_xattn_all = _L1_xattn_setup()
    _L1_xattn_in = {k: v for k, v in _L1_xattn_all.items() if k in ('Wq', 'bq', 'Wk', 'bk', 'Wv', 'bv', 'Wout', 'bout')}
    del _L1_xattn_all

    def _L1_ffn_setup():
        import jax, jax.numpy as jnp
        import numpy as np
        DIM = 256
        INTER = 512
        E = 8
        TOPK = 2
        ROUTE_SCALE = 1.0

        def _mlp(x, w1, w2, w3):
            h = jax.nn.silu(x @ w1.T) * (x @ w3.T)
            return h @ w2.T
        key = jax.random.key(seed)
        ks = jax.random.split(key, 10)
        s_in = 0.02
        return {'x': jax.random.normal(ks[0], (4, 512, DIM), dtype=jnp.float32), 'gate_w': jax.random.normal(ks[1], (E, DIM), dtype=jnp.float32) * s_in, 'gate_bias': jax.random.normal(ks[2], (E,), dtype=jnp.float32) * 0.01, 'w1': jax.random.normal(ks[3], (E, INTER, DIM), dtype=jnp.float32) * s_in, 'w2': jax.random.normal(ks[4], (E, DIM, INTER), dtype=jnp.float32) * s_in, 'w3': jax.random.normal(ks[5], (E, INTER, DIM), dtype=jnp.float32) * s_in, 'sw1': jax.random.normal(ks[6], (INTER, DIM), dtype=jnp.float32) * s_in, 'sw2': jax.random.normal(ks[7], (DIM, INTER), dtype=jnp.float32) * s_in, 'sw3': jax.random.normal(ks[8], (INTER, DIM), dtype=jnp.float32) * s_in}
    _L1_ffn_all = _L1_ffn_setup()
    _L1_ffn_in = {k: v for k, v in _L1_ffn_all.items() if k in ('gate_w', 'gate_bias', 'w1', 'w2', 'w3', 'sw1', 'sw2', 'sw3')}
    del _L1_ffn_all

    def _L2_xattn_setup():
        import jax, jax.numpy as jnp
        import numpy as np
        D_MODEL = 256
        NUM_HEADS = 16
        D_K = D_MODEL // NUM_HEADS
        key = jax.random.key(seed)
        ks = jax.random.split(key, 8)
        B, S, D = (4, 512, D_MODEL)
        scale = 1.0 / np.sqrt(D)
        return {'query': jax.random.normal(ks[0], (B, S, D), dtype=jnp.float32), 'key': jax.random.normal(ks[1], (B, S, D), dtype=jnp.float32), 'value': jax.random.normal(ks[2], (B, S, D), dtype=jnp.float32), 'Wq': jax.random.normal(ks[3], (D, D), dtype=jnp.float32) * scale, 'bq': jnp.zeros((D,), dtype=jnp.float32), 'Wk': jax.random.normal(ks[4], (D, D), dtype=jnp.float32) * scale, 'bk': jnp.zeros((D,), dtype=jnp.float32), 'Wv': jax.random.normal(ks[5], (D, D), dtype=jnp.float32) * scale, 'bv': jnp.zeros((D,), dtype=jnp.float32), 'Wo': jax.random.normal(ks[6], (D, D), dtype=jnp.float32) * scale, 'bo': jnp.zeros((D,), dtype=jnp.float32)}
    _L2_xattn_all = _L2_xattn_setup()
    _L2_xattn_in = {k: v for k, v in _L2_xattn_all.items() if k in ('Wq', 'bq', 'Wk', 'bk', 'Wv', 'bv', 'Wo', 'bo')}
    del _L2_xattn_all

    def _L2_ffn_setup():
        import jax, jax.numpy as jnp
        import numpy as np
        T, Z, D_DIM = (8, 512, 256)
        N_EXP, P_SLOT, H = (64, 32, 256)
        LN_EPS = 1e-05
        key = jax.random.key(seed)
        k = jax.random.split(key, 5)
        s = 0.02
        return {'x': jax.random.normal(k[0], (T, Z, D_DIM), dtype=jnp.float32), 'phi_w': jax.random.normal(k[1], (N_EXP * P_SLOT, D_DIM), dtype=jnp.float32) * s, 'phi_b': jax.random.normal(k[2], (N_EXP * P_SLOT,), dtype=jnp.float32) * s, 'expert_w': jax.random.normal(k[3], (N_EXP, D_DIM, H), dtype=jnp.float32) * s, 'expert_b': jax.random.normal(k[4], (N_EXP, H), dtype=jnp.float32) * s}
    _L2_ffn_all = _L2_ffn_setup()
    _L2_ffn_in = {k: v for k, v in _L2_ffn_all.items() if k in ('phi_w', 'phi_b', 'expert_w', 'expert_b')}
    del _L2_ffn_all

    def _L3_xattn_setup():
        import jax, jax.numpy as jnp
        import numpy as np
        NUM_HEADS = 16
        HIDDEN = 256
        KEY_SIZE = 64
        VALUE_SIZE = 64
        B, S = (4, 512)

        def _split_heads(x, d):
            b, s, _ = x.shape
            return x.reshape(b, s, NUM_HEADS, d).transpose(0, 2, 1, 3)
        key = jax.random.key(seed)
        ks = jax.random.split(key, 7)
        xavier = lambda k, shp: jax.random.normal(k, shp, jnp.float32) * jnp.sqrt(2.0 / (shp[0] + shp[1]))
        return {'X_Q': jax.random.normal(ks[0], (B, S, HIDDEN), jnp.float32), 'X_KV': jax.random.normal(ks[1], (B, S, HIDDEN), jnp.float32), 'key_padding_mask': jax.random.randint(ks[2], (B, S), 0, 2).astype(bool), 'W_Q': xavier(ks[3], (HIDDEN, KEY_SIZE * NUM_HEADS)), 'W_K': xavier(ks[4], (HIDDEN, KEY_SIZE * NUM_HEADS)), 'W_V': xavier(ks[5], (HIDDEN, VALUE_SIZE * NUM_HEADS)), 'W_O': xavier(ks[6], (VALUE_SIZE * NUM_HEADS, HIDDEN))}
    _L3_xattn_all = _L3_xattn_setup()
    _L3_xattn_in = {k: v for k, v in _L3_xattn_all.items() if k in ('W_Q', 'W_K', 'W_V', 'W_O')}
    del _L3_xattn_all

    def _L3_ffn_setup():
        import jax, jax.numpy as jnp
        import numpy as np
        H = 8
        QD = 64
        HALF = QD // 2
        DIMS = (32, 32)
        TOPK = 16
        DTK = 4
        EPS_BN = 1e-05
        EPS_NORM = 1e-12

        def _l2norm(x):
            n = jnp.linalg.norm(x, axis=-1, keepdims=True)
            return x / jnp.maximum(n, EPS_NORM)
        key = jax.random.key(seed)
        ks = jax.random.split(key, 6)
        B, S, D, O, E = (2, 128, 256, 256, 256)
        hidden_states = jax.random.normal(ks[0], (B, S, D), jnp.float32)
        Wq = jax.random.normal(ks[1], (D, H * QD), jnp.float32) * 0.02
        bq = jnp.zeros((H * QD,), jnp.float32)
        bn_gamma = jnp.ones((QD,), jnp.float32)
        bn_beta = jnp.zeros((QD,), jnp.float32)
        sub_key0 = jax.random.normal(ks[2], (DIMS[0], HALF), jnp.float32) * 0.02
        sub_key1 = jax.random.normal(ks[3], (DIMS[1], HALF), jnp.float32) * 0.02
        expert_down = jax.random.normal(ks[4], (E, D), jnp.float32) * 0.02
        expert_up = jax.random.normal(ks[5], (E, O), jnp.float32) * 0.02
        return {'hidden_states': hidden_states, 'Wq': Wq, 'bq': bq, 'bn_gamma': bn_gamma, 'bn_beta': bn_beta, 'sub_key0': sub_key0, 'sub_key1': sub_key1, 'expert_down': expert_down, 'expert_up': expert_up}
    _L3_ffn_all = _L3_ffn_setup()
    _L3_ffn_in = {k: v for k, v in _L3_ffn_all.items() if k in ('Wq', 'bq', 'bn_gamma', 'bn_beta', 'sub_key0', 'sub_key1', 'expert_down', 'expert_up')}
    del _L3_ffn_all
    return {'x': x, 'ctx_1024': ctx_1024, 'fside_Bx1xSxS2_0': fside_Bx1xSxS2_0, 'mask_BxSxS2_bk0': mask_BxSxS2_bk0, 'mask_BxS2_bk0': mask_BxS2_bk0, 'g_xattn': g_xattn, 'g_ffn': g_ffn, 'L0_xattn_Wq': _L0_xattn_in['Wq'], 'L0_xattn_bq': _L0_xattn_in['bq'], 'L0_xattn_Wk': _L0_xattn_in['Wk'], 'L0_xattn_bk': _L0_xattn_in['bk'], 'L0_xattn_Wv': _L0_xattn_in['Wv'], 'L0_xattn_bv': _L0_xattn_in['bv'], 'L0_xattn_Wo': _L0_xattn_in['Wo'], 'L0_xattn_bo': _L0_xattn_in['bo'], 'L0_ffn_router_w': _L0_ffn_in['router_w'], 'L0_ffn_gate_w': _L0_ffn_in['gate_w'], 'L0_ffn_up_w': _L0_ffn_in['up_w'], 'L0_ffn_down_w': _L0_ffn_in['down_w'], 'L1_xattn_Wq': _L1_xattn_in['Wq'], 'L1_xattn_bq': _L1_xattn_in['bq'], 'L1_xattn_Wk': _L1_xattn_in['Wk'], 'L1_xattn_bk': _L1_xattn_in['bk'], 'L1_xattn_Wv': _L1_xattn_in['Wv'], 'L1_xattn_bv': _L1_xattn_in['bv'], 'L1_xattn_Wout': _L1_xattn_in['Wout'], 'L1_xattn_bout': _L1_xattn_in['bout'], 'L1_ffn_gate_w': _L1_ffn_in['gate_w'], 'L1_ffn_gate_bias': _L1_ffn_in['gate_bias'], 'L1_ffn_w1': _L1_ffn_in['w1'], 'L1_ffn_w2': _L1_ffn_in['w2'], 'L1_ffn_w3': _L1_ffn_in['w3'], 'L1_ffn_sw1': _L1_ffn_in['sw1'], 'L1_ffn_sw2': _L1_ffn_in['sw2'], 'L1_ffn_sw3': _L1_ffn_in['sw3'], 'L2_xattn_Wq': _L2_xattn_in['Wq'], 'L2_xattn_bq': _L2_xattn_in['bq'], 'L2_xattn_Wk': _L2_xattn_in['Wk'], 'L2_xattn_bk': _L2_xattn_in['bk'], 'L2_xattn_Wv': _L2_xattn_in['Wv'], 'L2_xattn_bv': _L2_xattn_in['bv'], 'L2_xattn_Wo': _L2_xattn_in['Wo'], 'L2_xattn_bo': _L2_xattn_in['bo'], 'L2_ffn_phi_w': _L2_ffn_in['phi_w'], 'L2_ffn_phi_b': _L2_ffn_in['phi_b'], 'L2_ffn_expert_w': _L2_ffn_in['expert_w'], 'L2_ffn_expert_b': _L2_ffn_in['expert_b'], 'L3_xattn_W_Q': _L3_xattn_in['W_Q'], 'L3_xattn_W_K': _L3_xattn_in['W_K'], 'L3_xattn_W_V': _L3_xattn_in['W_V'], 'L3_xattn_W_O': _L3_xattn_in['W_O'], 'L3_ffn_Wq': _L3_ffn_in['Wq'], 'L3_ffn_bq': _L3_ffn_in['bq'], 'L3_ffn_bn_gamma': _L3_ffn_in['bn_gamma'], 'L3_ffn_bn_beta': _L3_ffn_in['bn_beta'], 'L3_ffn_sub_key0': _L3_ffn_in['sub_key0'], 'L3_ffn_sub_key1': _L3_ffn_in['sub_key1'], 'L3_ffn_expert_down': _L3_ffn_in['expert_down'], 'L3_ffn_expert_up': _L3_ffn_in['expert_up']}

def reference(x, ctx_1024, fside_Bx1xSxS2_0, mask_BxSxS2_bk0, mask_BxS2_bk0, g_xattn, g_ffn, L0_xattn_Wq, L0_xattn_bq, L0_xattn_Wk, L0_xattn_bk, L0_xattn_Wv, L0_xattn_bv, L0_xattn_Wo, L0_xattn_bo, L0_ffn_router_w, L0_ffn_gate_w, L0_ffn_up_w, L0_ffn_down_w, L1_xattn_Wq, L1_xattn_bq, L1_xattn_Wk, L1_xattn_bk, L1_xattn_Wv, L1_xattn_bv, L1_xattn_Wout, L1_xattn_bout, L1_ffn_gate_w, L1_ffn_gate_bias, L1_ffn_w1, L1_ffn_w2, L1_ffn_w3, L1_ffn_sw1, L1_ffn_sw2, L1_ffn_sw3, L2_xattn_Wq, L2_xattn_bq, L2_xattn_Wk, L2_xattn_bk, L2_xattn_Wv, L2_xattn_bv, L2_xattn_Wo, L2_xattn_bo, L2_ffn_phi_w, L2_ffn_phi_b, L2_ffn_expert_w, L2_ffn_expert_b, L3_xattn_W_Q, L3_xattn_W_K, L3_xattn_W_V, L3_xattn_W_O, L3_ffn_Wq, L3_ffn_bq, L3_ffn_bn_gamma, L3_ffn_bn_beta, L3_ffn_sub_key0, L3_ffn_sub_key1, L3_ffn_expert_down, L3_ffn_expert_up):
    import jax
    import jax.numpy as jnp

    def _L0_xattn_ref(q, k, v, Wq, bq, Wk, bk, Wv, bv, Wo, bo):
        import jax, jax.numpy as jnp
        import numpy as np
        D_MODEL = 256
        NHEAD = 16
        D_HEAD = D_MODEL // NHEAD
        B, Nq, _ = q.shape
        Nk = k.shape[1]
        Q = q @ Wq + bq
        K = k @ Wk + bk
        V = v @ Wv + bv
        Q = Q.reshape(B, Nq, NHEAD, D_HEAD).transpose(0, 2, 1, 3)
        K = K.reshape(B, Nk, NHEAD, D_HEAD).transpose(0, 2, 1, 3)
        V = V.reshape(B, Nk, NHEAD, D_HEAD).transpose(0, 2, 1, 3)
        scores = jnp.einsum('bhqd,bhkd->bhqk', Q, K) / jnp.sqrt(jnp.float32(D_HEAD))
        attn = jax.nn.softmax(scores, axis=-1)
        context = jnp.einsum('bhqk,bhkd->bhqd', attn, V)
        context = context.transpose(0, 2, 1, 3).reshape(B, Nq, D_MODEL)
        out = context @ Wo + bo
        return out

    def _L0_ffn_ref(hidden_states, router_w, gate_w, up_w, down_w):
        import jax, jax.numpy as jnp
        import numpy as np
        S, B, H, I, E = (128, 2, 256, 704, 8)
        router_logits = jnp.einsum('sbh,eh->sbe', hidden_states, router_w)
        routing_indices = jnp.argmax(router_logits, axis=-1)
        out = jnp.zeros_like(hidden_states)
        for e in range(E):
            mask = (routing_indices == e)[..., None]
            xe = jnp.where(mask, hidden_states, 0.0)
            g = jnp.einsum('sbh,ih->sbi', xe, gate_w[e])
            u = jnp.einsum('sbh,ih->sbi', xe, up_w[e])
            ye = jnp.einsum('sbi,hi->sbh', jax.nn.silu(g) * u, down_w[e])
            out = out + jnp.where(mask, ye, 0.0)
        return out

    def _L1_xattn_ref(query, key, value, relative_time, attn_mask, Wq, bq, Wk, bk, Wv, bv, Wout, bout):
        import jax, jax.numpy as jnp
        import numpy as np
        HIDDEN = 256
        HEADS = 16
        HEAD_DIM = HIDDEN // HEADS
        B, S = (4, 512)
        Bsz, Slen, _ = query.shape
        Q = query @ Wq.T + bq
        K = key @ Wk.T + bk
        V = value @ Wv.T + bv
        Q = Q.reshape(Bsz, Slen, HEADS, HEAD_DIM).transpose(0, 2, 1, 3)
        K = K.reshape(Bsz, Slen, HEADS, HEAD_DIM).transpose(0, 2, 1, 3)
        V = V.reshape(Bsz, Slen, HEADS, HEAD_DIM).transpose(0, 2, 1, 3)
        scale = HEAD_DIM ** (-0.5)
        scores = jnp.einsum('bhqd,bhkd->bhqk', Q, K)
        scores = (scores + relative_time) * scale
        scores = jnp.where(attn_mask[:, None, :, :], scores, -jnp.inf)
        attn = jax.nn.softmax(scores, axis=-1)
        attn = jnp.nan_to_num(attn, nan=0.0)
        out = jnp.einsum('bhqk,bhkd->bhqd', attn, V)
        out = out.transpose(0, 2, 1, 3).reshape(Bsz, Slen, HIDDEN)
        return out @ Wout.T + bout

    def _L1_ffn_ref(x, gate_w, gate_bias, w1, w2, w3, sw1, sw2, sw3):
        import jax, jax.numpy as jnp
        import numpy as np
        DIM = 256
        INTER = 512
        E = 8
        TOPK = 2
        ROUTE_SCALE = 1.0

        def _mlp(x, w1, w2, w3):
            h = jax.nn.silu(x @ w1.T) * (x @ w3.T)
            return h @ w2.T
        shape = x.shape
        xt = x.reshape(-1, DIM)
        T = xt.shape[0]
        logits = xt @ gate_w.T
        scores = jax.nn.softmax(logits.astype(jnp.float32), axis=-1)
        original_scores = scores
        biased = scores + gate_bias
        _, indices = jax.lax.top_k(biased, TOPK)
        weights = jnp.take_along_axis(original_scores, indices, axis=1)
        weights = (weights * ROUTE_SCALE).astype(x.dtype)
        combine = (jax.nn.one_hot(indices, E, dtype=weights.dtype) * weights[..., None]).sum(axis=1)
        y = jnp.zeros_like(xt)
        for e in range(E):
            y = y + _mlp(xt, w1[e], w2[e], w3[e]) * combine[:, e:e + 1]
        z = _mlp(xt, sw1, sw2, sw3)
        return (y + z).reshape(shape)

    def _L2_xattn_ref(query, key, value, Wq, bq, Wk, bk, Wv, bv, Wo, bo):
        import jax, jax.numpy as jnp
        import numpy as np
        D_MODEL = 256
        NUM_HEADS = 16
        D_K = D_MODEL // NUM_HEADS
        B, S, D = query.shape
        H, dk = (NUM_HEADS, D_K)

        def proj(x, W, b):
            y = jnp.einsum('bsd,ed->bse', x, W) + b
            return y.reshape(B, -1, H, dk).transpose(0, 2, 1, 3)
        Q = proj(query, Wq, bq)
        K = proj(key, Wk, bk)
        V = proj(value, Wv, bv)
        scores = jnp.einsum('bhqd,bhkd->bhqk', Q, K) / np.sqrt(dk).astype(jnp.float32)
        attn = jax.nn.softmax(scores, axis=-1)
        out = jnp.einsum('bhqk,bhkd->bhqd', attn, V)
        out = out.transpose(0, 2, 1, 3).reshape(B, -1, D)
        return jnp.einsum('bsd,ed->bse', out, Wo) + bo

    def _L2_ffn_ref(x, phi_w, phi_b, expert_w, expert_b):
        import jax, jax.numpy as jnp
        import numpy as np
        T, Z, D_DIM = (8, 512, 256)
        N_EXP, P_SLOT, H = (64, 32, 256)
        LN_EPS = 1e-05
        t, z, d = x.shape
        n = expert_w.shape[0]
        p = phi_w.shape[0] // n
        logits = (jnp.einsum('tzd,ed->tze', x, phi_w) + phi_b).reshape(t, z, n, p)
        D = jax.nn.softmax(logits, axis=3)
        C = jax.nn.softmax(logits, axis=2)
        X_tilde = jnp.einsum('tznp,tzd->npd', D, x)
        X_tilde = jnp.clip(X_tilde, -33000.0, 65000.0)
        mu = jnp.mean(X_tilde, axis=-1, keepdims=True)
        var = jnp.mean(jnp.square(X_tilde - mu), axis=-1, keepdims=True)
        X_tilde = (X_tilde - mu) * jax.lax.rsqrt(var + LN_EPS)
        X_tilde = jnp.tanh(X_tilde)
        Y_tilde = jnp.einsum('npd,ndH->npH', X_tilde, expert_w) + expert_b[:, None, :]
        Y = jnp.einsum('tznp,npH->tzH', C, Y_tilde)
        return Y

    def _L3_xattn_ref(X_Q, X_KV, key_padding_mask, W_Q, W_K, W_V, W_O):
        import jax, jax.numpy as jnp
        import numpy as np
        NUM_HEADS = 16
        HIDDEN = 256
        KEY_SIZE = 64
        VALUE_SIZE = 64
        B, S = (4, 512)

        def _split_heads(x, d):
            b, s, _ = x.shape
            return x.reshape(b, s, NUM_HEADS, d).transpose(0, 2, 1, 3)
        Q = _split_heads(X_Q @ W_Q, KEY_SIZE)
        K = _split_heads(X_KV @ W_K, KEY_SIZE)
        V = _split_heads(X_KV @ W_V, VALUE_SIZE)
        E = jnp.einsum('bhqd,bhkd->bhqk', Q, K)
        E = jnp.where(key_padding_mask[:, None, None, :], -jnp.inf, E)
        A = jax.nn.softmax(E / jnp.sqrt(jnp.float32(KEY_SIZE)), axis=-1)
        Yp = jnp.einsum('bhqk,bhkd->bhqd', A, V)
        b, h, sq, dv = Yp.shape
        Y = Yp.transpose(0, 2, 1, 3).reshape(b, sq, h * dv) @ W_O
        return Y

    def _L3_ffn_ref(hidden_states, Wq, bq, bn_gamma, bn_beta, sub_key0, sub_key1, expert_down, expert_up):
        import jax, jax.numpy as jnp
        import numpy as np
        H = 8
        QD = 64
        HALF = QD // 2
        DIMS = (32, 32)
        TOPK = 16
        DTK = 4
        EPS_BN = 1e-05
        EPS_NORM = 1e-12

        def _l2norm(x):
            n = jnp.linalg.norm(x, axis=-1, keepdims=True)
            return x / jnp.maximum(n, EPS_NORM)
        B, S, D = hidden_states.shape
        q = (hidden_states @ Wq + bq).reshape(B, S, H, QD)
        mean = q.mean(axis=(0, 1, 2))
        var = q.var(axis=(0, 1, 2))
        q = (q - mean) / jnp.sqrt(var + EPS_BN) * bn_gamma + bn_beta
        q0 = _l2norm(q[..., :HALF])
        q1 = _l2norm(q[..., HALF:])
        k0 = _l2norm(sub_key0)
        k1 = _l2norm(sub_key1)
        s0 = jnp.einsum('bshq,kq->bshk', q0, k0)
        s1 = jnp.einsum('bshq,kq->bshk', q1, k1)
        ts0, ti0 = jax.lax.top_k(s0, DTK)
        ts1, ti1 = jax.lax.top_k(s1, DTK)
        comb_s = (ts0[..., :, None] + ts1[..., None, :]).reshape(B, S, H, DTK * DTK)
        comb_i = (ti0[..., :, None] * DIMS[1] + ti1[..., None, :]).reshape(B, S, H, DTK * DTK)
        top_s, pos = jax.lax.top_k(comb_s, TOPK)
        idx = jnp.take_along_axis(comb_i, pos, axis=-1)
        w = jax.nn.softmax(top_s, axis=-1)
        down = expert_down[idx]
        up = expert_up[idx]
        eh = jnp.einsum('bshkd,bsd->bshk', down, hidden_states)
        eh = jax.nn.gelu(eh, approximate=False)
        out = jnp.einsum('bshko,bshk->bso', up, eh * w)
        return out
    x = x + jnp.tanh(g_xattn[0]) * _L0_xattn_ref(_layernorm(x, axis=-1), ctx_1024, ctx_1024, L0_xattn_Wq, L0_xattn_bq, L0_xattn_Wk, L0_xattn_bk, L0_xattn_Wv, L0_xattn_bv, L0_xattn_Wo, L0_xattn_bo)
    x = x + jnp.tanh(g_ffn[0]) * _L0_ffn_ref(_layernorm(x, axis=-1), L0_ffn_router_w, L0_ffn_gate_w, L0_ffn_up_w, L0_ffn_down_w)
    x = x + jnp.tanh(g_xattn[1]) * _L1_xattn_ref(_layernorm(x, axis=-1), ctx_1024, ctx_1024, fside_Bx1xSxS2_0, mask_BxSxS2_bk0, L1_xattn_Wq, L1_xattn_bq, L1_xattn_Wk, L1_xattn_bk, L1_xattn_Wv, L1_xattn_bv, L1_xattn_Wout, L1_xattn_bout)
    x = x + jnp.tanh(g_ffn[1]) * _L1_ffn_ref(_layernorm(x, axis=-1), L1_ffn_gate_w, L1_ffn_gate_bias, L1_ffn_w1, L1_ffn_w2, L1_ffn_w3, L1_ffn_sw1, L1_ffn_sw2, L1_ffn_sw3)
    x = x + jnp.tanh(g_xattn[2]) * _L2_xattn_ref(_layernorm(x, axis=-1), ctx_1024, ctx_1024, L2_xattn_Wq, L2_xattn_bq, L2_xattn_Wk, L2_xattn_bk, L2_xattn_Wv, L2_xattn_bv, L2_xattn_Wo, L2_xattn_bo)
    x = x + jnp.tanh(g_ffn[2]) * _L2_ffn_ref(_layernorm(x, axis=-1), L2_ffn_phi_w, L2_ffn_phi_b, L2_ffn_expert_w, L2_ffn_expert_b)
    x = x + jnp.tanh(g_xattn[3]) * _L3_xattn_ref(_layernorm(x, axis=-1), ctx_1024, mask_BxS2_bk0, L3_xattn_W_Q, L3_xattn_W_K, L3_xattn_W_V, L3_xattn_W_O)
    x = x + jnp.tanh(g_ffn[3]) * _L3_ffn_ref(_layernorm(x, axis=-1), L3_ffn_Wq, L3_ffn_bq, L3_ffn_bn_gamma, L3_ffn_bn_beta, L3_ffn_sub_key0, L3_ffn_sub_key1, L3_ffn_expert_down, L3_ffn_expert_up)
    return x

_drawn_inputs = setup_inputs


def setup_inputs(seed=0):
    import zlib

    import numpy as np

    out = dict(_drawn_inputs(seed))
    spreads = {'L0_xattn_bq': (0.0, 0.544),
     'L0_xattn_bk': (0.0, 2.0),
     'L0_xattn_bv': (0.0, 0.1),
     'L0_xattn_bo': (0.0, 0.1),
     'L2_xattn_bq': (0.0, 2.0),
     'L2_xattn_bk': (0.0, 2.0),
     'L2_xattn_bv': (0.0, 0.711),
     'L2_xattn_bo': (0.0, 0.667),
     'L3_ffn_bq': (0.0, 2.0),
     'L3_ffn_bn_gamma': (1.0, 0.6),
     'L3_ffn_bn_beta': (0.0, 2.0)}
    factors = {'g_ffn': 8.0,
     'L0_ffn_router_w': 3.967,
     'L0_ffn_gate_w': 3.749,
     'L0_ffn_up_w': 3.716,
     'L0_ffn_down_w': 3.712,
     'L1_xattn_bq': 8.0,
     'L1_xattn_bk': 200.0,
     'L1_xattn_bv': 3.568,
     'L1_xattn_bout': 3.591,
     'L1_ffn_gate_w': 8.0,
     'L1_ffn_gate_bias': 8.0,
     'L1_ffn_w1': 8.0,
     'L1_ffn_w2': 8.0,
     'L1_ffn_w3': 8.0,
     'L1_ffn_sw1': 3.625,
     'L1_ffn_sw2': 3.533,
     'L1_ffn_sw3': 3.493,
     'L2_ffn_phi_b': 64.0,
     'L3_ffn_Wq': 200.0,
     'L3_ffn_sub_key0': 200.0,
     'L3_ffn_sub_key1': 200.0,
     'L3_ffn_expert_down': 12.457,
     'L3_ffn_expert_up': 8.725,
     'L2_xattn_Wq': 3.912,
     'L2_xattn_Wk': 3.369,
     'L2_ffn_phi_w': 8.0,
     'L2_ffn_expert_b': 8.0,
     'L3_xattn_W_Q': 8.0,
     'L3_xattn_W_K': 8.0}
    for name, (base, spread) in spreads.items():
        noise = np.random.default_rng([zlib.crc32(name.encode()), seed]).standard_normal(out[name].shape)
        drawn = base * np.exp(spread * noise) if base else spread * noise
        out[name] = jnp.asarray(drawn.astype(out[name].dtype))
    for name, factor in factors.items():
        out[name] = (out[name] * factor).astype(out[name].dtype)
    return out
```

```python
import numpy as np
import concourse.bass as bass
from concourse import mybir

F32, BF16, I32, U8 = mybir.dt.float32, mybir.dt.bfloat16, mybir.dt.int32, mybir.dt.uint8
ALU, ACT, AX = mybir.AluOpType, mybir.ActivationFunctionType, mybir.AxisListType

P = 128
B, S, D = 16, 128, 256
T = B * S
KD = D // P
HEADS = 16
EPS = 1e-5
BIG = 2.0 ** 100
E0, I0 = 8, 704
E1, I1 = 8, 512
SLOTS = 2048
NEXP, PSLOT = 64, 32
ST = SLOTS // P
QH, QD, NKEY, TOPK = 8, 64, 32, 4


class Lane:

    def __init__(self, engine, semaphore):
        self.engine, self.semaphore = engine, semaphore
        self.count, self.waited = 0, {}

    def wait(self, *events):
        for event in events:
            if event is None:
                continue
            semaphore, value = event
            if self.waited.get(semaphore.num, 0) < value:
                self.engine.wait_ge(semaphore, value)
                self.waited[semaphore.num] = value

    def done(self, instruction):
        self.count += 1
        instruction.then_inc(self.semaphore, 1)
        return (self.semaphore, self.count)

    @property
    def last(self):
        return (self.semaphore, self.count) if self.count else None


class Arrivals:

    def __init__(self, semaphore):
        self.semaphore, self.count = semaphore, 0

    def of(self, dma):
        self.count += 16
        dma.then_inc(self.semaphore, 16)
        return (self.semaphore, self.count)


class Ring:

    def __init__(self, buffers):
        self.buffers, self.freed, self.at = buffers, [None] * len(buffers), -1

    def take(self):
        self.at = (self.at + 1) % len(self.buffers)
        return self.at, self.buffers[self.at], self.freed[self.at]

    def release(self, n, *events):
        self.freed[n] = events[0] if len(events) == 1 else events


def events_of(freed):
    if freed is None:
        return ()
    return freed if isinstance(freed[0], tuple) else (freed,)


class Core:
    def __init__(self, nc, d, out):
        self.nc, self.d, self.out = nc, d, out
        self.pe = Lane(nc.tensor, nc.alloc_semaphore("pe_done"))
        self.act = Lane(nc.scalar, nc.alloc_semaphore("act_done"))
        self.dve = Lane(nc.vector, nc.alloc_semaphore("dve_done"))
        self.pool = Lane(nc.gpsimd, nc.alloc_semaphore("pool_done"))
        self.sp = Lane(nc.sync, nc.alloc_semaphore("sp_done"))
        self.floor = nc.sbuf_base // 32 * 32 + 32
        self.names = 0
        self.region_free = ()
        self.x_ready = [None] * B
        self.xn_ready = [None] * B
        self.xnT_ready = [None] * B
        self.x = self.sb("x_residual", [P, B, D])
        self.xn = self.sb("x_normed", [P, B, D])
        self.xnT = self.sb("x_normed_T", [P, KD, T])
        self.ctxT = self.sb("context_T", [P, KD, T])
        self.banks = [nc.alloc_psum_tensor(f"bank{i}", [P, 512], F32).ap() for i in range(8)]

    def place(self, name, shape, dtype, offset):
        size = {F32: 4, BF16: 2, I32: 4, U8: 1}[dtype] * int(np.prod(shape[1:]))
        self.names += 1
        t = self.nc.alloc_sbuf_tensor_at(f"{name}_{self.names}", shape, dtype, offset=offset)
        return t.ap(), offset + (size + 31) // 32 * 32

    def sb(self, name, shape, dtype=F32):
        ap, self.floor = self.place(name, shape, dtype, self.floor)
        return ap

    def phase(self):
        self.region_free = tuple(x.last for x in (self.pe, self.act, self.dve, self.pool) if x.last)
        self.at = self.floor

    def tmp(self, name, shape, dtype=F32):
        ap, self.at = self.place(name, shape, dtype, self.at)
        return ap

    def arrivals(self, name):
        self.names += 1
        return Arrivals(self.nc.alloc_semaphore(f"{name}_{self.names}"))

    def load(self, arrivals, dst, src, *after):
        self.sp.wait(*after)
        return arrivals.of(self.nc.sync.dma_start(dst, src))

    def transpose(self, out, in_):
        return self.nc.tensor.transpose(out, in_, self.ident)

    def constants(self):
        nc, pool, dve, d = self.nc, self.pool, self.dve, self.d
        self.ident = self.sb("identity", [P, P])
        self.ones = self.sb("ones", [P, P])
        self.before = self.sb("strictly_before", [P, P])
        self.neg_ident = self.sb("minus_identity", [P, P], BF16)
        self.identb = self.sb("identity_bf16", [P, P], BF16)
        self.onesb = self.sb("ones_row_bf16", [P, 512], BF16)
        self.par = self.sb("even_odd_heads", [P, 2])
        self.gates = self.sb("gates", [P, 8])
        self.half_power = self.sb("minus_half", [P, B])
        self.stats = self.sb("ln_stats", [P, B, 6])
        self.meanvar = self.sb("ln_mean_var", [P, B, 2])
        self.vareps = self.sb("ln_var_eps", [P, B])
        self.rstd = self.sb("ln_rstd", [P, B])
        g = nc.gpsimd
        pool.done(g.memset(self.ident, 0.0))
        pool.done(g.memset(self.identb, 0.0))
        pool.done(g.memset(self.neg_ident, 0.0))
        pool.done(g.memset(self.ones, 1.0))
        pool.done(g.memset(self.onesb, 1.0))
        zeroed = pool.done(g.memset(self.half_power, -0.5))
        pool.wait(zeroed)
        for m, value in ((self.ident, 1.0), (self.identb, 1.0), (self.neg_ident, -1.0)):
            pool.done(g.affine_select(out=m, in_=m, compare_op=ALU.not_equal, fill=value, base=0,
                                      pattern=[[-1, P]], channel_multiplier=1))
        self.const_ready = pool.done(g.affine_select(
            out=self.before, in_=self.ones, compare_op=ALU.is_gt, fill=0.0, base=0,
            pattern=[[1, P]], channel_multiplier=-1))
        dve.wait(self.const_ready)
        cols = self.ident.rearrange("p (w c r) -> p c w r", c=2, r=16)
        for c in range(2):
            self.par_ready = dve.done(nc.vector.tensor_reduce(
                self.par[:, c:c + 1], cols[:, c, :, :], AX.XY, ALU.add))
        small = self.arrivals("small_loads")
        self.load(small, self.gates[:, 0:4], d["g_xattn"].to_broadcast([P, 4]))
        loaded = self.load(small, self.gates[:, 4:8], d["g_ffn"].to_broadcast([P, 4]))
        self.act.wait(loaded)
        self.gates_ready = self.act.done(nc.scalar.activation(self.gates, self.gates, ACT.Tanh))
        xs = self.arrivals("x_load")
        x_in = self.load(xs, self.x, d["x"].rearrange("b s d -> s b d"))
        for b in range(B):
            self.x_ready[b] = x_in
        cs = self.arrivals("context_load")
        self.ctx_ready = self.load(cs, self.ctxT, d["ctxT"])
        dve.wait(self.gates_ready)

    def ln_stats(self, b):
        nc, dve, pool = self.nc, self.dve, self.pool
        dve.wait(self.x_ready[b])
        e = dve.done(nc.vector.bn_stats(self.stats[:, b, :], self.x[:, b, :]))
        dve.wait(e)
        aggregated = dve.done(nc.vector.bn_aggr(self.meanvar[:, b, :], self.stats[:, b, :]))
        pool.wait(aggregated)
        e = pool.done(nc.gpsimd.tensor_scalar(self.vareps[:, b:b + 1], self.meanvar[:, b, 1:2], EPS, None, ALU.add))
        pool.wait(e)
        self.rstd_ready = pool.done(nc.gpsimd.tensor_tensor(
            self.rstd[:, b:b + 1], self.vareps[:, b:b + 1], self.half_power[:, 0:1], ALU.pow))
        return self.rstd_ready

    def ln_apply(self, b, rstd_ready, *readers):
        dve = self.dve
        dve.wait(rstd_ready, *readers)
        self.xn_ready[b] = dve.done(self.nc.vector.tensor_scalar(
            self.xn[:, b, :], self.x[:, b, :], self.meanvar[:, b, 0:1], self.rstd[:, b:b + 1],
            ALU.subtract, ALU.mult))

    def ln_transpose(self, b, ring):
        pe, act = self.pe, self.act
        n, bank, freed = ring.take()
        pe.wait(self.xn_ready[b], *events_of(freed))
        for k in range(KD):
            turned = self.transpose(bank[:, k * P:(k + 1) * P], self.xn[:, b, k * P:(k + 1) * P])
        act.wait(pe.done(turned))
        self.xnT_ready[b] = act.done(self.nc.scalar.activation(
            self.xnT[:, :, b * P:(b + 1) * P], bank[:, 0:KD * P].rearrange("p (k t) -> p k t", k=KD), ACT.Copy))
        ring.release(n, self.xnT_ready[b])

    def first_layernorm(self):
        ring = Ring(self.banks[6:8])
        self.pe.wait(self.const_ready)
        pend = {}
        for b in range(B + 2):
            if b < B:
                pend[b] = self.ln_stats(b)
            if 2 <= b:
                self.ln_apply(b - 2, pend[b - 2])
                self.ln_transpose(b - 2, ring)

    def attention(self, layer, dk, group, scale, bias, mask):
        nc, pe, act, dve, pool, d = self.nc, self.pe, self.act, self.dve, self.pool, self.d
        small = dk == 16
        width = HEADS * dk
        tiles = width // P
        dv1 = dk + 1
        tok = group * P
        pre = f"L{layer}_"
        self.phase()
        copies = 2 if small else 1
        wq = self.tmp("wq", [P, KD, width])
        wk = self.tmp("wk", [P, KD, width])
        wv = self.tmp("wv", [P, KD, width])
        wo = self.tmp("wo", [P, tiles, D])
        qT = [[self.tmp("qT", [P, tiles, tok]) for _ in range(copies)] for _ in range(2)]
        kT = [self.tmp("kT", [P, tiles, tok]) for _ in range(2)]
        v1 = [self.tmp("v_and_ones", [P, group, HEADS, dv1]) for _ in range(2)]
        probs = [self.tmp("probsT", [P, 4, P]) for _ in range(4)]
        maxes = [self.tmp("row_max", [P, 2, 4], BF16) for _ in range(2)]
        recips = [self.tmp("recips", [P, HEADS]) for _ in range(2)]
        o_row = [self.tmp("attn_out", [P, HEADS, dk]) for _ in range(2)]
        o_col = [self.tmp("attn_outT", [P, tiles, P]) for _ in range(2)]
        weights = self.arrivals("attn_weights")
        self.load(weights, wk, d[pre + "Wk"], *self.region_free)
        self.load(weights, wv, d[pre + "Wv"])
        self.load(weights, wq, d[pre + "Wq"])
        w_ready = self.load(weights, wo, d[pre + "Wo"])
        if bias:
            bq = self.tmp("bq", [P, tiles])
            bk = self.tmp("bk", [P, tiles])
            bqm = self.tmp("bq_by_parity", [P, 2, tiles])
            bv = self.tmp("bv", [P, width])
            bo = self.tmp("bo", [1, D])
            self.load(weights, bq, d[pre + "bq"])
            self.load(weights, bk, d[pre + "bk"])
            self.load(weights, bv, d[pre + "bv"].to_broadcast([P, width]))
            w_ready = self.load(weights, bo, d[pre + "bo"])
            dve.wait(w_ready, self.par_ready, *self.region_free)
            for c in range(2):
                bqm_ready = dve.done(nc.vector.tensor_scalar(
                    bqm[:, c, :], bq, self.par[:, c:c + 1], None, ALU.mult))
        pool.wait(*self.region_free)
        for v in v1:
            ones_ready = pool.done(nc.gpsimd.memset(v[:, :, :, dk:dv1], 1.0))
        act.wait(*self.region_free)
        dve.wait(*self.region_free)
        if mask == "keys":
            kmask = self.tmp("key_mask", [1, T], U8)
            kneg = self.tmp("key_neg", [1, T], BF16)
            kload = self.arrivals("key_mask")
            dve.wait(self.load(kload, kmask, d["mask_keys"]))
            kneg_ready = dve.done(nc.vector.tensor_scalar(kneg, kmask, -BIG, None, ALU.mult))
        if mask == "pairs":
            rt = [[self.tmp("rel", [P, P]) for _ in range(2)] for _ in range(2)]
            mk = [[self.tmp("keep", [P, P], U8) for _ in range(2)] for _ in range(2)]
            neg, kept = self.tmp("neg", [P, P]), self.tmp("kept", [P, P])
            r_q = [self.tmp("bias_qk", [P, P], BF16) for _ in range(2)]
            r_k = [self.tmp("bias_kq", [P, P]) for _ in range(2)]
            any_kept = self.tmp("any_kept", [P, B])
            rload = [self.arrivals("rel_load") for _ in range(2)]
            r_ready, r_read, any_ready = [None] * B, [None] * B, [None] * B

        s_bank, t_bank = self.banks[0:2], self.banks[2:4]
        o_ring, misc = Ring(self.banks[4:6]), Ring(self.banks[6:8])

        q_ready, k_ready, v_ready = {}, {}, {}
        pv_done = {}

        def project(g, kind, m):
            dst = g % 2
            before = (pv_done.get((g - 2) * group + group - 1),)
            n, bank, freed = misc.take()
            pe.wait(w_ready, *events_of(freed))
            if kind == "v":
                bi, half = m
                b = g * group + bi
                cols = min(width, 512)
                pe.wait(self.ctx_ready)
                for k in range(KD):
                    mm = nc.tensor.matmul(bank[:, 0:cols], self.ctxT[:, k, b * P:(b + 1) * P],
                                          wv[:, k, half * cols:(half + 1) * cols], start=k == 0, stop=k == KD - 1)
                hs = cols // dk
                target = v1[dst][:, bi, half * hs:(half + 1) * hs, 0:dk]
                src = bank[:, 0:cols].rearrange("p (h d) -> p h d", d=dk)
                if bias:
                    dve.wait(pe.done(mm), *before)
                    e = dve.done(nc.vector.tensor_tensor(
                        target, src, bv[:, half * cols:(half + 1) * cols].rearrange("p (h d) -> p h d", d=dk), ALU.add))
                else:
                    act.wait(pe.done(mm), *before)
                    e = act.done(nc.scalar.activation(target, src, ACT.Copy))
                v_ready[(g, bi)] = v_ready.get((g, bi), ()) + (e,)
                misc.release(n, e)
                return
            src = self.ctxT if kind == "k" else self.xnT
            w = wk if kind == "k" else wq
            if kind == "q":
                pe.wait(*[self.xnT_ready[b] for b in range(g * group, (g + 1) * group)])
            else:
                pe.wait(self.ctx_ready)
            for k in range(KD):
                mm = nc.tensor.matmul(bank[:, 0:tok], w[:, k, m * P:(m + 1) * P],
                                      src[:, k, g * tok:(g + 1) * tok], start=k == 0, stop=k == KD - 1)
            act.wait(pe.done(mm), *before)
            if kind == "k":
                if bias:
                    e = act.done(nc.scalar.activation(kT[dst][:, m, :], bank[:, 0:tok], ACT.Identity, bias=bk[:, m:m + 1]))
                else:
                    e = act.done(nc.scalar.activation(kT[dst][:, m, :], bank[:, 0:tok], ACT.Copy))
                k_ready[g] = e
            elif small:
                act.wait(bqm_ready)
                for c in range(2):
                    e = act.done(nc.scalar.activation(qT[dst][c][:, m, :], bank[:, 0:tok], ACT.Identity,
                                                      bias=bqm[:, c, m:m + 1], scale=self.par[:, c:c + 1]))
                q_ready[g] = e
            else:
                e = act.done(nc.scalar.activation(qT[dst][0][:, m, :], bank[:, 0:tok], ACT.Copy))
                q_ready[g] = e
            misc.release(n, e)

        def projections(g):
            steps = [(g, "k", m) for m in range(tiles)] + [(g, "q", m) for m in range(tiles)]
            return steps + [(g, "v", (bi, h)) for bi in range(group) for h in range((width + 511) // 512)]

        def pair_bias(b):
            c = b % 2
            after = (r_read[b - 2],) if b >= 2 else ()
            for i, (rel, keep) in enumerate((("rel", "keep"), ("relT", "keepT"))):
                self.load(rload[c], rt[c][i], d[rel][b], *(r_ready[b - 2] if b >= 2 else self.region_free))
                e = self.load(rload[c], mk[c][i], d[keep][b])
            pool.wait(e, *after)
            ends = []
            for i, dst in enumerate((r_q[c], r_k[c])):
                e1 = pool.done(nc.gpsimd.tensor_scalar(neg, mk[c][i], BIG, -BIG, ALU.mult, ALU.add))
                e2 = pool.done(nc.gpsimd.tensor_copy(kept, mk[c][i]))
                pool.wait(e2)
                e2 = pool.done(nc.gpsimd.tensor_tensor(rt[c][i], rt[c][i], kept, ALU.mult))
                pool.wait(e1, e2)
                e3 = pool.done(nc.gpsimd.tensor_tensor(dst, rt[c][i], neg, ALU.add))
                pool.wait(e3)
                ends.append(e3)
            dve.wait(e)
            any_ready[b] = dve.done(nc.vector.tensor_reduce(any_kept[:, b:b + 1], mk[c][0], AX.X, ALU.max))
            r_ready[b] = (ends[-1], any_ready[b])

        if small:
            quads = [[8 * a + 2 * r + c for a in range(2) for c in range(2)] for r in range(4)]
            place = lambda h: (h // 8, 32 * ((h % 8) // 2), 32, h % 2)
        else:
            quads = [[2 * (4 * (r // 2) + i) + r % 2 for i in range(4)] for r in range(4)]
            place = lambda h: (h // 2, 64 * (h % 2), 64, 0)

        def operands(h, b):
            g, bi = b // group, b % group
            tile, base, rows, c = place(h)
            t = slice(bi * P, (bi + 1) * P)
            return qT[g % 2][c][base:base + rows, tile, t], kT[g % 2][base:base + rows, tile, t]

        units = [(b, pair) for b in range(B) for pair in range(2)]
        max_done, exp_done, pv_of, st_done = {}, {}, {}, {}
        s_free = [None, None]
        t_free = [None, None]

        def scores_for_max(u):
            b, pair = units[u]
            pe.wait(q_ready[b // group], k_ready[b // group], *s_free)
            if mask == "pairs":
                pe.wait(*r_ready[b])
            if mask == "keys":
                pe.wait(kneg_ready)
            for j in range(2):
                if mask == "pairs":
                    nc.tensor.matmul(s_bank[j].rearrange("p (h k) -> p h k", h=4), self.identb,
                                     r_q[b % 2][:, None, :].to_broadcast([P, 4, P]), start=True, stop=False, skip_group_check=True)
                if mask == "keys":
                    nc.tensor.matmul(s_bank[j].rearrange("p (h k) -> p h k", h=4), self.onesb[0:1, 0:P],
                                     kneg[0:1, None, b * P:(b + 1) * P].to_broadcast([1, 4, P]), start=True, stop=False, skip_group_check=True)
            for i in range(4):
                for j in range(2):
                    q, k = operands(quads[2 * pair + j][i], b)
                    mm = nc.tensor.matmul(s_bank[j][:, i * P:(i + 1) * P], q, k, start=mask is None, stop=True, skip_group_check=True)
            e = pe.done(mm)
            dve.wait(e, st_done.get(u - 2))
            for j in range(2):
                s_free[j] = dve.done(nc.vector.tensor_reduce(
                    maxes[u % 2][:, j, :], s_bank[j].rearrange("p (h k) -> p h k", h=4), AX.X, ALU.max))
            max_done[u] = s_free[1]

        def scores_for_exp(u):
            b, pair = units[u]
            pe.wait(max_done[u], *t_free)
            for j in range(2):
                if mask == "pairs":
                    nc.tensor.matmul(t_bank[j].rearrange("p (h q) -> p h q", h=4), self.ident,
                                     r_k[b % 2][:, None, :].to_broadcast([P, 4, P]), start=True, stop=False, skip_group_check=True)
                if mask == "keys":
                    nc.tensor.matmul(t_bank[j], kneg[0:1, b * P:(b + 1) * P], self.onesb[0:1, :],
                                     start=True, stop=False, skip_group_check=True)
            for j in range(2):
                for i in range(4):
                    q, k = operands(quads[2 * pair + j][i], b)
                    region = t_bank[j][:, i * P:(i + 1) * P]
                    nc.tensor.matmul(region, maxes[u % 2][:, j, i:i + 1].to_broadcast([P, P]), self.neg_ident,
                                     start=mask is None, stop=False, skip_group_check=True)
                    mm = nc.tensor.matmul(region, k, q, start=False, stop=True, skip_group_check=True)
            e = st_done[u] = pe.done(mm)
            if mask == "pairs":
                r_read[b] = e
            act.wait(e, pv_of.get(u - 2))
            for j in range(2):
                t_free[j] = act.done(nc.scalar.activation(
                    probs[2 * (u % 2) + j].rearrange("p h q -> p (h q)"), t_bank[j], ACT.Exp, scale=scale))
            exp_done[u] = t_free[1]

        o_now = {}
        rest = {}

        def times_v(u):
            b, pair = units[u]
            g, bi = b // group, b % group
            pe.wait(exp_done[u], ones_ready, *v_ready[(g, bi)])
            orow = o_row[b % 2]
            for j in range(2):
                r = 2 * pair + j
                if not small or r == 0:
                    o_now[b] = o_ring.take()
                    pe.wait(*events_of(o_now[b][2]))
                n, bank, _ = o_now[b]
                for i, h in enumerate(quads[r]):
                    at = (h if small else i) * dv1
                    mm = nc.tensor.matmul(bank[:, at:at + dv1], probs[2 * (u % 2) + j][:, i, :],
                                          v1[g % 2][:, bi, h, :], start=True, stop=True)
                if small and r < 3:
                    continue
                heads = HEADS if small else 4
                full = bank[:, 0:heads * dv1].rearrange("p (h d) -> p h d", d=dv1)
                rec = recips[b % 2][:, 0:HEADS] if small else recips[b % 2][:, 4 * r:4 * r + 4]
                pv = pe.done(mm)
                dve.wait(pv, o_read.get(b - 2))
                e = dve.done(nc.vector.reciprocal(rec[:, :, None], full[:, :, dk:dv1]))
                dve.wait(e)
                if mask == "pairs":
                    dve.wait(any_ready[b])
                    e = dve.done(nc.vector.tensor_scalar(rec, rec, any_kept[:, b:b + 1], None, ALU.mult))
                    dve.wait(e)
                if small:
                    target = orow
                else:
                    target = orow.rearrange("p (r i c) d -> p r c i d", r=2, c=2)[:, r // 2, r % 2]
                e = dve.done(nc.vector.tensor_tensor(
                    target, full[:, :, 0:dk], rec[:, :, None].to_broadcast([P, heads, dk]), ALU.mult))
                o_ring.release(n, e)
                o_done[b] = e
            pv_of[u] = pe.done(mm) if (small and 2 * pair + 1 < 3) else pv
            if pair == 1:
                pv_done[b] = pv_of[u]

        o_done, o_read = {}, {}

        def turn_out(b):
            flat = o_row[b % 2].rearrange("p h d -> p (h d)")
            col = o_col[b % 2]
            pe.wait(o_done[b])
            for t0 in range(0, tiles, 4):
                n, bank, freed = misc.take()
                pe.wait(*events_of(freed))
                some = range(t0, min(tiles, t0 + 4))
                for t in some:
                    mm = self.transpose(bank[:, (t - t0) * P:(t - t0 + 1) * P], flat[:, t * P:(t + 1) * P])
                e = o_read[b] = pe.done(mm)
                act.wait(e, proj_done.get(b - 2))
                e = act.done(nc.scalar.activation(
                    col[:, t0:t0 + len(some), :], bank[:, 0:len(some) * P].rearrange("p (t q) -> p t q", q=P), ACT.Copy))
                misc.release(n, e)
            col_ready[b] = e

        col_ready, proj_done = {}, {}

        def out_project(b):
            n, bank, freed = misc.take()
            pe.wait(col_ready[b], *events_of(freed))
            for t in range(tiles):
                mm = nc.tensor.matmul(bank[:, 0:D], o_col[b % 2][:, t, :], wo[:, t, :],
                                      start=t == 0, stop=t == tiles - 1 and not bias)
            if bias:
                mm = nc.tensor.matmul(bank[:, 0:D], self.ones[0:1, 0:P], bo[0:1, :], start=False, stop=True)
            e = proj_done[b] = pe.done(mm)
            misc.release(n, self.update(b, bank[:, 0:D], layer, e))
            pend[b] = self.ln_stats(b)

        pend = {}
        for step in projections(0):
            project(*step)
        if mask == "pairs":
            pair_bias(0)
        todo = []
        for u in range(len(units) + 9):
            for step in rest.pop(u, ()):
                step()
            if u < len(units):
                b, pair = units[u]
                if b % group == 0 and pair == 0 and b // group + 1 < B // group:
                    todo = projections(b // group + 1)
                    pace = -(-len(todo) // (2 * group - 1))
                if mask == "pairs" and pair == 1 and b + 1 < B:
                    pair_bias(b + 1)
                scores_for_max(u)
            if 1 <= u <= len(units):
                scores_for_exp(u - 1)
            if u < len(units) and not (b % group == 0 and pair == 0):
                for step in todo[:pace]:
                    project(*step)
                todo = todo[pace:]
            if 2 <= u <= len(units) + 1:
                times_v(u - 2)
                b, pair = units[u - 2]
                if pair == 1:
                    rest.setdefault(u + 1, []).append(lambda b=b: turn_out(b))
                    rest.setdefault(u + 2, []).append(lambda b=b: out_project(b))
                    rest.setdefault(u + 4, []).append(lambda b=b: self.ln_apply(b, pend[b]))
                    rest.setdefault(u + 5, []).append(lambda b=b: self.ln_transpose(b, misc))

    def first_max(self, values, pick, top, ramp, equal):
        nc, dve = self.nc, self.dve
        spread = lambda m: m[:, :, None].to_broadcast([P, B, 8])
        e = dve.done(nc.vector.tensor_reduce(top, values, AX.X, ALU.max))
        dve.wait(e)
        e = dve.done(nc.vector.tensor_tensor(equal, values, spread(top), ALU.is_equal))
        dve.wait(e)
        e = dve.done(nc.vector.tensor_tensor(equal, equal, ramp, ALU.mult))
        dve.wait(e)
        e = dve.done(nc.vector.tensor_reduce(top, equal, AX.X, ALU.max))
        dve.wait(e)
        e = dve.done(nc.vector.tensor_tensor(pick, equal, spread(top), ALU.is_equal))
        dve.wait(e)
        return e

    def moe(self, layer, experts, inter, topk):
        nc, pe, act, dve, pool, sp, d = self.nc, self.pe, self.act, self.dve, self.pool, self.sp, self.d
        V = nc.vector
        shared = layer == 1
        gate = 4 + layer
        blocks = T * topk // P + experts - 1
        chunks = -(-inter // P)
        last_rows = inter - (chunks - 1) * P
        wide = KD * 2 * inter + chunks * D
        groups, c = [], 0
        while c < chunks:
            n = 2 if c + 2 < chunks or (c + 2 == chunks and last_rows == P) else 1
            groups.append(list(range(c, c + n)))
            c += n
        self.phase()
        free = self.region_free
        nw = 3
        weights = [self.tmp("expert_w", [P, wide]) for _ in range(nw)]
        w_sems = [self.arrivals("expert_w") for _ in range(nw)]
        rows = [self.tmp("block_rows", [P, D]) for _ in range(nw)]
        r_sems = [self.arrivals("block_rows") for _ in range(nw)]
        cols = [self.tmp("block_T", [P, KD, P]) for _ in range(2)]
        silu = [self.tmp("silu", [P, 2 * P]) for _ in range(2)]
        hid = [self.tmp("hidden", [P, chunks, P]) for _ in range(2)]
        youts = [self.tmp("block_out", [P, D]) for _ in range(3)]
        y_sems = [self.arrivals("block_out") for _ in range(3)]
        back = [self.tmp("gathered", [P, D]) for _ in range(8)]
        b_sems = [self.arrivals("gathered") for _ in range(8)]
        xs_dram = nc.dram_tensor(f"sorted_x_{layer}", [blocks * P, D], F32, kind="Internal").ap()
        ys_dram = nc.dram_tensor(f"sorted_y_{layer}", [blocks * P, D], F32, kind="Internal").ap()
        t = lambda name, shape, dtype=F32: self.tmp(name, shape, dtype)
        BE = B * 8
        router = t("router", [P, KD, 8])
        zeros = t("zeros", [P, 2 * D])
        ramp, step, reset = t("ramp", [P, B, 8]), t("block_step", [P, 8, B]), t("reset", [P, 8, B])
        index = t("block_index", [P, blocks, 8])
        logits, equal, top = t("logits", [P, B, 8]), t("equal", [P, B, 8]), t("top", [P, B])
        picks = [t("pick", [P, B, 8]) for _ in range(topk)]
        both = t("either_pick", [P, B, 8])
        total, upto = t("tile_totals", [P, 8, B]), t("totals_upto", [P, 8, B])
        more, nblk, end, ones8 = t("more", [P, 8, B]), t("nblk", [P, 8]), t("end_block", [P, 8]), t("ones8", [P, 8])
        base, rank, tmp8 = t("base", [P, 8]), t("rank", [P, B, 8]), t("tmp8", [P, B, 8])
        past, eid, eid_i = t("past", [P, blocks, 8]), t("expert_row", [P, blocks]), t("expert_row_int", [P, blocks], I32)
        pos = [t("pos", [P, B]) for _ in range(topk)]
        pos_i = [t("pos_int", [P, B], I32) for _ in range(topk)]
        tw = [t("token_weight", [P, B]) for _ in range(topk)]

        g = nc.gpsimd
        pool.wait(*free)
        pool.done(g.iota(ramp, pattern=[[0, B], [-1, 8]], base=8, channel_multiplier=0, allow_small_or_imprecise_dtypes=True))
        pool.done(g.iota(step, pattern=[[0, 8], [P, B]], base=0, channel_multiplier=0, allow_small_or_imprecise_dtypes=True))
        pool.done(g.iota(index, pattern=[[1, blocks], [0, 8]], base=0, channel_multiplier=0, allow_small_or_imprecise_dtypes=True))
        pool.done(g.memset(zeros, 0.0))
        pool.done(g.memset(ones8, 1.0))
        e = pool.done(g.memset(reset, 1.0))
        pool.wait(e)
        tables_ready = pool.done(g.memset(reset[:, :, 0:1], 0.0))
        zero_sem = self.arrivals("zero_fill")
        sp.wait(tables_ready)
        half = blocks * P // (2 * P)
        zero_done = zero_sem.of(nc.sync.dma_start(
            xs_dram[0:half * 2 * P, :].rearrange("(p n r) d -> p n (r d)", p=P, r=2),
            zeros[:, None, :].to_broadcast([P, half, 2 * D])))
        if blocks % 2:
            zero_done = zero_sem.of(nc.sync.dma_start(xs_dram[half * 2 * P:, :], zeros[:, 0:D]))
        small = self.arrivals("router_w")
        router_ready = self.load(small, router, d[f"L{layer}_router"], *free)
        if shared:
            bias8 = t("gate_bias", [P, 8])
            router_ready = self.load(small, bias8, d["L1_gate_bias"].to_broadcast([P, 8]))
            shared_w = t("shared_w", [P, wide])
            shared_sem = self.arrivals("shared_w")
            shared_ready = self.load(shared_sem, shared_w, d["L1_shared"])

        rb = self.banks[0]
        pe.wait(router_ready, *self.xnT_ready, *free)
        for b in range(B):
            for k in range(KD):
                mm = nc.tensor.matmul(rb[:, b * 8:(b + 1) * 8], self.xnT[:, k, b * P:(b + 1) * P], router[:, k, :],
                                      start=k == 0, stop=k == KD - 1)
        dve.wait(pe.done(mm), tables_ready, router_ready, *free)
        spread = lambda m: m[:, :, None].to_broadcast([P, B, 8])
        bank3 = rb[:, 0:BE].rearrange("p (b e) -> p b e", e=8)
        e = dve.done(V.tensor_copy(logits, bank3))
        dve.wait(e)
        if shared:
            prob = t("router_prob", [P, B, 8])
            e = dve.done(V.tensor_reduce(top, logits, AX.X, ALU.max))
            dve.wait(e)
            e = dve.done(V.tensor_tensor(logits, logits, spread(top), ALU.subtract))
            act.wait(e)
            e = act.done(nc.scalar.activation(prob, logits, ACT.Exp))
            dve.wait(e)
            e = dve.done(V.tensor_reduce(top, prob, AX.X, ALU.add))
            dve.wait(e)
            e = dve.done(V.reciprocal(top, top))
            dve.wait(e)
            e = dve.done(V.tensor_tensor(prob, prob, spread(top), ALU.mult))
            dve.wait(e)
            e = dve.done(V.tensor_tensor(logits, prob, bias8[:, None, :].to_broadcast([P, B, 8]), ALU.add))
            dve.wait(e)
        for n in range(topk):
            e = self.first_max(logits, picks[n], top, ramp, equal)
            if n + 1 < topk:
                e = dve.done(V.tensor_scalar(tmp8, picks[n], BIG, None, ALU.mult))
                dve.wait(e)
                e = dve.done(V.tensor_tensor(logits, logits, tmp8, ALU.subtract))
                dve.wait(e)
            if shared:
                e = dve.done(V.tensor_tensor(tmp8, prob, picks[n], ALU.mult))
                dve.wait(e)
                e = dve.done(V.tensor_reduce(tw[n], tmp8, AX.X, ALU.add))
                dve.wait(e)
                e = dve.done(V.tensor_scalar(tw[n], tw[n], self.gates[:, gate:gate + 1], None, ALU.mult))
                dve.wait(e)
        if topk == 2:
            e = dve.done(V.tensor_tensor(both, picks[0], picks[1], ALU.add))
        else:
            both = picks[0]
        pb = self.banks[1]
        flat = both.rearrange("p b e -> p (b e)")
        pe.wait(e)
        nc.tensor.matmul(pb[:, 0:BE], self.before, flat, start=True, stop=True)
        e = pe.done(nc.tensor.matmul(pb[:, BE:2 * BE], self.ones, flat, start=True, stop=True))
        dve.wait(e)
        e = dve.done(V.tensor_copy(total, pb[:, BE:2 * BE].rearrange("p (b e) -> p e b", e=8)))
        dve.wait(e)
        line = lambda m: m.rearrange("p e b -> p (e b)")
        e = dve.done(V.tensor_tensor_scan(line(upto), line(reset), line(total), 0.0, ALU.mult, ALU.add))
        dve.wait(e)
        e = dve.done(V.tensor_tensor(more, upto[:, :, B - 1:B].to_broadcast([P, 8, B]), step, ALU.is_gt))
        dve.wait(e)
        e = dve.done(V.tensor_reduce(nblk, more, AX.X, ALU.add))
        e2 = dve.done(V.tensor_tensor(upto, upto, total, ALU.subtract))
        dve.wait(e)
        e = dve.done(V.tensor_tensor_scan(end, ones8, nblk, 0.0, ALU.mult, ALU.add))
        dve.wait(e)
        e = dve.done(V.tensor_tensor(base, end, nblk, ALU.subtract))
        dve.wait(e)
        e = dve.done(V.tensor_scalar(base, base, float(P), None, ALU.mult))
        e1 = dve.done(V.tensor_tensor(past, index, end[:, None, :].to_broadcast([P, blocks, 8]), ALU.is_ge))
        dve.wait(e1)
        e1 = dve.done(V.tensor_reduce(eid, past, AX.X, ALU.add))
        dve.wait(e1)
        e1 = dve.done(V.tensor_scalar(eid, eid, float(experts - 1), float(P), ALU.min, ALU.mult))
        dve.wait(e1)
        ids_ready = dve.done(V.tensor_copy(eid_i, eid))
        dve.wait(e, e2)
        e = dve.done(V.tensor_tensor(rank, pb[:, 0:BE].rearrange("p (b e) -> p b e", e=8),
                                     upto.rearrange("p e b -> p b e"), ALU.add))
        dve.wait(e)
        e = dve.done(V.tensor_tensor(rank, rank, base[:, None, :].to_broadcast([P, B, 8]), ALU.add))
        dve.wait(e)
        for n in range(topk):
            e = dve.done(V.tensor_tensor(tmp8, rank, picks[n], ALU.mult))
            dve.wait(e)
            e = dve.done(V.tensor_reduce(pos[n], tmp8, AX.X, ALU.add))
            dve.wait(e)
            pos_ready = dve.done(V.tensor_copy(pos_i[n], pos[n]))

        scattered = self.arrivals("scattered")
        pool.wait(pos_ready, zero_done, *self.xn_ready)
        for b in range(B):
            for n in range(topk):
                all_scattered = scattered.of(g.indirect_dma_start(
                    xs_dram, bass.IndirectOffsetOnAxis(pos_i[n][:, b:b + 1], 0), self.xn[:, b, :], None))

        gu_ring, y_ring, t_ring = Ring(self.banks[0:4]), Ring(self.banks[4:6]), Ring(self.banks[6:8])
        gu_ring.release(0, pos_ready)
        gu_ring.release(1, pos_ready)
        silu_ring, down_done, w_read, hid_read = Ring(silu), {}, {}, {}
        col_read, y_stored, row_read = {}, {}, {}
        steps = ([("shared", b) for b in range(B)] if shared else []) + [("routed", i) for i in range(blocks)]
        w_ready, rows_ready, cols_ready, h_ready = {}, {}, {}, {}

        def load_block(i):
            slot = i % nw
            sp.wait(ids_ready)
            row = nc.sync.value_load(eid_i[0:1, i:i + 1], min_val=0, max_val=(experts - 1) * P)
            w_ready[i] = self.load(w_sems[slot], weights[slot], d[f"L{layer}_experts"][bass.ds(row, P), :], w_read.get(i - nw))
            rows_ready[i] = self.load(r_sems[slot], rows[slot], xs_dram[i * P:(i + 1) * P, :], all_scattered, row_read.get(i - nw))

        def turn_block(i):
            n, bank, freed = t_ring.take()
            pe.wait(rows_ready[i], *events_of(freed))
            for k in range(KD):
                mm = self.transpose(bank[:, k * P:(k + 1) * P], rows[i % nw][:, k * P:(k + 1) * P])
            row_read[i] = pe.done(mm)
            act.wait(row_read[i], col_read.get(i - 2))
            cols_ready[i] = act.done(nc.scalar.activation(
                cols[i % 2], bank[:, 0:KD * P].rearrange("p (k t) -> p k t", k=KD), ACT.Copy))
            t_ring.release(n, cols_ready[i])

        def up(s, kind, i):
            if kind == "shared":
                w, x_in = shared_w, self.xnT[:, :, i * P:(i + 1) * P]
                pe.wait(shared_ready)
            else:
                w, x_in = weights[i % nw], cols[i % 2]
                pe.wait(w_ready[i], cols_ready[i])
            for gr in groups:
                n, bank, freed = gu_ring.take()
                pe.wait(*events_of(freed))
                m = last_rows if gr[-1] == chunks - 1 else P
                for half in range(2):
                    for j, c in enumerate(gr):
                        at = (half * len(gr) + j) * P
                        for k in range(KD):
                            col = (k * 2 + half) * inter + c * P
                            mm = nc.tensor.matmul(bank[0:m, at:at + P], w[:, col:col + m], x_in[:, k, :],
                                                  start=k == 0, stop=k == KD - 1)
                e = pe.done(mm)
                size = len(gr) * P
                sn, sbuf, sfreed = silu_ring.take()
                act.wait(e, *events_of(sfreed))
                e = act.done(nc.scalar.activation(sbuf[0:m, 0:size], bank[0:m, 0:size], ACT.Silu))
                dve.wait(e, hid_read.get(s - 2))
                h_ready[s] = dve.done(V.tensor_tensor(
                    hid[s % 2][0:m, gr[0]:gr[0] + len(gr), :], sbuf[0:m, 0:size].rearrange("p (c t) -> p c t", t=P),
                    bank[0:m, size:2 * size].rearrange("p (c t) -> p c t", t=P), ALU.mult))
                gu_ring.release(n, h_ready[s])
                silu_ring.release(sn, h_ready[s])
            if kind == "routed":
                col_read[i] = (pe.semaphore, pe.count)

        def down(s, kind, i):
            w = shared_w if kind == "shared" else weights[i % nw]
            n, bank, freed = y_ring.take()
            pe.wait(h_ready[s], *events_of(freed))
            for c in range(chunks):
                m = last_rows if c == chunks - 1 else P
                col = KD * 2 * inter + c * D
                mm = nc.tensor.matmul(bank[:, 0:D], hid[s % 2][0:m, c, :], w[0:m, col:col + D],
                                      start=c == 0, stop=c == chunks - 1)
            e = hid_read[s] = pe.done(mm)
            if kind == "shared":
                y_ring.release(n, self.update(i, bank[:, 0:D], gate, e))
                return
            w_read[i] = e
            dve.wait(e, y_stored.get(i - 3))
            e = dve.done(V.tensor_copy(youts[i % 3], bank[:, 0:D]))
            y_ring.release(n, e)
            sp.wait(e)
            y_stored[i] = y_sems[i % 3].of(nc.sync.dma_start(ys_dram[i * P:(i + 1) * P, :], youts[i % 3]))

        for i in range(2):
            load_block(i)
        for s in range(len(steps) + 1):
            if s < len(steps):
                kind, i = steps[s]
                if steps[s] == ("routed", 0):
                    turn_block(0)
                up(s, kind, i)
                if kind == "routed" and i + 1 < blocks:
                    turn_block(i + 1)
            if s >= 1:
                down(s - 1, *steps[s - 1])
            if s < len(steps) and kind == "routed" and i + 2 < blocks:
                load_block(i + 2)

        pool.wait(*[y_stored[i] for i in range(blocks - 3, blocks)])
        order = [(b, n) for b in range(B) for n in range(topk)]
        read, pend = {}, {}
        for m, (b, n) in enumerate(order):
            pool.wait(read.get(m - 8))
            slot = m % 8
            e = b_sems[slot].of(g.indirect_dma_start(
                back[slot], None, ys_dram, bass.IndirectOffsetOnAxis(pos_i[n][:, b:b + 1], 0)))
            if shared:
                dve.wait(self.x_ready[b], e)
                self.x_ready[b] = dve.done(V.scalar_tensor_tensor(
                    self.x[:, b, :], back[slot], tw[n][:, b:b + 1], self.x[:, b, :], ALU.mult, ALU.add))
                read[m] = self.x_ready[b]
            else:
                read[m] = self.update(b, back[slot], gate, e)
            if n == topk - 1:
                pend[b] = self.ln_stats(b)
                if b >= 2:
                    self.ln_apply(b - 2, pend[b - 2])
                    self.ln_transpose(b - 2, t_ring)
        for b in (B - 2, B - 1):
            self.ln_apply(b, pend[b])
            self.ln_transpose(b, t_ring)

    def soft_moe(self):
        nc, pe, act, dve, pool, sp, d = self.nc, self.pe, self.act, self.dve, self.pool, self.sp, self.d
        V = nc.vector
        self.phase()
        free = self.region_free
        group, nd = 4, 5
        phi = self.tmp("phiT", [P, KD, SLOTS])
        phib = self.tmp("phi_b_parts", [3, SLOTS], BF16)
        lg = self.tmp("slot_logits", [P, SLOTS])
        disp = [self.tmp("dispatch", [P, SLOTS]) for _ in range(nd)]
        comb = [self.tmp("combine", [P, SLOTS]) for _ in range(2)]
        combT = self.tmp("combineT", [P, ST, P])
        acc = self.tmp("slot_sums", [P, ST, D])
        gmax, gsum = self.tmp("expert_max", [P, NEXP]), self.tmp("expert_sum", [P, NEXP])
        smax, ssum = self.tmp("slot_max", [P, PSLOT]), self.tmp("slot_sum", [P, PSLOT])
        ct_dram = nc.dram_tensor("combineT_rows", [B, P, ST * P], F32, kind="Internal").ap()
        loads = self.arrivals("phi")
        phi_ready = self.load(loads, phi, d["phiT"], *free)
        braw = lg[0:1, :]
        part = combT.rearrange("p s t -> p (s t)")[0:1, 0:SLOTS]
        pbf = [self.tmp("phi_part", [1, SLOTS], BF16) for _ in range(1)][0]
        b_ready = self.load(loads, braw, d["phi_b"])
        dve.wait(b_ready, *free)
        ps = self.arrivals("phi_parts")
        for n in range(3):
            e = dve.done(V.tensor_copy(pbf, braw))
            dve.wait(e)
            if n < 2:
                e2 = dve.done(V.tensor_copy(part, pbf))
                dve.wait(e2)
                e2 = dve.done(V.tensor_tensor(braw, braw, part, ALU.subtract))
            sp.wait(e)
            parts_ready = ps.of(nc.sync.dma_start(phib[n:n + 1, :], pbf))
            if n < 2:
                dve.wait(e2, parts_ready)
        lbank = self.banks[0:4]
        xt_ring, misc = Ring(self.banks[4:6]), Ring(self.banks[6:8])
        pe.wait(phi_ready, parts_ready, *free)
        act.wait(*free)
        pool.wait(*free)
        lg_free, lb_free, d_ready, d_read, c_ready, c_read, ct_stored = (), [None] * 4, {}, {}, {}, {}, None
        cts = self.arrivals("combineT_store")
        acc_ready = [None] * (ST // 2)
        by_expert = lambda m: m.rearrange("p (n s) -> p n s", s=PSLOT)
        by_slot = lambda m: m.rearrange("p (n s) -> p s n", s=PSLOT)

        def slot_logits(b):
            nonlocal lg_free
            pe.wait(self.xnT_ready[b])
            for j in range(4):
                pe.wait(lb_free[j])
                cs = slice(j * 512, (j + 1) * 512)
                for k in range(KD):
                    nc.tensor.matmul(lbank[j], self.xnT[:, k, b * P:(b + 1) * P], phi[:, k, cs], start=k == 0, stop=False)
                e = pe.done(nc.tensor.matmul(lbank[j], self.onesb[0:3, 0:P], phib[:, cs], start=False, stop=True))
                act.wait(e, *lg_free)
                e = lb_free[j] = act.done(nc.scalar.activation(lg[:, cs], lbank[j], ACT.Copy))
            lg_ready = e
            D_, C_ = disp[b % nd], comb[b % 2]
            dve.wait(lg_ready, d_read.get(b - nd))
            e1 = dve.done(V.tensor_reduce(gmax, by_expert(lg), AX.X, ALU.max))
            e2 = dve.done(V.tensor_reduce(smax, by_slot(lg), AX.X, ALU.max))
            pool.wait(e2, lg_ready, c_read.get(b - 2))
            e4 = pool.done(nc.gpsimd.tensor_tensor(by_expert(C_), by_expert(lg), smax[:, None, :].to_broadcast([P, NEXP, PSLOT]), ALU.subtract))
            dve.wait(e1)
            e3 = dve.done(V.tensor_tensor(by_expert(D_), by_expert(lg), gmax[:, :, None].to_broadcast([P, NEXP, PSLOT]), ALU.subtract))
            lg_free = (e3, e4)
            act.wait(e3)
            e3 = act.done(nc.scalar.activation(D_, D_, ACT.Exp))
            act.wait(e4)
            e4 = act.done(nc.scalar.activation(C_, C_, ACT.Exp))
            dve.wait(e3)
            e3 = dve.done(V.tensor_reduce(gsum, by_expert(D_), AX.X, ALU.add))
            dve.wait(e3)
            e3 = dve.done(V.reciprocal(gsum, gsum))
            dve.wait(e3)
            d_ready[b] = dve.done(V.tensor_tensor(by_expert(D_), by_expert(D_), gsum[:, :, None].to_broadcast([P, NEXP, PSLOT]), ALU.mult))
            dve.wait(e4, c_ready.get(b - 1))
            e4 = dve.done(V.tensor_reduce(ssum, by_slot(C_), AX.X, ALU.add))
            dve.wait(e4)
            e4 = dve.done(V.reciprocal(ssum, ssum))
            pool.wait(e4)
            c_ready[b] = pool.done(nc.gpsimd.tensor_tensor(by_expert(C_), by_expert(C_), ssum[:, None, :].to_broadcast([P, NEXP, PSLOT]), ALU.mult))

        def turn_combine(b):
            nonlocal ct_stored
            pe.wait(c_ready[b])
            for j in range(0, ST, 4):
                n, bank, freed = misc.take()
                pe.wait(*events_of(freed))
                for i in range(4):
                    mm = self.transpose(bank[:, i * P:(i + 1) * P], comb[b % 2][:, (j + i) * P:(j + i + 1) * P])
                e = pe.done(mm)
                act.wait(e, ct_stored)
                e2 = act.done(nc.scalar.activation(combT[:, j:j + 4, :], bank.rearrange("p (s t) -> p s t", t=P), ACT.Copy))
                misc.release(n, e2)
            c_read[b] = e
            sp.wait(e2)
            ct_stored = cts.of(nc.sync.dma_start(ct_dram[b], combT.rearrange("p s t -> p (s t)")))

        def slot_sums(gp):
            tiles = range(gp * group, (gp + 1) * group)
            for j in range(0, ST, 2):
                n, bank, freed = xt_ring.take()
                pe.wait(*[d_ready[b] for b in tiles], *events_of(freed))
                for i in range(2):
                    for b in tiles:
                        mm = nc.tensor.matmul(bank[:, i * D:(i + 1) * D], disp[b % nd][:, (j + i) * P:(j + i + 1) * P],
                                              self.xn[:, b, :], start=b == tiles[0], stop=b == tiles[-1])
                e = pe.done(mm)
                target, src = acc[:, j:j + 2, :], bank.rearrange("p (s d) -> p s d", d=D)
                dve.wait(e, acc_ready[j // 2])
                if gp == 0:
                    e2 = dve.done(V.tensor_copy(target, src))
                else:
                    e2 = dve.done(V.tensor_tensor(target, target, src, ALU.add))
                acc_ready[j // 2] = e2
                xt_ring.release(n, e2)
            for b in tiles:
                d_read[b] = e

        for b in range(B + 1):
            if b < B:
                slot_logits(b)
            if b >= 1:
                turn_combine(b - 1)
                if b % group == 0:
                    slot_sums(b // group - 1)

        self.phase()
        free = self.region_free
        acc_end = self.at
        xt = self.tmp("slots_normed", [P, ST, D])
        xtT = self.tmp("slots_normed_T", [P, KD, SLOTS])
        yt = self.tmp("slot_outputs", [P, ST, D])
        nwe = 2
        ew = [self.tmp("expert_w", [P, 4, KD, D]) for _ in range(nwe)]
        ctl = [self.tmp("combineT_load", [P, ST, P]) for _ in range(2)]
        sst, smv = self.tmp("slot_stats", [P, ST, 6]), self.tmp("slot_mean_var", [P, ST, 2])
        sve, srs, sneg = self.tmp("slot_var_eps", [P, ST]), self.tmp("slot_rstd", [P, ST]), self.tmp("slot_shift", [P, ST])
        ews = [self.arrivals("expert_w") for _ in range(nwe)]
        ebs, ctls = self.arrivals("expert_b"), [self.arrivals("combineT_load") for _ in range(2)]
        dve.wait(*free, *acc_ready)
        e = dve.done(V.tensor_scalar(acc, acc, -33000.0, 65000.0, ALU.max, ALU.min))
        dve.wait(e)
        for s in range(ST):
            e = dve.done(V.bn_stats(sst[:, s, :], acc[:, s, :]))
        dve.wait(e)
        for s in range(ST):
            e = dve.done(V.bn_aggr(smv[:, s, :], sst[:, s, :]))
        pool.wait(e, *free)
        e = pool.done(nc.gpsimd.tensor_scalar(sve[:, :, None], smv[:, :, 1:2], EPS, None, ALU.add))
        pool.wait(e)
        rs = pool.done(nc.gpsimd.tensor_tensor(srs, sve, self.half_power, ALU.pow))
        dve.wait(rs)
        e = None
        for s in range(ST):
            e = dve.done(V.tensor_scalar(acc[:, s, :], acc[:, s, :], smv[:, s, 0:1], srs[:, s:s + 1], ALU.subtract, ALU.mult))
            act.wait(e, *free)
            tanh_done = act.done(nc.scalar.activation(xt[:, s, :], acc[:, s, :], ACT.Tanh))
            n, bank, freed = misc.take()
            pe.wait(tanh_done, *events_of(freed))
            for k in range(KD):
                mm = self.transpose(bank[:, k * P:(k + 1) * P], xt[:, s, k * P:(k + 1) * P])
            act.wait(pe.done(mm))
            turned = act.done(nc.scalar.activation(xtT[:, :, s * P:(s + 1) * P], bank[:, 0:KD * P].rearrange("p (k t) -> p k t", k=KD), ACT.Copy))
            misc.release(n, turned)
        for j in range(4):
            yb_ready = self.load(ebs, yt[j * PSLOT:(j + 1) * PSLOT, :, :],
                                 d["expert_b"][j].rearrange("(a s) d -> a s d", a=1).to_broadcast([PSLOT, ST, D]), *free)
        ew_read, ew_ready = {}, {}
        for s in range(ST + 1):
            if s < ST:
                ew_ready[s] = self.load(ews[s % nwe], ew[s % nwe], d["expert_w"][s], ew_read.get(s - nwe), *free)
            if s == 0:
                continue
            s -= 1
            n, bank, freed = xt_ring.take()
            pe.wait(ew_ready[s], turned, *events_of(freed))
            for j in range(4):
                for k in range(KD):
                    mm = nc.tensor.matmul(bank[j * PSLOT:(j + 1) * PSLOT, 0:D], xtT[:, k, s * P + j * PSLOT:s * P + (j + 1) * PSLOT],
                                          ew[s % nwe][:, j, k, :], start=k == 0, stop=k == KD - 1)
            ew_read[s] = pe.done(mm)
            dve.wait(ew_read[s], yb_ready)
            yt_ready = dve.done(V.tensor_tensor(yt[:, s, :], yt[:, s, :], bank[:, 0:D], ALU.add))
            xt_ring.release(n, yt_ready)

        ct_read, pend = {}, {}
        pe.wait(yt_ready)
        for b in range(B + 2):
            if b < B:
                ct_ready = self.load(ctls[b % 2], ctl[b % 2].rearrange("p s t -> p (s t)"), ct_dram[b], ct_stored, ct_read.get(b - 2))
                n, bank, freed = xt_ring.take()
                pe.wait(ct_ready, *events_of(freed))
                for s in range(ST):
                    mm = nc.tensor.matmul(bank[:, 0:D], ctl[b % 2][:, s, :], yt[:, s, :], start=s == 0, stop=s == ST - 1)
                ct_read[b] = pe.done(mm)
                xt_ring.release(n, self.update(b, bank[:, 0:D], 6, ct_read[b]))
                pend[b] = self.ln_stats(b)
            if b >= 2:
                self.ln_apply(b - 2, pend[b - 2])
                self.ln_transpose(b - 2, misc)

    def peer(self):
        nc, pe, act, dve, pool, sp, d = self.nc, self.pe, self.act, self.dve, self.pool, self.sp, self.d
        V, G = nc.vector, nc.gpsimd
        self.phase()
        free = self.region_free
        QT = QH * QD // P
        NG = 2 * QH
        wq, down, up = self.tmp("wq", [P, KD, QH * QD]), self.tmp("downT", [P, KD, D]), self.tmp("up", [P, 2, D])
        bq, gamma, beta = self.tmp("bq", [P, QT]), self.tmp("gamma", [P, 1]), self.tmp("beta", [P, 1])
        keys, keysq, kn = self.tmp("keys", [P, 32]), self.tmp("keys_sq", [P, 32]), self.tmp("key_norm", [P, 1])
        kdiag, kT = self.tmp("keys_diag", [P, P]), self.tmp("keys_diag_T", [P, P])
        blocks32, pairm = self.tmp("block_of_32", [P, 4]), self.tmp("pair_mean", [P, P])
        q = self.tmp("queries_T", [P, QT, T])
        qst, qmv, ex2 = self.tmp("q_stats", [P, QT, 4, 6]), self.tmp("q_mv", [P, QT, 2]), self.tmp("q_ex2", [P, QT, 1])
        mom, var, sc, sh = self.tmp("moments", [P, 2]), self.tmp("q_var", [P, 1]), self.tmp("q_scale", [P, 1]), self.tmp("q_shift", [P, 1])
        gl = self.tmp("gelu", [P, B, D])
        reset = self.tmp("reset", [P, NG, NKEY])
        ws = self.arrivals("peer_w")
        self.load(ws, wq, d["L3f_Wq"], *free)
        self.load(ws, bq, d["L3f_bq"])
        for i in range(2):
            for name, m in (("gamma", gamma), ("beta", beta)):
                self.load(ws, m[i * QD:(i + 1) * QD, :], d["L3f_" + name])
            for j in range(2):
                at = (2 * i + j) * NKEY
                self.load(ws, keys[at:at + NKEY, :], d[f"key{j}"])
        self.load(ws, down, d["downT"])
        w_ready = self.load(ws, up, d["up"])
        pool.wait(*free)
        pool.done(G.memset(kdiag, 0.0))
        e = pool.done(G.memset(reset, 1.0))
        pool.wait(e)
        set_ready = pool.done(G.memset(reset[:, :, 0:1], 0.0))
        dve.wait(w_ready, set_ready, *free)
        e = dve.done(V.tensor_tensor(keysq, keys, keys, ALU.mult))
        dve.wait(e)
        e = dve.done(V.tensor_reduce(kn, keysq, AX.X, ALU.add))
        dve.wait(e)
        e = dve.done(V.tensor_scalar(kn, kn, 1e-24, None, ALU.max))
        pool.wait(e)
        e = pool.done(G.tensor_tensor(kn, kn, self.half_power[:, 0:1], ALU.pow))
        dve.wait(e)
        for i in range(4):
            r = slice(i * NKEY, (i + 1) * NKEY)
            kd_ready = dve.done(V.tensor_scalar(kdiag[r, r], keys[r, :], kn[r, :], None, ALU.mult))
        b32_ready = dve.done(V.tensor_reduce(blocks32, self.ident.rearrange("p (i c) -> p i c", c=32), AX.X, ALU.add))
        ids = self.ident.rearrange("p (i c) -> p i c", i=2)
        e = dve.done(V.tensor_tensor(pairm[:, 0:QD], ids[:, 0, :], ids[:, 1, :], ALU.add))
        dve.wait(e)
        e = dve.done(V.tensor_scalar(pairm[:, 0:QD], pairm[:, 0:QD], 1.0 / QH, None, ALU.mult))
        dve.wait(e)
        pm_ready = dve.done(V.tensor_copy(pairm[:, QD:P], pairm[:, 0:QD]))
        ring, misc = Ring(self.banks[0:4]), Ring(self.banks[4:6])
        pe.wait(kd_ready, *free)
        n, bank, _ = misc.take()
        e = pe.done(self.transpose(bank[:, 0:P], kdiag))
        act.wait(e, *free)
        kT_ready = act.done(nc.scalar.activation(kT, bank[:, 0:P], ACT.Copy))
        misc.release(n, kT_ready)
        for g in range(4):
            pe.wait(w_ready, *self.xnT_ready[4 * g:4 * g + 4])
            for m in range(QT):
                n, bank, freed = ring.take()
                pe.wait(*events_of(freed))
                for k in range(KD):
                    mm = nc.tensor.matmul(bank, wq[:, k, m * P:(m + 1) * P], self.xnT[:, k, g * 512:(g + 1) * 512],
                                          start=k == 0, stop=k == KD - 1)
                act.wait(pe.done(mm), w_ready)
                e = act.done(nc.scalar.activation(q[:, m, g * 512:(g + 1) * 512], bank, ACT.Identity, bias=bq[:, m:m + 1]))
                ring.release(n, e)
                dve.wait(e)
                st_ready = dve.done(V.bn_stats(qst[:, m, g, :], q[:, m, g * 512:(g + 1) * 512]))
        for b in range(B):
            n, bank, freed = ring.take()
            pe.wait(*events_of(freed))
            for k in range(KD):
                mm = nc.tensor.matmul(bank[:, 0:D], self.xnT[:, k, b * P:(b + 1) * P], down[:, k, :], start=k == 0, stop=k == KD - 1)
            act.wait(pe.done(mm))
            gelu_ready = act.done(nc.scalar.activation(gl[:, b, :], bank[:, 0:D], ACT.Gelu))
            ring.release(n, gelu_ready)
        dve.wait(st_ready)
        for m in range(QT):
            e = dve.done(V.bn_aggr(qmv[:, m, :], qst[:, m, :, :].rearrange("p g s -> p (g s)")))
        dve.wait(e)
        e = dve.done(V.tensor_tensor(ex2, qmv[:, :, 0:1], qmv[:, :, 0:1], ALU.mult))
        dve.wait(e)
        e = dve.done(V.tensor_tensor(qmv[:, :, 1:2], qmv[:, :, 1:2], ex2, ALU.add))
        n, bank, freed = misc.take()
        pe.wait(e, pm_ready, *events_of(freed))
        for m in range(QT):
            mm = nc.tensor.matmul(bank[:, 0:2], pairm, qmv[:, m, :], start=m == 0, stop=m == QT - 1)
        dve.wait(pe.done(mm))
        e = dve.done(V.tensor_copy(mom, bank[:, 0:2]))
        misc.release(n, e)
        dve.wait(e)
        e = dve.done(V.tensor_tensor(var, mom[:, 0:1], mom[:, 0:1], ALU.mult))
        dve.wait(e)
        e = dve.done(V.tensor_tensor(var, mom[:, 1:2], var, ALU.subtract))
        dve.wait(e)
        e = dve.done(V.tensor_scalar(var, var, EPS, None, ALU.add))
        pool.wait(e)
        e = pool.done(G.tensor_tensor(var, var, self.half_power[:, 0:1], ALU.pow))
        dve.wait(e)
        e = dve.done(V.tensor_tensor(sc, var, gamma, ALU.mult))
        dve.wait(e)
        e = dve.done(V.tensor_tensor(sh, mom[:, 0:1], sc, ALU.mult))
        dve.wait(e)
        e = dve.done(V.tensor_tensor(sh, beta, sh, ALU.subtract))
        dve.wait(e)

        s_buf = [self.tmp("scores", [P, NG, NKEY]) for _ in range(2)]
        sq = [self.tmp("q_squares", [P, QT, P]) for _ in range(2)]
        ge, gt = self.tmp("at_least", [P, NG, NKEY]), self.tmp("greater", [P, NG, NKEY])
        cnt = self.tmp("equal_count", [P, NG, NKEY])
        inv, v8 = self.tmp("inv_norm", [P, NG]), self.tmp("top8", [P, NG, 8])
        g4, need, zsum = self.tmp("greater4", [P, NG, 4]), self.tmp("need", [P, NG]), self.tmp("exp_sum", [P, NG])
        prod = [self.tmp("expert_weight_parts", [P, D, QH]) for _ in range(1)]
        wt, restw = self.tmp("expert_weight", [P, D]), self.tmp("rest_weight", [P, 1])
        wg, wgT = self.tmp("weighted", [P, D]), self.tmp("weighted_T", [P, 2, P])
        spread = lambda m: m[:, :, None].to_broadcast([P, NG, NKEY])
        flat = lambda m: m.rearrange("p g k -> p (g k)")
        s_banks, n_bank = Ring(self.banks[0:2]), Ring(self.banks[2:4])
        s_banks.release(0, gelu_ready)
        s_banks.release(1, gelu_ready)
        n_bank.release(0, gelu_ready)
        n_bank.release(1, gelu_ready)
        s_read, wgT_read, wg_read, prod_read = {}, None, None, None
        for b in range(B):
            ts = slice(b * P, (b + 1) * P)
            c = b % 2
            dve.wait(s_read.get(b - 2))
            qn = dve.done(V.tensor_scalar(q[:, :, ts], q[:, :, ts], sc, sh, ALU.mult, ALU.add))
            act.wait(qn, s_read.get(b - 2))
            sq_ready = act.done(nc.scalar.activation(sq[c], q[:, :, ts], ACT.Square))
            n1, sbank, f1 = s_banks.take()
            n2, nbank, f2 = n_bank.take()
            pe.wait(qn, kT_ready, *events_of(f1))
            for m in range(QT):
                mm = nc.tensor.matmul(sbank[:, m * P:(m + 1) * P], q[:, m, ts], kT, start=True, stop=True)
            pe.wait(sq_ready, b32_ready, *events_of(f2))
            for m in range(QT):
                mm = nc.tensor.matmul(nbank[:, m * 4:(m + 1) * 4], sq[c][:, m, :], blocks32, start=True, stop=True)
            s_read[b] = pe.done(mm)
            dve.wait(s_read[b])
            e = dve.done(V.tensor_scalar(inv, nbank[:, 0:NG], 1e-24, None, ALU.max))
            n_bank.release(n2, e)
            pool.wait(e)
            e = pool.done(G.tensor_tensor(inv, inv, self.half_power[:, 0:1].to_broadcast([P, NG]), ALU.pow))
            dve.wait(e)
            s = s_buf[c]
            e = dve.done(V.tensor_tensor(s, sbank.rearrange("p (g k) -> p g k", k=NKEY), spread(inv), ALU.mult))
            s_banks.release(n1, e)
            dve.wait(e)
            for g in range(NG):
                e = dve.done(V.max(v8[:, g, :], s[:, g, :]))
            dve.wait(e)
            kth = v8[:, :, TOPK - 1:TOPK]
            kth_all = kth.to_broadcast([P, NG, NKEY])
            e1 = dve.done(V.tensor_tensor(ge, s, kth_all, ALU.is_ge))
            e2 = dve.done(V.tensor_tensor(gt, s, kth_all, ALU.is_gt))
            e3 = dve.done(V.tensor_tensor(g4, v8[:, :, 0:TOPK], kth.to_broadcast([P, NG, TOPK]), ALU.is_gt))
            dve.wait(e2, e3)
            e = dve.done(V.tensor_tensor(ge, ge, gt, ALU.subtract))
            e3 = dve.done(V.tensor_reduce(need, g4, AX.X, ALU.add))
            dve.wait(e3)
            e3 = dve.done(V.tensor_scalar(need, need, -1.0, float(TOPK), ALU.mult, ALU.add))
            e4 = dve.done(V.tensor_tensor(s, s, v8[:, :, 0:1].to_broadcast([P, NG, NKEY]), ALU.subtract))
            act.wait(e4)
            ex = act.done(nc.scalar.activation(s, s, ACT.Exp))
            dve.wait(e)
            e = dve.done(V.tensor_tensor_scan(flat(cnt), flat(reset), flat(ge), 0.0, ALU.mult, ALU.add))
            dve.wait(e, e3)
            e = dve.done(V.tensor_tensor(cnt, cnt, spread(need), ALU.is_le))
            dve.wait(e)
            e = dve.done(V.tensor_tensor(ge, ge, cnt, ALU.mult))
            dve.wait(e)
            e = dve.done(V.tensor_tensor(gt, gt, ge, ALU.add))
            dve.wait(e, ex)
            e = dve.done(V.tensor_tensor(s, s, gt, ALU.mult))
            dve.wait(e)
            e = dve.done(V.tensor_reduce(zsum, s, AX.X, ALU.add))
            dve.wait(e)
            e = dve.done(V.reciprocal(zsum, zsum))
            dve.wait(e)
            e = dve.done(V.tensor_tensor(s, s, spread(zsum), ALU.mult))
            dve.wait(e)
            halves = s.rearrange("p (h c) k -> p c k h", c=2)
            rows_i = D // NKEY
            first = halves[:, 0, 0:rows_i, :][:, :, None, :].to_broadcast([P, rows_i, NKEY, QH])
            second = halves[:, 1, :, :][:, None, :, :].to_broadcast([P, rows_i, NKEY, QH])
            pool.wait(e, prod_read)
            pr = pool.done(G.tensor_tensor(prod[0].rearrange("p (i j) h -> p i j h", i=rows_i), first, second, ALU.mult))
            e1 = dve.done(V.tensor_reduce(restw, halves[:, 0, rows_i:, :], AX.XY, ALU.add))
            dve.wait(pr)
            e = prod_read = dve.done(V.tensor_reduce(wt, prod[0], AX.X, ALU.add))
            dve.wait(e, e1)
            e = dve.done(V.tensor_tensor(wt[:, D - 1:D], wt[:, D - 1:D], restw, ALU.add))
            dve.wait(e, gelu_ready, wg_read)
            e = dve.done(V.tensor_tensor(wg, wt, gl[:, b, :], ALU.mult))
            n, bank, freed = misc.take()
            pe.wait(e, *events_of(freed))
            for k in range(2):
                mm = self.transpose(bank[:, k * P:(k + 1) * P], wg[:, k * P:(k + 1) * P])
            wg_read = pe.done(mm)
            act.wait(wg_read, wgT_read)
            e = act.done(nc.scalar.activation(wgT, bank[:, 0:2 * P].rearrange("p (k t) -> p k t", k=2), ACT.Copy))
            misc.release(n, e)
            n, bank, freed = misc.take()
            pe.wait(e, *events_of(freed))
            for k in range(2):
                mm = nc.tensor.matmul(bank[:, 0:D], wgT[:, k, :], up[:, k, :], start=k == 0, stop=k == 1)
            wgT_read = pe.done(mm)
            misc.release(n, self.update(b, bank[:, 0:D], 7, wgT_read))

    def update(self, b, y, gate, *after):
        self.dve.wait(self.x_ready[b], *after)
        self.x_ready[b] = self.dve.done(self.nc.vector.scalar_tensor_tensor(
            self.x[:, b, :], y, self.gates[:, gate:gate + 1], self.x[:, b, :], ALU.mult, ALU.add))
        return self.x_ready[b]

    def finish(self):
        stores = self.arrivals("out_store")
        self.sp.wait(*self.x_ready)
        e = stores.of(self.nc.sync.dma_start(self.out.rearrange("b s d -> s b d"), self.x))
        self.sp.wait(e)


def program(nc, d, out, stop=8, start=0):
    core = Core(nc, d, out)
    core.constants()
    core.first_layernorm()
    layers = [
        lambda: core.attention(0, 16, 4, 0.25, True, None),
        lambda: core.moe(0, E0, I0, 1),
        lambda: core.attention(1, 16, 4, 0.25, True, "pairs"),
        lambda: core.moe(1, E1, I1, 2),
        lambda: core.attention(2, 16, 4, 0.25, True, None),
        lambda: core.soft_moe(),
        lambda: core.attention(3, 64, 2, 0.125, False, "keys"),
        lambda: core.peer(),
    ]
    for layer in layers[start:stop]:
        layer()
    core.finish()


def laid_out(x):
    a = {k: np.asarray(v) for k, v in x.items()}
    rows = lambda w: np.ascontiguousarray(w.reshape(-1, P, w.shape[-1]).transpose(1, 0, 2))
    column = lambda v: np.ascontiguousarray(v.reshape(-1, P).T)
    d = {"x": a["x"], "g_xattn": a["g_xattn"][None], "g_ffn": a["g_ffn"][None]}
    d["ctxT"] = rows(np.ascontiguousarray(a["ctx_1024"].reshape(T, D).T))
    d["mask_keys"] = a["mask_BxS2_bk0"].reshape(1, T)
    d["rel"] = a["fside_Bx1xSxS2_0"][:, 0]
    d["relT"] = np.ascontiguousarray(d["rel"].transpose(0, 2, 1))
    keep = a["mask_BxSxS2_bk0"]
    d["keep"] = keep
    d["keepT"] = np.ascontiguousarray(keep.transpose(0, 2, 1))
    for n, out_name in ((0, "o"), (1, "out"), (2, "o")):
        for name in ("q", "k", "v", out_name):
            w = a[f"L{n}_xattn_W{name}"]
            short = name[0]
            d[f"L{n}_W{short}"] = rows(w if n == 0 else np.ascontiguousarray(w.T))
            b = a[f"L{n}_xattn_b{name}"]
            d[f"L{n}_b{short}"] = column(b) if short in "qk" else b[None]
    for name in "QKVO":
        d[f"L3_W{name.lower()}"] = rows(a[f"L3_xattn_W_{name}"])

    def experts(gate, up, down):
        n, inter, _ = gate.shape
        both = np.stack([gate, up], 1).reshape(n, 2, inter, KD, P).transpose(0, 4, 3, 1, 2).reshape(n, P, -1)
        chunks = -(-inter // P)
        low = np.zeros((n, chunks * P, D), down.dtype)
        low[:, :inter] = down.transpose(0, 2, 1)
        low = low.reshape(n, chunks, P, D).transpose(0, 2, 1, 3).reshape(n, P, -1)
        return np.concatenate([both, low], 2).reshape(n * P, -1)

    d["L0_experts"] = experts(a["L0_ffn_gate_w"], a["L0_ffn_up_w"], a["L0_ffn_down_w"])
    d["L1_experts"] = experts(a["L1_ffn_w1"], a["L1_ffn_w3"], a["L1_ffn_w2"])
    d["L1_shared"] = experts(a["L1_ffn_sw1"][None], a["L1_ffn_sw3"][None], a["L1_ffn_sw2"][None])
    d["L0_router"] = rows(np.ascontiguousarray(a["L0_ffn_router_w"].T))
    d["L1_router"] = rows(np.ascontiguousarray(a["L1_ffn_gate_w"].T))
    d["L1_gate_bias"] = a["L1_ffn_gate_bias"][None]
    d["phiT"] = rows(np.ascontiguousarray(a["L2_ffn_phi_w"].T))
    d["phi_b"] = a["L2_ffn_phi_b"][None]
    d["expert_w"] = np.ascontiguousarray(a["L2_ffn_expert_w"].reshape(ST, 4, KD, P, D).transpose(0, 3, 1, 2, 4))
    d["expert_b"] = np.ascontiguousarray(a["L2_ffn_expert_b"].reshape(ST, 4, D).transpose(1, 0, 2))
    d["L3f_Wq"] = rows(a["L3_ffn_Wq"])
    d["L3f_bq"] = column(a["L3_ffn_bq"])
    d["L3f_gamma"], d["L3f_beta"] = a["L3_ffn_bn_gamma"][:, None], a["L3_ffn_bn_beta"][:, None]
    d["key0"], d["key1"] = a["L3_ffn_sub_key0"], a["L3_ffn_sub_key1"]
    d["downT"] = rows(np.ascontiguousarray(a["L3_ffn_expert_down"].T))
    d["up"] = rows(a["L3_ffn_expert_up"])
    return d


def kernel(**inputs):
    import concourse.bacc as _bacc
    from concourse.bass_utils import run_bass_kernel_spmd as _run

    nc = _bacc.Bacc("TRN2", target_bir_lowering=False, num_devices=1)
    arrays = laid_out(inputs)
    d = {k: nc.dram_tensor(f"in_{k}", list(v.shape), mybir.dt.from_np(v.dtype), kind="ExternalInput").ap()
         for k, v in arrays.items()}
    out = nc.dram_tensor("out", [B, S, D], F32, kind="ExternalOutput").ap()
    program(nc, d, out)
    r = _run(nc, [{f"in_{k}": v for k, v in arrays.items()}], core_ids=[0])
    return r.results[0]["out"]
```

```python
import numpy as np
import concourse.bass as bass
from concourse import mybir

F32, BF16, I32, U8 = mybir.dt.float32, mybir.dt.bfloat16, mybir.dt.int32, mybir.dt.uint8
ALU, ACT, AX = mybir.AluOpType, mybir.ActivationFunctionType, mybir.AxisListType

P = 128
B, S, D = 16, 128, 256
T = B * S
KD = D // P
HEADS = 16
EPS = 1e-5
BIG = 2.0 ** 100
E0, I0 = 8, 704
E1, I1 = 8, 512
SLOTS = 2048
NEXP, PSLOT = 64, 32
ST = SLOTS // P
QPARTS, KPARTS = (0, 0, 1, 1, 0, 2), (0, 1, 0, 1, 2, 0)
TERMS = len(QPARTS)
QH, QD, NKEY, TOPK = 8, 64, 32, 4


class Lane:

    def __init__(self, engine, semaphore):
        self.engine, self.semaphore = engine, semaphore
        self.count, self.waited = 0, {}

    def wait(self, *events):
        for event in events:
            if event is None:
                continue
            semaphore, value = event
            if self.waited.get(semaphore.num, 0) < value:
                self.engine.wait_ge(semaphore, value)
                self.waited[semaphore.num] = value

    def done(self, instruction):
        self.count += 1
        instruction.then_inc(self.semaphore, 1)
        return (self.semaphore, self.count)

    @property
    def last(self):
        return (self.semaphore, self.count) if self.count else None


class Arrivals:

    def __init__(self, semaphore):
        self.semaphore, self.count = semaphore, 0

    def of(self, dma):
        self.count += 16
        dma.then_inc(self.semaphore, 16)
        return (self.semaphore, self.count)


class Ring:

    def __init__(self, buffers):
        self.buffers, self.freed, self.at = buffers, [None] * len(buffers), -1

    def take(self):
        self.at = (self.at + 1) % len(self.buffers)
        return self.at, self.buffers[self.at], self.freed[self.at]

    def release(self, n, *events):
        self.freed[n] = events[0] if len(events) == 1 else events


def events_of(freed):
    if freed is None:
        return ()
    return freed if isinstance(freed[0], tuple) else (freed,)


class Core:
    def __init__(self, nc, d, out):
        self.nc, self.d, self.out = nc, d, out
        self.pe = Lane(nc.tensor, nc.alloc_semaphore("pe_done"))
        self.act = Lane(nc.scalar, nc.alloc_semaphore("act_done"))
        self.dve = Lane(nc.vector, nc.alloc_semaphore("dve_done"))
        self.pool = Lane(nc.gpsimd, nc.alloc_semaphore("pool_done"))
        self.sp = Lane(nc.sync, nc.alloc_semaphore("sp_done"))
        self.floor = nc.sbuf_base // 32 * 32 + 32
        self.names = 0
        self.region_free = ()
        self.stores, self.stored = Arrivals(nc.alloc_semaphore("out_store")), None
        self.x_ready = [None] * B
        self.xn_ready = [None] * B
        self.xnT_ready = [None] * B
        self.x = self.sb("x_residual", [P, B, D])
        self.xn = self.sb("x_normed", [P, B, D])
        self.xnT = self.sb("x_normed_T", [P, KD, T])
        self.ctxT = self.sb("context_T", [P, KD, T])
        self.banks = [nc.alloc_psum_tensor(f"bank{i}", [P, 512], F32).ap() for i in range(8)]

    def place(self, name, shape, dtype, offset):
        size = {F32: 4, BF16: 2, I32: 4, U8: 1}[dtype] * int(np.prod(shape[1:]))
        self.names += 1
        t = self.nc.alloc_sbuf_tensor_at(f"{name}_{self.names}", shape, dtype, offset=offset)
        return t.ap(), offset + (size + 31) // 32 * 32

    def sb(self, name, shape, dtype=F32):
        ap, self.floor = self.place(name, shape, dtype, self.floor)
        return ap

    def phase(self):
        self.region_free = tuple(x.last for x in (self.pe, self.act, self.dve, self.pool) if x.last)
        self.at = self.floor

    def tmp(self, name, shape, dtype=F32):
        ap, self.at = self.place(name, shape, dtype, self.at)
        return ap

    def arrivals(self, name):
        self.names += 1
        return Arrivals(self.nc.alloc_semaphore(f"{name}_{self.names}"))

    def load(self, arrivals, dst, src, *after):
        self.sp.wait(*after)
        return arrivals.of(self.nc.sync.dma_start(dst, src))

    def transpose(self, out, in_):
        return self.nc.tensor.transpose(out, in_, self.ident)

    def constants(self):
        nc, pool, dve, d = self.nc, self.pool, self.dve, self.d
        self.ident = self.sb("identity", [P, P])
        self.ones = self.sb("ones", [P, P])
        self.before = self.sb("strictly_before", [P, P])
        self.neg_ident = self.sb("minus_identity", [P, P], BF16)
        self.identb = self.sb("identity_bf16", [P, P], BF16)
        self.onesb = self.sb("ones_bf16", [P, P], BF16)
        self.par = self.sb("lower_upper_half", [P, 2])
        self.gates = self.sb("gates", [P, 8])
        self.half_power = self.sb("minus_half", [P, B])
        self.stats = self.sb("ln_stats", [P, B, 6])
        self.meanvar = self.sb("ln_mean_var", [P, B, 2])
        self.vareps = self.sb("ln_var_eps", [P, B])
        self.rstd = self.sb("ln_rstd", [P, B])
        g = nc.gpsimd
        pool.done(g.memset(self.ident, 0.0))
        pool.done(g.memset(self.identb, 0.0))
        pool.done(g.memset(self.neg_ident, 0.0))
        pool.done(g.memset(self.ones, 1.0))
        pool.done(g.memset(self.onesb, 1.0))
        zeroed = pool.done(g.memset(self.half_power, -0.5))
        pool.wait(zeroed)
        for m, value in ((self.ident, 1.0), (self.identb, 1.0), (self.neg_ident, -1.0)):
            pool.done(g.affine_select(out=m, in_=m, compare_op=ALU.not_equal, fill=value, base=0,
                                      pattern=[[-1, P]], channel_multiplier=1))
        self.const_ready = pool.done(g.affine_select(
            out=self.before, in_=self.ones, compare_op=ALU.is_gt, fill=0.0, base=0,
            pattern=[[1, P]], channel_multiplier=-1))
        dve.wait(self.const_ready)
        cols = self.ident.rearrange("p (c r) -> p c r", c=2)
        for c in range(2):
            self.par_ready = dve.done(nc.vector.tensor_reduce(
                self.par[:, c:c + 1], cols[:, c, :], AX.X, ALU.add))
        small = self.arrivals("small_loads")
        self.load(small, self.gates[:, 0:4], d["g_xattn"].to_broadcast([P, 4]))
        loaded = self.load(small, self.gates[:, 4:8], d["g_ffn"].to_broadcast([P, 4]))
        self.act.wait(loaded)
        self.gates_ready = self.act.done(nc.scalar.activation(self.gates, self.gates, ACT.Tanh))
        for b in range(0, B, 2):
            xs = self.arrivals("x_load")
            self.x_ready[b] = self.x_ready[b + 1] = self.load(xs, self.x[:, b:b + 2, :], d["x"][b:b + 2].rearrange("b s d -> s b d"))
        cs = self.arrivals("context_load")
        self.ctx_ready = self.load(cs, self.ctxT, d["ctxT"])
        dve.wait(self.gates_ready)

    def ln_stats(self, b):
        nc, dve, pool = self.nc, self.dve, self.pool
        dve.wait(self.x_ready[b])
        e = dve.done(nc.vector.bn_stats(self.stats[:, b, :], self.x[:, b, :]))
        dve.wait(e)
        aggregated = dve.done(nc.vector.bn_aggr(self.meanvar[:, b, :], self.stats[:, b, :]))
        pool.wait(aggregated)
        e = pool.done(nc.gpsimd.tensor_scalar(self.vareps[:, b:b + 1], self.meanvar[:, b, 1:2], EPS, None, ALU.add))
        pool.wait(e)
        self.rstd_ready = pool.done(nc.gpsimd.tensor_tensor(
            self.rstd[:, b:b + 1], self.vareps[:, b:b + 1], self.half_power[:, 0:1], ALU.pow))
        return self.rstd_ready

    def ln_apply(self, b, rstd_ready, *readers):
        dve = self.dve
        dve.wait(rstd_ready, *readers)
        self.xn_ready[b] = dve.done(self.nc.vector.tensor_scalar(
            self.xn[:, b, :], self.x[:, b, :], self.meanvar[:, b, 0:1], self.rstd[:, b:b + 1],
            ALU.subtract, ALU.mult))

    def ln_transpose(self, b, ring):
        pe, act = self.pe, self.act
        n, bank, freed = ring.take()
        pe.wait(self.xn_ready[b], *events_of(freed))
        for k in range(KD):
            turned = self.transpose(bank[:, k * P:(k + 1) * P], self.xn[:, b, k * P:(k + 1) * P])
        act.wait(pe.done(turned))
        self.xnT_ready[b] = act.done(self.nc.scalar.activation(
            self.xnT[:, :, b * P:(b + 1) * P], bank[:, 0:KD * P].rearrange("p (k t) -> p k t", k=KD), ACT.Copy))
        ring.release(n, self.xnT_ready[b])

    def first_layernorm(self):
        ring = Ring(self.banks[6:8])
        self.pe.wait(self.const_ready)
        pend = {}
        for b in range(B + 2):
            if b < B:
                pend[b] = self.ln_stats(b)
            if 2 <= b:
                self.ln_apply(b - 2, pend[b - 2])
                self.ln_transpose(b - 2, ring)

    def attention(self, layer, dk, group, scale, bias, mask):
        nc, pe, act, dve, pool, sp, d = self.nc, self.pe, self.act, self.dve, self.pool, self.sp, self.d
        small = dk == 16
        width = HEADS * dk
        tiles = width // P
        dv1 = dk + 1
        tok = group * P
        pre = f"L{layer}_"
        self.phase()
        wq = self.tmp("wq", [P, KD, width])
        wk = self.tmp("wk", [P, KD, width])
        wv = self.tmp("wv", [P, KD, width])
        wo = self.tmp("wo", [P, tiles, D])
        if small:
            raw = [self.tmp("projected", [P, tok]) for _ in range(2)]
            parts = [self.tmp("parts", [P, 3, tiles, tok], BF16) for _ in range(2)]
            stack = {k: [self.tmp(f"{k}_stack", [TERMS * dk, HEADS, tok], BF16) for _ in range(2)] for k in "qk"}
            parts_dram = [[nc.dram_tensor(f"parts_{layer}_{k}{i}", [3, width, tok], BF16, kind="Internal").ap()
                           for i in range(2)] for k in "qk"]
            parts_sem = [[self.arrivals("parts_store") for _ in range(2)] for _ in "qk"]
            stack_sem = [[self.arrivals("stack_load") for _ in range(2)] for _ in "qk"]
            raw_ring, parts_ring = Ring(raw), Ring(parts)
        else:
            qT = [[self.tmp("qT", [P, tiles, tok]) for _ in range(2)] for _ in range(2)]
            kT = [self.tmp("kT", [P, tiles, tok]) for _ in range(2)]
            qb = [self.tmp("q_bf16", [P, tiles, tok], BF16) for _ in range(2)]
            kb = [self.tmp("k_bf16", [P, tiles, tok], BF16) for _ in range(2)]
        v1 = [self.tmp("v_and_ones", [P, group, HEADS, dv1]) for _ in range(2)]
        probs = [self.tmp("probsT", [P, 4, P]) for _ in range(4)]
        maxes = [self.tmp("row_max", [P, 2, 4], BF16) for _ in range(2)]
        recips = [self.tmp("recips", [P, HEADS]) for _ in range(2)]
        o_row = [self.tmp("attn_out", [P, HEADS, dk]) for _ in range(2)]
        o_col = [self.tmp("attn_outT", [P, tiles, P]) for _ in range(2)]
        weights = self.arrivals("attn_weights")
        self.load(weights, wk, d[pre + "Wk"], *self.region_free)
        self.load(weights, wv, d[pre + "Wv"])
        self.load(weights, wq, d[pre + "Wq"])
        w_ready = self.load(weights, wo, d[pre + "Wo"])
        if bias:
            bq = self.tmp("bq", [P, tiles])
            bk = self.tmp("bk", [P, tiles])
            bv = self.tmp("bv", [P, width])
            gbo = self.tmp("gated_bo", [P, D])
            self.load(weights, bq, d[pre + "bq"])
            self.load(weights, bk, d[pre + "bk"])
            self.load(weights, bv, d[pre + "bv"].to_broadcast([P, width]))
            w_ready = self.load(weights, gbo, d[pre + "bo"].to_broadcast([P, D]))
            dve.wait(w_ready, self.par_ready, *self.region_free)
            gbo_ready = dve.done(nc.vector.tensor_scalar(gbo, gbo, self.gates[:, layer:layer + 1], None, ALU.mult))
        pool.wait(*self.region_free)
        for v in v1:
            ones_ready = pool.done(nc.gpsimd.memset(v[:, :, :, dk:dv1], 1.0))
        act.wait(*self.region_free)
        dve.wait(*self.region_free)
        if mask == "keys":
            kmask = o_col[1].rearrange("p t q -> p (t q)").bitcast(U8)[0:1, 0:T]
            kneg = self.tmp("key_neg", [1, T], BF16)
            kload = self.arrivals("key_mask")
            dve.wait(self.load(kload, kmask, d["mask_keys"]))
            kneg_ready = dve.done(nc.vector.tensor_scalar(kneg, kmask, -BIG, None, ALU.mult))
        if mask == "pairs":
            rt = [[self.tmp("rel", [P, P]) for _ in range(2)] for _ in range(2)]
            mk = [[self.tmp("keep", [P, P], U8) for _ in range(2)] for _ in range(2)]
            neg, kept = self.tmp("neg", [P, P]), self.tmp("kept", [P, P])
            r_q = [self.tmp("bias_qk", [P, P], BF16) for _ in range(2)]
            r_k = [self.tmp("bias_kq", [P, P]) for _ in range(2)]
            any_kept = self.tmp("any_kept", [P, B])
            rload = [self.arrivals("rel_load") for _ in range(2)]
            r_ready, r_read, any_ready = [None] * B, [None] * B, [None] * B

        s_bank, t_bank = self.banks[0:2], self.banks[2:4]
        o_ring, misc = Ring(self.banks[4:6]), Ring(self.banks[6:8])

        q_ready, k_ready, v_ready = {}, {}, {}
        pv_done = {}

        def project(g, kind, m):
            dst = g % 2
            before = (pv_done.get((g - 2) * group + group - 1),)
            n, bank, freed = misc.take()
            pe.wait(w_ready, *events_of(freed))
            if kind == "v":
                bi, half = m
                b = g * group + bi
                cols = min(width, 512)
                pe.wait(self.ctx_ready)
                for k in range(KD):
                    mm = nc.tensor.matmul(bank[:, 0:cols], self.ctxT[:, k, b * P:(b + 1) * P],
                                          wv[:, k, half * cols:(half + 1) * cols], start=k == 0, stop=k == KD - 1)
                hs = cols // dk
                target = v1[dst][:, bi, half * hs:(half + 1) * hs, 0:dk]
                src = bank[:, 0:cols].rearrange("p (h d) -> p h d", d=dk)
                if bias:
                    dve.wait(pe.done(mm), *before)
                    e = dve.done(nc.vector.tensor_tensor(
                        target, src, bv[:, half * cols:(half + 1) * cols].rearrange("p (h d) -> p h d", d=dk), ALU.add))
                else:
                    act.wait(pe.done(mm), *before)
                    e = act.done(nc.scalar.activation(target, src, ACT.Copy))
                v_ready[(g, bi)] = v_ready.get((g, bi), ()) + (e,)
                misc.release(n, e)
                return
            src = self.ctxT if kind == "k" else self.xnT
            w = wk if kind == "k" else wq
            if kind == "q":
                pe.wait(*[self.xnT_ready[b] for b in range(g * group, (g + 1) * group)])
            else:
                pe.wait(self.ctx_ready)
            for k in range(KD):
                mm = nc.tensor.matmul(bank[:, 0:tok], w[:, k, m * P:(m + 1) * P],
                                      src[:, k, g * tok:(g + 1) * tok], start=k == 0, stop=k == KD - 1)
            projected = pe.done(mm)
            if small:
                split(g, kind, m, n, bank, projected)
                return
            act.wait(projected, *before)
            dve.wait(*before)
            if kind == "k":
                e = act.done(nc.scalar.activation(kT[dst][:, m, :], bank[:, 0:tok], ACT.Copy))
                dve.wait(e)
                k_ready[g] = (e, dve.done(nc.vector.tensor_copy(kb[dst][:, m, :], bank[:, 0:tok])))
                misc.release(n, k_ready[g][1])
                return
            for c in range(2):
                e = act.done(nc.scalar.activation(qT[dst][c][:, m, :], bank[:, 0:tok], ACT.Copy,
                                                  scale=self.par[:, c:c + 1]))
            dve.wait(e)
            q_ready[g] = (e, dve.done(nc.vector.tensor_copy(qb[dst][:, m, :], bank[:, 0:tok])))
            misc.release(n, q_ready[g][1])

        def split(g, kind, m, n, bank, projected):
            i = "qk".index(kind)
            if m == 0:
                split.pn, split.parts, freed = parts_ring.take()
                split.before = events_of(freed)
            part = split.parts
            rn, y, rfreed = raw_ring.take()
            act.wait(projected, *split.before, *events_of(rfreed))
            bias_col = (bq if kind == "q" else bk)[:, m:m + 1]
            act.done(nc.scalar.activation(y, bank, ACT.Identity, bias=bias_col))
            e = act.done(nc.scalar.activation(part[:, 0, m, :], bank, ACT.Identity, bias=bias_col))
            misc.release(n, e)
            dve.wait(e)
            e = dve.done(nc.vector.tensor_tensor(y, y, part[:, 0, m, :], ALU.subtract))
            pool.wait(e, *split.before)
            e = pool.done(nc.gpsimd.tensor_copy(part[:, 1, m, :], y))
            pool.wait(e)
            e = pool.done(nc.gpsimd.tensor_tensor(part[:, 2, m, :], y, part[:, 1, m, :], ALU.subtract))
            raw_ring.release(rn, e)
            if m < tiles - 1:
                return
            c = g % 2
            sp.wait(e, *[x for x in (stack_ready.get((kind, g - 2)),) if x])
            stored = parts_sem[i][c].of(nc.sync.dma_start(
                parts_dram[i][c].rearrange("s (m p) c -> p s m c", p=P), part))
            parts_ring.release(split.pn, stored)
            if g == 0:
                load_stack(kind, g, stored)
            else:
                rest.setdefault(now[0] + 1, []).append(lambda: load_stack(kind, g, stored))

        def load_stack(kind, g, stored):
            i, c = "qk".index(kind), g % 2
            sp.wait(stored, pv_done.get((g - 2) * group + group - 1))
            for s, which in enumerate(QPARTS if kind == "q" else KPARTS):
                ready = stack_sem[i][c].of(nc.sync.dma_start(
                    stack[kind][c][s * dk:(s + 1) * dk, :, :], parts_dram[i][c][which].rearrange("(d h) c -> d h c", d=dk)))
            stack_ready[(kind, g)] = ready
            (q_ready if kind == "q" else k_ready)[g] = (ready,)

        stack_ready, now = {}, [0]

        def projections(g):
            steps = [(g, "k", m) for m in range(tiles)] + [(g, "q", m) for m in range(tiles)]
            return steps + [(g, "v", (bi, h)) for bi in range(group) for h in range((width + 511) // 512)]

        def pair_bias(b):
            c = b % 2
            after = (r_read[b - 2],) if b >= 2 else ()
            for i, (rel, keep) in enumerate((("rel", "keep"), ("relT", "keepT"))):
                self.load(rload[c], rt[c][i], d[rel][b], *(r_ready[b - 2] if b >= 2 else self.region_free))
                e = self.load(rload[c], mk[c][i], d[keep][b])
            pool.wait(e, *after)
            ends = []
            for i, dst in enumerate((r_q[c], r_k[c])):
                e1 = pool.done(nc.gpsimd.tensor_scalar(neg, mk[c][i], BIG, -BIG, ALU.mult, ALU.add))
                e2 = pool.done(nc.gpsimd.tensor_copy(kept, mk[c][i]))
                pool.wait(e2)
                e2 = pool.done(nc.gpsimd.tensor_tensor(rt[c][i], rt[c][i], kept, ALU.mult))
                pool.wait(e1, e2)
                e3 = pool.done(nc.gpsimd.tensor_tensor(dst, rt[c][i], neg, ALU.add))
                pool.wait(e3)
                ends.append(e3)
            dve.wait(e)
            any_ready[b] = dve.done(nc.vector.tensor_reduce(any_kept[:, b:b + 1], mk[c][0], AX.X, ALU.max))
            r_ready[b] = (ends[-1], any_ready[b])

        if small:
            quads = [list(range(4 * r, 4 * r + 4)) for r in range(4)]
        else:
            quads = [[2 * (4 * (r // 2) + i) + r % 2 for i in range(4)] for r in range(4)]

        def operands(h, b, exact):
            g, bi = b // group, b % group
            t = slice(bi * P, (bi + 1) * P)
            if small:
                return stack["q"][g % 2][:, h, t], stack["k"][g % 2][:, h, t]
            if exact:
                return qT[g % 2][h % 2][:, h // 2, t], kT[g % 2][:, h // 2, t]
            rows = slice(dk * (h % 2), dk * (h % 2 + 1))
            return qb[g % 2][rows, h // 2, t], kb[g % 2][rows, h // 2, t]

        units = [(b, pair) for b in range(B) for pair in range(2)]
        max_done, exp_done, pv_of, st_done = {}, {}, {}, {}
        s_free = [None, None]
        t_free = [None, None]

        def scores_for_max(u):
            b, pair = units[u]
            pe.wait(*q_ready[b // group], *k_ready[b // group], *s_free)
            if mask == "pairs":
                pe.wait(*r_ready[b])
            if mask == "keys":
                pe.wait(kneg_ready)
            for j in range(2):
                if mask == "pairs":
                    nc.tensor.matmul(s_bank[j].rearrange("p (h k) -> p h k", h=4), self.identb,
                                     r_q[b % 2][:, None, :].to_broadcast([P, 4, P]), start=True, stop=False, skip_group_check=True)
                if mask == "keys":
                    nc.tensor.matmul(s_bank[j].rearrange("p (h k) -> p h k", h=4), self.onesb[0:1, 0:P],
                                     kneg[0:1, None, b * P:(b + 1) * P].to_broadcast([1, 4, P]), start=True, stop=False, skip_group_check=True)
            for i in range(4):
                for j in range(2):
                    q, k = operands(quads[2 * pair + j][i], b, False)
                    mm = nc.tensor.matmul(s_bank[j][:, i * P:(i + 1) * P], q, k, start=mask is None, stop=True, skip_group_check=True)
            e = pe.done(mm)
            dve.wait(e, st_done.get(u - 2))
            for j in range(2):
                s_free[j] = dve.done(nc.vector.tensor_reduce(
                    maxes[u % 2][:, j, :], s_bank[j].rearrange("p (h k) -> p h k", h=4), AX.X, ALU.max))
            max_done[u] = s_free[1]

        def scores_for_exp(u):
            b, pair = units[u]
            pe.wait(max_done[u], *t_free)
            for j in range(2):
                if mask == "pairs":
                    nc.tensor.matmul(t_bank[j].rearrange("p (h q) -> p h q", h=4), self.ident,
                                     r_k[b % 2][:, None, :].to_broadcast([P, 4, P]), start=True, stop=False, skip_group_check=True)
                if mask == "keys":
                    nc.tensor.matmul(t_bank[j].rearrange("p (h q) -> p h q", h=4), kneg[0:1, b * P:(b + 1) * P],
                                     self.onesb[0:1, None, :].to_broadcast([1, 4, P]),
                                     start=True, stop=False, skip_group_check=True)
            for j in range(2):
                for i in range(4):
                    q, k = operands(quads[2 * pair + j][i], b, True)
                    region = t_bank[j][:, i * P:(i + 1) * P]
                    nc.tensor.matmul(region, maxes[u % 2][:, j, i:i + 1].to_broadcast([P, P]), self.neg_ident,
                                     start=mask is None, stop=False, skip_group_check=True)
                    mm = nc.tensor.matmul(region, k, q, start=False, stop=True, skip_group_check=True)
            e = st_done[u] = pe.done(mm)
            if mask == "pairs":
                r_read[b] = e
            act.wait(e, pv_of.get(u - 2))
            for j in range(2):
                t_free[j] = act.done(nc.scalar.activation(
                    probs[2 * (u % 2) + j].rearrange("p h q -> p (h q)"), t_bank[j], ACT.Exp, scale=scale))
            exp_done[u] = t_free[1]

        o_now = {}
        rest = {}

        def times_v(u):
            b, pair = units[u]
            g, bi = b // group, b % group
            pe.wait(exp_done[u], ones_ready, *v_ready[(g, bi)])
            orow = o_row[b % 2]
            for j in range(2):
                r = 2 * pair + j
                if not small or r == 0:
                    o_now[b] = o_ring.take()
                    pe.wait(*events_of(o_now[b][2]))
                n, bank, _ = o_now[b]
                for i, h in enumerate(quads[r]):
                    at = (h if small else i) * dv1
                    mm = nc.tensor.matmul(bank[:, at:at + dv1], probs[2 * (u % 2) + j][:, i, :],
                                          v1[g % 2][:, bi, h, :], start=True, stop=True)
                if small and r < 3:
                    continue
                heads = HEADS if small else 4
                full = bank[:, 0:heads * dv1].rearrange("p (h d) -> p h d", d=dv1)
                rec = recips[b % 2][:, 0:HEADS] if small else recips[b % 2][:, 4 * r:4 * r + 4]
                pv = pe.done(mm)
                dve.wait(pv, o_read.get(b - 2))
                e = dve.done(nc.vector.reciprocal(rec[:, :, None], full[:, :, dk:dv1]))
                dve.wait(e)
                if mask == "pairs":
                    dve.wait(any_ready[b])
                    e = dve.done(nc.vector.tensor_scalar(rec, rec, any_kept[:, b:b + 1], None, ALU.mult))
                    dve.wait(e)
                target = orow if small else orow.rearrange("p (r i c) d -> p r c i d", r=2, c=2)[:, r // 2, r % 2]
                e = dve.done(nc.vector.tensor_tensor(
                    target, full[:, :, 0:dk], rec[:, :, None].to_broadcast([P, heads, dk]), ALU.mult))
                o_ring.release(n, e)
                o_done[b] = e
            pv_of[u] = pe.done(mm) if (small and 2 * pair + 1 < 3) else pv
            if pair == 1:
                pv_done[b] = pv_of[u]

        o_done, o_read = {}, {}

        def turn_out(b):
            flat = o_row[b % 2].rearrange("p h d -> p (h d)")
            col = o_col[b % 2]
            pe.wait(o_done[b])
            if bias:
                pool.wait(self.xn_ready[b], self.x_ready[b], gbo_ready)
                self.x_ready[b] = pool.done(nc.gpsimd.tensor_tensor(self.x[:, b, :], self.x[:, b, :], gbo, ALU.add))
            for t0 in range(0, tiles, 4):
                n, bank, freed = misc.take()
                pe.wait(*events_of(freed))
                some = range(t0, min(tiles, t0 + 4))
                for t in some:
                    mm = self.transpose(bank[:, (t - t0) * P:(t - t0 + 1) * P], flat[:, t * P:(t + 1) * P])
                e = o_read[b] = pe.done(mm)
                act.wait(e, proj_done.get(b - 2))
                e = act.done(nc.scalar.activation(
                    col[:, t0:t0 + len(some), :], bank[:, 0:len(some) * P].rearrange("p (t q) -> p t q", q=P), ACT.Copy))
                misc.release(n, e)
            col_ready[b] = e

        col_ready, proj_done = {}, {}

        def out_project(b):
            n, bank, freed = misc.take()
            pe.wait(col_ready[b], *events_of(freed))
            for t in range(tiles):
                mm = nc.tensor.matmul(bank[:, 0:D], o_col[b % 2][:, t, :], wo[:, t, :],
                                      start=t == 0, stop=t == tiles - 1)
            e = proj_done[b] = pe.done(mm)
            misc.release(n, self.update(b, bank[:, 0:D], layer, e))
            pend[b] = self.ln_stats(b)

        pend = {}
        for step in projections(0):
            project(*step)
        if mask == "pairs":
            pair_bias(0)
        todo = []
        for u in range(len(units) + 9):
            now[0] = u
            for step in rest.pop(u, ()):
                step()
            if u < len(units):
                b, pair = units[u]
                if b % group == 0 and pair == 0 and b // group + 1 < B // group:
                    todo = projections(b // group + 1)
                    pace = -(-len(todo) // (2 * group - 1))
                if mask == "pairs" and pair == 1 and b + 1 < B:
                    pair_bias(b + 1)
                scores_for_max(u)
            if 1 <= u <= len(units):
                scores_for_exp(u - 1)
            if u < len(units) and not (b % group == 0 and pair == 0):
                for step in todo[:pace]:
                    project(*step)
                todo = todo[pace:]
            if 2 <= u <= len(units) + 1:
                times_v(u - 2)
                b, pair = units[u - 2]
                if pair == 1:
                    rest.setdefault(u + 1, []).append(lambda b=b: turn_out(b))
                    rest.setdefault(u + 2, []).append(lambda b=b: out_project(b))
                    rest.setdefault(u + 4, []).append(lambda b=b: self.ln_apply(b, pend[b]))
                    rest.setdefault(u + 5, []).append(lambda b=b: self.ln_transpose(b, misc))

    def first_max(self, values, pick, top, ramp, equal):
        nc, dve = self.nc, self.dve
        spread = lambda m: m[:, :, None].to_broadcast([P, B, 8])
        e = dve.done(nc.vector.tensor_reduce(top, values, AX.X, ALU.max))
        dve.wait(e)
        e = dve.done(nc.vector.tensor_tensor(equal, values, spread(top), ALU.is_equal))
        dve.wait(e)
        e = dve.done(nc.vector.tensor_tensor(equal, equal, ramp, ALU.mult))
        dve.wait(e)
        e = dve.done(nc.vector.tensor_reduce(top, equal, AX.X, ALU.max))
        dve.wait(e)
        e = dve.done(nc.vector.tensor_tensor(pick, equal, spread(top), ALU.is_equal))
        dve.wait(e)
        return e

    def moe(self, layer, experts, inter, topk):
        nc, pe, act, dve, pool, sp, d = self.nc, self.pe, self.act, self.dve, self.pool, self.sp, self.d
        V = nc.vector
        shared = layer == 1
        gate = 4 + layer
        blocks = T * topk // P + experts - 1
        chunks = -(-inter // P)
        last_rows = inter - (chunks - 1) * P
        wide = KD * 2 * inter + chunks * D
        groups, c = [], 0
        while c < chunks:
            n = 2 if c + 2 < chunks or (c + 2 == chunks and last_rows == P) else 1
            groups.append(list(range(c, c + n)))
            c += n
        self.phase()
        free = self.region_free
        nw = 3
        weights = [self.tmp("expert_w", [P, wide]) for _ in range(nw)]
        w_sems = [self.arrivals("expert_w") for _ in range(nw)]
        nr = 4
        rows = [self.tmp("block_rows", [P, D]) for _ in range(nr)]
        r_sems = [self.arrivals("block_rows") for _ in range(nr)]
        cols = [self.tmp("block_T", [P, KD, P]) for _ in range(2)]
        silu = [self.tmp("silu", [P, 2 * P]) for _ in range(2)]
        hid = [self.tmp("hidden", [P, chunks, P]) for _ in range(2)]
        youts = [self.tmp("block_out", [P, D]) for _ in range(3)]
        y_sems = [self.arrivals("block_out") for _ in range(3)]
        back = [self.tmp("gathered", [P, D]) for _ in range(B * topk)]
        b_sems = [self.arrivals("gathered") for _ in range(B)]
        xs_dram = nc.dram_tensor(f"sorted_x_{layer}", [blocks * P, D], F32, kind="Internal").ap()
        ys_dram = nc.dram_tensor(f"sorted_y_{layer}", [blocks * P, D], F32, kind="Internal").ap()
        t = lambda name, shape, dtype=F32: self.tmp(name, shape, dtype)
        BE = B * 8
        router = t("router", [P, KD, 8])
        zeros = t("zeros", [P, 2 * D])
        ramp, step, reset = t("ramp", [P, B, 8]), t("block_step", [P, 8, B]), t("reset", [P, 8, B])
        index = t("block_index", [P, blocks, 8])
        logits, equal, top = t("logits", [P, B, 8]), t("equal", [P, B, 8]), t("top", [P, B])
        picks = [t("pick", [P, B, 8]) for _ in range(topk)]
        both = t("either_pick", [P, B, 8])
        total, upto = t("tile_totals", [P, 8, B]), t("totals_upto", [P, 8, B])
        more, nblk, end, ones8 = t("more", [P, 8, B]), t("nblk", [P, 8]), t("end_block", [P, 8]), t("ones8", [P, 8])
        base, rank, tmp8 = t("base", [P, 8]), t("rank", [P, B, 8]), t("tmp8", [P, B, 8])
        past, eid, eid_i = t("past", [P, blocks, 8]), t("expert_row", [P, blocks]), t("expert_row_int", [P, blocks], I32)
        pos = [t("pos", [P, B]) for _ in range(topk)]
        pos_i = [t("pos_int", [P, B], I32) for _ in range(topk)]
        tw = [t("token_weight", [P, B]) for _ in range(topk)]

        g = nc.gpsimd
        pool.wait(*free)
        pool.done(g.iota(ramp, pattern=[[0, B], [-1, 8]], base=8, channel_multiplier=0, allow_small_or_imprecise_dtypes=True))
        pool.done(g.iota(step, pattern=[[0, 8], [P, B]], base=0, channel_multiplier=0, allow_small_or_imprecise_dtypes=True))
        pool.done(g.iota(index, pattern=[[1, blocks], [0, 8]], base=0, channel_multiplier=0, allow_small_or_imprecise_dtypes=True))
        pool.done(g.memset(zeros, 0.0))
        pool.done(g.memset(ones8, 1.0))
        e = pool.done(g.memset(reset, 1.0))
        pool.wait(e)
        tables_ready = pool.done(g.memset(reset[:, :, 0:1], 0.0))
        zero_sem = self.arrivals("zero_fill")
        sp.wait(tables_ready)
        half = blocks * P // (2 * P)
        zero_done = zero_sem.of(nc.sync.dma_start(
            xs_dram[0:half * 2 * P, :].rearrange("(p n r) d -> p n (r d)", p=P, r=2),
            zeros[:, None, :].to_broadcast([P, half, 2 * D])))
        if blocks % 2:
            zero_done = zero_sem.of(nc.sync.dma_start(xs_dram[half * 2 * P:, :], zeros[:, 0:D]))
        small = self.arrivals("router_w")
        router_ready = self.load(small, router, d[f"L{layer}_router"], *free)
        if shared:
            bias8 = t("gate_bias", [P, 8])
            router_ready = self.load(small, bias8, d["L1_gate_bias"].to_broadcast([P, 8]))
            shared_w = t("shared_w", [P, wide])
            shared_sem = self.arrivals("shared_w")
            shared_ready = self.load(shared_sem, shared_w, d["L1_shared"])

        rb = self.banks[0]
        pe.wait(router_ready, *self.xnT_ready, *free)
        for b in range(B):
            for k in range(KD):
                mm = nc.tensor.matmul(rb[:, b * 8:(b + 1) * 8], self.xnT[:, k, b * P:(b + 1) * P], router[:, k, :],
                                      start=k == 0, stop=k == KD - 1)
        dve.wait(pe.done(mm), tables_ready, router_ready, *free)
        spread = lambda m: m[:, :, None].to_broadcast([P, B, 8])
        bank3 = rb[:, 0:BE].rearrange("p (b e) -> p b e", e=8)
        e = dve.done(V.tensor_copy(logits, bank3))
        dve.wait(e)
        if shared:
            prob = t("router_prob", [P, B, 8])
            e = dve.done(V.tensor_reduce(top, logits, AX.X, ALU.max))
            dve.wait(e)
            e = dve.done(V.tensor_tensor(logits, logits, spread(top), ALU.subtract))
            act.wait(e)
            e = act.done(nc.scalar.activation(prob, logits, ACT.Exp))
            dve.wait(e)
            e = dve.done(V.tensor_reduce(top, prob, AX.X, ALU.add))
            dve.wait(e)
            e = dve.done(V.reciprocal(top, top))
            dve.wait(e)
            e = dve.done(V.tensor_tensor(prob, prob, spread(top), ALU.mult))
            dve.wait(e)
            e = dve.done(V.tensor_tensor(logits, prob, bias8[:, None, :].to_broadcast([P, B, 8]), ALU.add))
            dve.wait(e)
        for n in range(topk):
            e = self.first_max(logits, picks[n], top, ramp, equal)
            if n + 1 < topk:
                e = dve.done(V.tensor_scalar(tmp8, picks[n], BIG, None, ALU.mult))
                dve.wait(e)
                e = dve.done(V.tensor_tensor(logits, logits, tmp8, ALU.subtract))
                dve.wait(e)
            if shared:
                e = dve.done(V.tensor_tensor(tmp8, prob, picks[n], ALU.mult))
                dve.wait(e)
                e = dve.done(V.tensor_reduce(tw[n], tmp8, AX.X, ALU.add))
                dve.wait(e)
                e = dve.done(V.tensor_scalar(tw[n], tw[n], self.gates[:, gate:gate + 1], None, ALU.mult))
                dve.wait(e)
        if topk == 2:
            e = dve.done(V.tensor_tensor(both, picks[0], picks[1], ALU.add))
        else:
            both = picks[0]
        pb = self.banks[1]
        flat = both.rearrange("p b e -> p (b e)")
        pe.wait(e)
        nc.tensor.matmul(pb[:, 0:BE], self.before, flat, start=True, stop=True)
        e = pe.done(nc.tensor.matmul(pb[:, BE:2 * BE], self.ones, flat, start=True, stop=True))
        dve.wait(e)
        e = dve.done(V.tensor_copy(total, pb[:, BE:2 * BE].rearrange("p (b e) -> p e b", e=8)))
        dve.wait(e)
        line = lambda m: m.rearrange("p e b -> p (e b)")
        e = dve.done(V.tensor_tensor_scan(line(upto), line(reset), line(total), 0.0, ALU.mult, ALU.add))
        dve.wait(e)
        e = dve.done(V.tensor_tensor(more, upto[:, :, B - 1:B].to_broadcast([P, 8, B]), step, ALU.is_gt))
        dve.wait(e)
        e = dve.done(V.tensor_reduce(nblk, more, AX.X, ALU.add))
        e2 = dve.done(V.tensor_tensor(upto, upto, total, ALU.subtract))
        dve.wait(e)
        e = dve.done(V.tensor_tensor_scan(end, ones8, nblk, 0.0, ALU.mult, ALU.add))
        dve.wait(e)
        e = dve.done(V.tensor_tensor(base, end, nblk, ALU.subtract))
        dve.wait(e)
        e = dve.done(V.tensor_scalar(base, base, float(P), None, ALU.mult))
        e1 = dve.done(V.tensor_tensor(past, index, end[:, None, :].to_broadcast([P, blocks, 8]), ALU.is_ge))
        dve.wait(e1)
        e1 = dve.done(V.tensor_reduce(eid, past, AX.X, ALU.add))
        dve.wait(e1)
        e1 = dve.done(V.tensor_scalar(eid, eid, float(experts - 1), float(P), ALU.min, ALU.mult))
        dve.wait(e1)
        ids_ready = dve.done(V.tensor_copy(eid_i, eid))
        dve.wait(e, e2)
        e = dve.done(V.tensor_tensor(rank, pb[:, 0:BE].rearrange("p (b e) -> p b e", e=8),
                                     upto.rearrange("p e b -> p b e"), ALU.add))
        dve.wait(e)
        e = dve.done(V.tensor_tensor(rank, rank, base[:, None, :].to_broadcast([P, B, 8]), ALU.add))
        dve.wait(e)
        for n in range(topk):
            e = dve.done(V.tensor_tensor(tmp8, rank, picks[n], ALU.mult))
            dve.wait(e)
            e = dve.done(V.tensor_reduce(pos[n], tmp8, AX.X, ALU.add))
            dve.wait(e)
            pos_ready = dve.done(V.tensor_copy(pos_i[n], pos[n]))

        scattered = self.arrivals("scattered")
        pool.wait(pos_ready, zero_done, *self.xn_ready)
        for b in range(B):
            for n in range(topk):
                all_scattered = scattered.of(g.indirect_dma_start(
                    xs_dram, bass.IndirectOffsetOnAxis(pos_i[n][:, b:b + 1], 0), self.xn[:, b, :], None))

        gu_ring, y_ring, t_ring = Ring(self.banks[0:4]), Ring(self.banks[4:6]), Ring(self.banks[6:8])
        gu_ring.release(0, pos_ready)
        gu_ring.release(1, pos_ready)
        silu_ring, down_done, w_read, hid_read = Ring(silu), {}, {}, {}
        col_read, y_copied, y_stored, row_read = {}, {}, {}, {}
        steps = ([("shared", b) for b in range(B)] if shared else []) + [("routed", i) for i in range(blocks)]
        w_ready, rows_ready, cols_ready, h_ready = {}, {}, {}, {}

        def load_rows(i):
            rows_ready[i] = self.load(r_sems[i % nr], rows[i % nr], xs_dram[i * P:(i + 1) * P, :], all_scattered, row_read.get(i - nr))

        def load_weights(i):
            slot = i % nw
            sp.wait(ids_ready)
            row = nc.sync.value_load(eid_i[0:1, i:i + 1], min_val=0, max_val=(experts - 1) * P)
            w_ready[i] = self.load(w_sems[slot], weights[slot], d[f"L{layer}_experts"][bass.ds(row, P), :], w_read.get(i - nw))

        def turn_block(i):
            n, bank, freed = t_ring.take()
            pe.wait(rows_ready[i], *events_of(freed))
            for k in range(KD):
                mm = self.transpose(bank[:, k * P:(k + 1) * P], rows[i % nr][:, k * P:(k + 1) * P])
            row_read[i] = pe.done(mm)
            act.wait(row_read[i], col_read.get(i - 2))
            cols_ready[i] = act.done(nc.scalar.activation(
                cols[i % 2], bank[:, 0:KD * P].rearrange("p (k t) -> p k t", k=KD), ACT.Copy))
            t_ring.release(n, cols_ready[i])

        def up(s, kind, i):
            if kind == "shared":
                w, x_in = shared_w, self.xnT[:, :, i * P:(i + 1) * P]
                pe.wait(shared_ready)
            else:
                w, x_in = weights[i % nw], cols[i % 2]
                pe.wait(w_ready[i], cols_ready[i])
            for gr in groups:
                n, bank, freed = gu_ring.take()
                pe.wait(*events_of(freed))
                m = last_rows if gr[-1] == chunks - 1 else P
                for half in range(2):
                    for j, c in enumerate(gr):
                        at = (half * len(gr) + j) * P
                        for k in range(KD):
                            col = (k * 2 + half) * inter + c * P
                            mm = nc.tensor.matmul(bank[0:m, at:at + P], w[:, col:col + m], x_in[:, k, :],
                                                  start=k == 0, stop=k == KD - 1)
                e = pe.done(mm)
                size = len(gr) * P
                sn, sbuf, sfreed = silu_ring.take()
                act.wait(e, *events_of(sfreed))
                e = act.done(nc.scalar.activation(sbuf[0:m, 0:size], bank[0:m, 0:size], ACT.Silu))
                dve.wait(e, hid_read.get(s - 2))
                h_ready[s] = dve.done(V.tensor_tensor(
                    hid[s % 2][0:m, gr[0]:gr[0] + len(gr), :], sbuf[0:m, 0:size].rearrange("p (c t) -> p c t", t=P),
                    bank[0:m, size:2 * size].rearrange("p (c t) -> p c t", t=P), ALU.mult))
                gu_ring.release(n, h_ready[s])
                silu_ring.release(sn, h_ready[s])
            if kind == "routed":
                col_read[i] = (pe.semaphore, pe.count)

        def down(s, kind, i):
            w = shared_w if kind == "shared" else weights[i % nw]
            n, bank, freed = y_ring.take()
            pe.wait(h_ready[s], *events_of(freed))
            for c in range(chunks):
                m = last_rows if c == chunks - 1 else P
                col = KD * 2 * inter + c * D
                mm = nc.tensor.matmul(bank[:, 0:D], hid[s % 2][0:m, c, :], w[0:m, col:col + D],
                                      start=c == 0, stop=c == chunks - 1)
            e = hid_read[s] = pe.done(mm)
            if kind == "shared":
                y_ring.release(n, self.update(i, bank[:, 0:D], gate, e))
                return
            w_read[i] = e
            dve.wait(e, y_stored.get(i - 3))
            e = dve.done(V.tensor_copy(youts[i % 3], bank[:, 0:D]))
            y_ring.release(n, e)
            y_copied[i] = e

        def store_block(i):
            sp.wait(y_copied[i])
            y_stored[i] = y_sems[i % 3].of(nc.sync.dma_start(ys_dram[i * P:(i + 1) * P, :], youts[i % 3]))

        for i in range(nw):
            load_weights(i)
        for i in range(nr):
            load_rows(i)
        for s in range(len(steps) + 1):
            if s < len(steps):
                kind, i = steps[s]
                if steps[s] == ("routed", 0):
                    turn_block(0)
                up(s, kind, i)
                if kind == "routed" and i + 1 < blocks:
                    turn_block(i + 1)
            if s >= 1:
                kind, i = steps[s - 1]
                down(s - 1, kind, i)
                if kind == "routed":
                    if i + nr < blocks:
                        load_rows(i + nr)
                    if i + nw < blocks:
                        load_weights(i + nw)
                    store_block(i)

        pool.wait(*[y_stored[i] for i in range(blocks - 3, blocks)])
        order = [(b, n) for b in range(B) for n in range(topk)]
        gathered = {}
        for m, (b, n) in enumerate(order):
            gathered[b] = b_sems[b].of(g.indirect_dma_start(
                back[m], None, ys_dram, bass.IndirectOffsetOnAxis(pos_i[n][:, b:b + 1], 0)))
        pend = {}
        for b in range(B + 2):
            if b < B:
                for n in range(topk):
                    slot = back[b * topk + n]
                    if shared:
                        dve.wait(self.x_ready[b], gathered[b])
                        self.x_ready[b] = dve.done(V.scalar_tensor_tensor(
                            self.x[:, b, :], slot, tw[n][:, b:b + 1], self.x[:, b, :], ALU.mult, ALU.add))
                    else:
                        self.update(b, slot, gate, gathered[b])
                pend[b] = self.ln_stats(b)
            if b >= 2:
                self.ln_apply(b - 2, pend[b - 2])
                self.ln_transpose(b - 2, t_ring)

    def soft_moe(self):
        nc, pe, act, dve, pool, sp, d = self.nc, self.pe, self.act, self.dve, self.pool, self.sp, self.d
        V = nc.vector
        self.phase()
        free = self.region_free
        group, nd = 4, 5
        phi = self.tmp("phiT", [P, KD, SLOTS])
        phib = self.tmp("phi_b_parts", [3, SLOTS], BF16)
        lg = self.tmp("slot_logits", [P, SLOTS])
        disp = [self.tmp("dispatch", [P, SLOTS]) for _ in range(nd)]
        comb = [self.tmp("combine", [P, SLOTS]) for _ in range(2)]
        combT = self.tmp("combineT", [P, ST, P])
        acc = self.tmp("slot_sums", [P, ST, D])
        gmax, gsum = self.tmp("expert_max", [P, NEXP]), self.tmp("expert_sum", [P, NEXP])
        smax, ssum = self.tmp("slot_max", [P, PSLOT]), self.tmp("slot_sum", [P, PSLOT])
        ct_dram = nc.dram_tensor("combineT_rows", [B, P, ST * P], F32, kind="Internal").ap()
        loads = self.arrivals("phi")
        phi_ready = self.load(loads, phi, d["phiT"], *free)
        braw = lg[0:1, :]
        part = combT.rearrange("p s t -> p (s t)")[0:1, 0:SLOTS]
        pbf = [self.tmp("phi_part", [1, SLOTS], BF16) for _ in range(1)][0]
        b_ready = self.load(loads, braw, d["phi_b"])
        dve.wait(b_ready, *free)
        ps = self.arrivals("phi_parts")
        for n in range(3):
            e = dve.done(V.tensor_copy(pbf, braw))
            dve.wait(e)
            if n < 2:
                e2 = dve.done(V.tensor_copy(part, pbf))
                dve.wait(e2)
                e2 = dve.done(V.tensor_tensor(braw, braw, part, ALU.subtract))
            sp.wait(e)
            parts_ready = ps.of(nc.sync.dma_start(phib[n:n + 1, :], pbf))
            if n < 2:
                dve.wait(e2, parts_ready)
        lbank = self.banks[0:4]
        xt_ring, misc = Ring(self.banks[4:6]), Ring(self.banks[6:8])
        pe.wait(phi_ready, parts_ready, *free)
        act.wait(*free)
        pool.wait(*free)
        lg_free, lb_free, d_ready, d_read, c_ready, c_read, ct_stored = (), [None] * 4, {}, {}, {}, {}, None
        cts = self.arrivals("combineT_store")
        acc_ready = [None] * (ST // 2)
        by_expert = lambda m: m.rearrange("p (n s) -> p n s", s=PSLOT)
        by_slot = lambda m: m.rearrange("p (n s) -> p s n", s=PSLOT)

        def slot_logits(b):
            nonlocal lg_free
            pe.wait(self.xnT_ready[b])
            for j in range(4):
                pe.wait(lb_free[j])
                cs = slice(j * 512, (j + 1) * 512)
                for k in range(KD):
                    nc.tensor.matmul(lbank[j], self.xnT[:, k, b * P:(b + 1) * P], phi[:, k, cs], start=k == 0, stop=False)
                e = pe.done(nc.tensor.matmul(lbank[j], self.onesb[0:3, 0:P], phib[:, cs], start=False, stop=True))
                act.wait(e, *lg_free)
                e = lb_free[j] = act.done(nc.scalar.activation(lg[:, cs], lbank[j], ACT.Copy))
            lg_ready = e
            D_, C_ = disp[b % nd], comb[b % 2]
            dve.wait(lg_ready, d_read.get(b - nd))
            e1 = dve.done(V.tensor_reduce(gmax, by_expert(lg), AX.X, ALU.max))
            e2 = dve.done(V.tensor_reduce(smax, by_slot(lg), AX.X, ALU.max))
            pool.wait(e2, lg_ready, c_read.get(b - 2))
            e4 = pool.done(nc.gpsimd.tensor_tensor(by_expert(C_), by_expert(lg), smax[:, None, :].to_broadcast([P, NEXP, PSLOT]), ALU.subtract))
            dve.wait(e1)
            e3 = dve.done(V.tensor_tensor(by_expert(D_), by_expert(lg), gmax[:, :, None].to_broadcast([P, NEXP, PSLOT]), ALU.subtract))
            lg_free = (e3, e4)
            act.wait(e3)
            e3 = act.done(nc.scalar.activation(D_, D_, ACT.Exp))
            act.wait(e4)
            e4 = act.done(nc.scalar.activation(C_, C_, ACT.Exp))
            dve.wait(e3)
            e3 = dve.done(V.tensor_reduce(gsum, by_expert(D_), AX.X, ALU.add))
            dve.wait(e3)
            e3 = dve.done(V.reciprocal(gsum, gsum))
            dve.wait(e3)
            d_ready[b] = dve.done(V.tensor_tensor(by_expert(D_), by_expert(D_), gsum[:, :, None].to_broadcast([P, NEXP, PSLOT]), ALU.mult))
            dve.wait(e4, c_ready.get(b - 1))
            e4 = dve.done(V.tensor_reduce(ssum, by_slot(C_), AX.X, ALU.add))
            dve.wait(e4)
            e4 = dve.done(V.reciprocal(ssum, ssum))
            pool.wait(e4)
            c_ready[b] = pool.done(nc.gpsimd.tensor_tensor(by_expert(C_), by_expert(C_), ssum[:, None, :].to_broadcast([P, NEXP, PSLOT]), ALU.mult))

        def turn_combine(b):
            nonlocal ct_stored
            pe.wait(c_ready[b])
            for j in range(0, ST, 4):
                n, bank, freed = misc.take()
                pe.wait(*events_of(freed))
                for i in range(4):
                    mm = self.transpose(bank[:, i * P:(i + 1) * P], comb[b % 2][:, (j + i) * P:(j + i + 1) * P])
                e = pe.done(mm)
                act.wait(e, ct_stored)
                e2 = act.done(nc.scalar.activation(combT[:, j:j + 4, :], bank.rearrange("p (s t) -> p s t", t=P), ACT.Copy))
                misc.release(n, e2)
            c_read[b] = e
            sp.wait(e2)
            ct_stored = cts.of(nc.sync.dma_start(ct_dram[b], combT.rearrange("p s t -> p (s t)")))

        def slot_sums(gp):
            tiles = range(gp * group, (gp + 1) * group)
            for j in range(0, ST, 2):
                n, bank, freed = xt_ring.take()
                pe.wait(*[d_ready[b] for b in tiles], *events_of(freed))
                for i in range(2):
                    for b in tiles:
                        mm = nc.tensor.matmul(bank[:, i * D:(i + 1) * D], disp[b % nd][:, (j + i) * P:(j + i + 1) * P],
                                              self.xn[:, b, :], start=b == tiles[0], stop=b == tiles[-1])
                e = pe.done(mm)
                target, src = acc[:, j:j + 2, :], bank.rearrange("p (s d) -> p s d", d=D)
                dve.wait(e, acc_ready[j // 2])
                if gp == 0:
                    e2 = dve.done(V.tensor_copy(target, src))
                else:
                    e2 = dve.done(V.tensor_tensor(target, target, src, ALU.add))
                acc_ready[j // 2] = e2
                xt_ring.release(n, e2)
            for b in tiles:
                d_read[b] = e

        for b in range(B + 1):
            if b < B:
                slot_logits(b)
            if b >= 1:
                turn_combine(b - 1)
                if b % group == 0:
                    slot_sums(b // group - 1)

        self.phase()
        free = self.region_free
        acc_end = self.at
        xt = self.tmp("slots_normed", [P, ST, D])
        xtT = self.tmp("slots_normed_T", [P, KD, SLOTS])
        yt = self.tmp("slot_outputs", [P, ST, D])
        nwe = 2
        ew = [self.tmp("expert_w", [P, 4, KD, D]) for _ in range(nwe)]
        ctl = [self.tmp("combineT_load", [P, ST, P]) for _ in range(2)]
        sst, smv = self.tmp("slot_stats", [P, ST, 6]), self.tmp("slot_mean_var", [P, ST, 2])
        sve, srs, sneg = self.tmp("slot_var_eps", [P, ST]), self.tmp("slot_rstd", [P, ST]), self.tmp("slot_shift", [P, ST])
        ews = [self.arrivals("expert_w") for _ in range(nwe)]
        ebs, ctls = self.arrivals("expert_b"), [self.arrivals("combineT_load") for _ in range(2)]
        dve.wait(*free, *acc_ready)
        e = dve.done(V.tensor_scalar(acc, acc, -33000.0, 65000.0, ALU.max, ALU.min))
        dve.wait(e)
        for s in range(ST):
            e = dve.done(V.bn_stats(sst[:, s, :], acc[:, s, :]))
        dve.wait(e)
        for s in range(ST):
            e = dve.done(V.bn_aggr(smv[:, s, :], sst[:, s, :]))
        pool.wait(e, *free)
        e = pool.done(nc.gpsimd.tensor_scalar(sve[:, :, None], smv[:, :, 1:2], EPS, None, ALU.add))
        pool.wait(e)
        rs = pool.done(nc.gpsimd.tensor_tensor(srs, sve, self.half_power, ALU.pow))
        dve.wait(rs)
        e = None
        for s in range(ST):
            e = dve.done(V.tensor_scalar(acc[:, s, :], acc[:, s, :], smv[:, s, 0:1], srs[:, s:s + 1], ALU.subtract, ALU.mult))
            act.wait(e, *free)
            tanh_done = act.done(nc.scalar.activation(xt[:, s, :], acc[:, s, :], ACT.Tanh))
            n, bank, freed = misc.take()
            pe.wait(tanh_done, *events_of(freed))
            for k in range(KD):
                mm = self.transpose(bank[:, k * P:(k + 1) * P], xt[:, s, k * P:(k + 1) * P])
            act.wait(pe.done(mm))
            turned = act.done(nc.scalar.activation(xtT[:, :, s * P:(s + 1) * P], bank[:, 0:KD * P].rearrange("p (k t) -> p k t", k=KD), ACT.Copy))
            misc.release(n, turned)
        for j in range(4):
            yb_ready = self.load(ebs, yt[j * PSLOT:(j + 1) * PSLOT, :, :],
                                 d["expert_b"][j].rearrange("(a s) d -> a s d", a=1).to_broadcast([PSLOT, ST, D]), *free)
        ew_read, ew_ready = {}, {}
        for s in range(ST + 1):
            if s < ST:
                ew_ready[s] = self.load(ews[s % nwe], ew[s % nwe], d["expert_w"][s], ew_read.get(s - nwe), *free)
            if s == 0:
                continue
            s -= 1
            n, bank, freed = xt_ring.take()
            pe.wait(ew_ready[s], turned, *events_of(freed))
            for j in range(4):
                for k in range(KD):
                    mm = nc.tensor.matmul(bank[j * PSLOT:(j + 1) * PSLOT, 0:D], xtT[:, k, s * P + j * PSLOT:s * P + (j + 1) * PSLOT],
                                          ew[s % nwe][:, j, k, :], start=k == 0, stop=k == KD - 1)
            ew_read[s] = pe.done(mm)
            dve.wait(ew_read[s], yb_ready)
            yt_ready = dve.done(V.tensor_tensor(yt[:, s, :], yt[:, s, :], bank[:, 0:D], ALU.add))
            xt_ring.release(n, yt_ready)

        ct_read, pend = {}, {}
        pe.wait(yt_ready)
        for b in range(B + 2):
            if b < B:
                ct_ready = self.load(ctls[b % 2], ctl[b % 2].rearrange("p s t -> p (s t)"), ct_dram[b], ct_stored, ct_read.get(b - 2))
                n, bank, freed = xt_ring.take()
                pe.wait(ct_ready, *events_of(freed))
                for s in range(ST):
                    mm = nc.tensor.matmul(bank[:, 0:D], ctl[b % 2][:, s, :], yt[:, s, :], start=s == 0, stop=s == ST - 1)
                ct_read[b] = pe.done(mm)
                xt_ring.release(n, self.update(b, bank[:, 0:D], 6, ct_read[b]))
                pend[b] = self.ln_stats(b)
            if b >= 2:
                self.ln_apply(b - 2, pend[b - 2])
                self.ln_transpose(b - 2, misc)

    def peer(self):
        nc, pe, act, dve, pool, sp, d = self.nc, self.pe, self.act, self.dve, self.pool, self.sp, self.d
        V, G = nc.vector, nc.gpsimd
        self.phase()
        free = self.region_free
        QT = QH * QD // P
        NG = 2 * QH
        wq, down, up = self.tmp("wq", [P, KD, QH * QD]), self.tmp("downT", [P, KD, D]), self.tmp("up", [P, 2, D])
        bq, gamma, beta = self.tmp("bq", [P, QT]), self.tmp("gamma", [P, 1]), self.tmp("beta", [P, 1])
        keys, keysq, kn = self.tmp("keys", [P, 32]), self.tmp("keys_sq", [P, 32]), self.tmp("key_norm", [P, 1])
        kdiag, kT = self.tmp("keys_diag", [P, P]), self.tmp("keys_diag_T", [P, P])
        blocks32, pairm = self.tmp("block_of_32", [P, 4]), self.tmp("pair_mean", [P, P])
        q = self.tmp("queries_T", [P, QT, T])
        qst, qmv, ex2 = self.tmp("q_stats", [P, QT, 4, 6]), self.tmp("q_mv", [P, QT, 2]), self.tmp("q_ex2", [P, QT, 1])
        mom, var, sc, sh = self.tmp("moments", [P, 2]), self.tmp("q_var", [P, 1]), self.tmp("q_scale", [P, 1]), self.tmp("q_shift", [P, 1])
        gl = self.tmp("gelu", [P, B, D])
        reset = self.tmp("reset", [P, NG, NKEY])
        ws = self.arrivals("peer_w")
        self.load(ws, wq, d["L3f_Wq"], *free)
        self.load(ws, bq, d["L3f_bq"])
        for i in range(2):
            for name, m in (("gamma", gamma), ("beta", beta)):
                self.load(ws, m[i * QD:(i + 1) * QD, :], d["L3f_" + name])
            for j in range(2):
                at = (2 * i + j) * NKEY
                self.load(ws, keys[at:at + NKEY, :], d[f"key{j}"])
        self.load(ws, down, d["downT"])
        w_ready = self.load(ws, up, d["up"])
        pool.wait(*free)
        pool.done(G.memset(kdiag, 0.0))
        e = pool.done(G.memset(reset, 1.0))
        pool.wait(e)
        set_ready = pool.done(G.memset(reset[:, :, 0:1], 0.0))
        dve.wait(w_ready, set_ready, *free)
        e = dve.done(V.tensor_tensor(keysq, keys, keys, ALU.mult))
        dve.wait(e)
        e = dve.done(V.tensor_reduce(kn, keysq, AX.X, ALU.add))
        dve.wait(e)
        e = dve.done(V.tensor_scalar(kn, kn, 1e-24, None, ALU.max))
        pool.wait(e)
        e = pool.done(G.tensor_tensor(kn, kn, self.half_power[:, 0:1], ALU.pow))
        dve.wait(e)
        for i in range(4):
            r = slice(i * NKEY, (i + 1) * NKEY)
            kd_ready = dve.done(V.tensor_scalar(kdiag[r, r], keys[r, :], kn[r, :], None, ALU.mult))
        b32_ready = dve.done(V.tensor_reduce(blocks32, self.ident.rearrange("p (i c) -> p i c", c=32), AX.X, ALU.add))
        ids = self.ident.rearrange("p (i c) -> p i c", i=2)
        e = dve.done(V.tensor_tensor(pairm[:, 0:QD], ids[:, 0, :], ids[:, 1, :], ALU.add))
        dve.wait(e)
        e = dve.done(V.tensor_scalar(pairm[:, 0:QD], pairm[:, 0:QD], 1.0 / QH, None, ALU.mult))
        dve.wait(e)
        pm_ready = dve.done(V.tensor_copy(pairm[:, QD:P], pairm[:, 0:QD]))
        ring, misc = Ring(self.banks[0:4]), Ring(self.banks[4:6])
        pe.wait(kd_ready, *free)
        n, bank, _ = misc.take()
        e = pe.done(self.transpose(bank[:, 0:P], kdiag))
        act.wait(e, *free)
        kT_ready = act.done(nc.scalar.activation(kT, bank[:, 0:P], ACT.Copy))
        misc.release(n, kT_ready)
        for g in range(4):
            pe.wait(w_ready, *self.xnT_ready[4 * g:4 * g + 4])
            for m in range(QT):
                n, bank, freed = ring.take()
                pe.wait(*events_of(freed))
                for k in range(KD):
                    mm = nc.tensor.matmul(bank, wq[:, k, m * P:(m + 1) * P], self.xnT[:, k, g * 512:(g + 1) * 512],
                                          start=k == 0, stop=k == KD - 1)
                act.wait(pe.done(mm), w_ready)
                e = act.done(nc.scalar.activation(q[:, m, g * 512:(g + 1) * 512], bank, ACT.Identity, bias=bq[:, m:m + 1]))
                ring.release(n, e)
                dve.wait(e)
                st_ready = dve.done(V.bn_stats(qst[:, m, g, :], q[:, m, g * 512:(g + 1) * 512]))
        def gelu(b):
            n, bank, freed = ring.take()
            pe.wait(*events_of(freed))
            for k in range(KD):
                mm = nc.tensor.matmul(bank[:, 0:D], self.xnT[:, k, b * P:(b + 1) * P], down[:, k, :], start=k == 0, stop=k == KD - 1)
            act.wait(pe.done(mm))
            e = act.done(nc.scalar.activation(gl[:, b, :], bank[:, 0:D], ACT.Gelu))
            ring.release(n, e)
            return e

        for b in range(6):
            gelu(b)
        dve.wait(st_ready)
        for m in range(QT):
            e = dve.done(V.bn_aggr(qmv[:, m, :], qst[:, m, :, :].rearrange("p g s -> p (g s)")))
        dve.wait(e)
        e = dve.done(V.tensor_tensor(ex2, qmv[:, :, 0:1], qmv[:, :, 0:1], ALU.mult))
        dve.wait(e)
        e = dve.done(V.tensor_tensor(qmv[:, :, 1:2], qmv[:, :, 1:2], ex2, ALU.add))
        n, bank, freed = misc.take()
        pe.wait(e, pm_ready, *events_of(freed))
        for m in range(QT):
            mm = nc.tensor.matmul(bank[:, 0:2], pairm, qmv[:, m, :], start=m == 0, stop=m == QT - 1)
        dve.wait(pe.done(mm))
        for b in range(6, B):
            gelu_ready = gelu(b)
        e = dve.done(V.tensor_copy(mom, bank[:, 0:2]))
        misc.release(n, e)
        dve.wait(e)
        e = dve.done(V.tensor_tensor(var, mom[:, 0:1], mom[:, 0:1], ALU.mult))
        dve.wait(e)
        e = dve.done(V.tensor_tensor(var, mom[:, 1:2], var, ALU.subtract))
        dve.wait(e)
        e = dve.done(V.tensor_scalar(var, var, EPS, None, ALU.add))
        pool.wait(e)
        e = pool.done(G.tensor_tensor(var, var, self.half_power[:, 0:1], ALU.pow))
        dve.wait(e)
        e = dve.done(V.tensor_tensor(sc, var, gamma, ALU.mult))
        dve.wait(e)
        e = dve.done(V.tensor_tensor(sh, mom[:, 0:1], sc, ALU.mult))
        dve.wait(e)
        sh_ready = dve.done(V.tensor_tensor(sh, beta, sh, ALU.subtract))

        s_buf = [self.tmp("scores", [P, NG, NKEY]) for _ in range(2)]
        qn = [self.tmp("queries_normed", [P, QT, P]) for _ in range(2)]
        sq = [self.tmp("q_squares", [P, QT, P]) for _ in range(2)]
        eq, gt = self.tmp("equals_kth", [P, NG, NKEY]), self.tmp("greater", [P, NG, NKEY])
        cnt = self.tmp("equal_count", [P, NG, NKEY])
        inv, v8 = [self.tmp("inv_norm", [P, NG]) for _ in range(2)], self.tmp("top8", [P, NG, 8])
        g4, need, zsum = self.tmp("greater4", [P, NG, 4]), self.tmp("need", [P, NG]), self.tmp("exp_sum", [P, NG])
        prod = [self.tmp("expert_weight_parts", [P, D, QH]) for _ in range(2)]
        wt, restw = self.tmp("expert_weight", [P, D]), [self.tmp("rest_weight", [P, 1]) for _ in range(2)]
        wg, wgT = self.tmp("weighted", [P, D]), self.tmp("weighted_T", [P, 2, P])
        spread = lambda m: m[:, :, None].to_broadcast([P, NG, NKEY])
        flat = lambda m: m.rearrange("p g k -> p (g k)")
        s_banks, n_bank = Ring(self.banks[0:2]), Ring(self.banks[2:4])
        rows_i = D // NKEY
        sq_read, inv_ready, banks, weights_ready, prod_ready, rest_ready, prod_read, used = {}, {}, {}, {}, {}, {}, {}, {}
        turned, wgT_read, wg_read = {}, {}, {}

        def tile_scores(b):
            ts, c = slice(b * P, (b + 1) * P), b % 2
            act.wait(sh_ready, sq_read.get(b - 2))
            qn_ready = act.done(nc.scalar.activation(qn[c], q[:, :, ts], ACT.Identity, scale=sc, bias=sh))
            act.wait(qn_ready)
            sq_ready = act.done(nc.scalar.activation(sq[c], qn[c], ACT.Square))
            n1, sbank, f1 = s_banks.take()
            n2, nbank, f2 = n_bank.take()
            pe.wait(qn_ready, kT_ready, *events_of(f1))
            for m in range(QT):
                mm = nc.tensor.matmul(sbank[:, m * P:(m + 1) * P], qn[c][:, m, :], kT, start=True, stop=True)
            pe.wait(sq_ready, b32_ready, *events_of(f2))
            for m in range(QT):
                mm = nc.tensor.matmul(nbank[:, m * 4:(m + 1) * 4], sq[c][:, m, :], blocks32, start=True, stop=True)
            sq_read[b] = pe.done(mm)
            banks[b] = (n1, sbank, n2, nbank)

        def tile_norms(b):
            _, _, n2, nbank = banks[b]
            dve.wait(sq_read[b])
            e = dve.done(V.tensor_scalar(inv[b % 2], nbank[:, 0:NG], 1e-24, None, ALU.max))
            n_bank.release(n2, e)
            pool.wait(e)
            inv_ready[b] = pool.done(G.tensor_tensor(inv[b % 2], inv[b % 2], self.half_power[:, 0:1].to_broadcast([P, NG]), ALU.pow))

        def tile_choice(b):
            c = b % 2
            n1, sbank, _, _ = banks[b]
            s = s_buf[c]
            dve.wait(inv_ready[b], sq_read[b], used.get(b - 2))
            e = dve.done(V.tensor_tensor(s, sbank.rearrange("p (g k) -> p g k", k=NKEY), spread(inv[c]), ALU.mult))
            s_banks.release(n1, e)
            dve.wait(e)
            for g in range(NG):
                e = dve.done(V.max(v8[:, g, :], s[:, g, :]))
            dve.wait(e)
            kth = v8[:, :, TOPK - 1:TOPK]
            kth_all = kth.to_broadcast([P, NG, NKEY])
            e1 = dve.done(V.tensor_tensor(eq, s, kth_all, ALU.is_equal))
            e3 = dve.done(V.tensor_tensor(g4, v8[:, :, 0:TOPK], kth.to_broadcast([P, NG, TOPK]), ALU.is_gt))
            e2 = dve.done(V.tensor_tensor(gt, s, kth_all, ALU.is_gt))
            dve.wait(e3)
            e3 = dve.done(V.tensor_reduce(need, g4, AX.X, ALU.add))
            e4 = dve.done(V.tensor_tensor(s, s, v8[:, :, 0:1].to_broadcast([P, NG, NKEY]), ALU.subtract))
            act.wait(e4)
            ex = act.done(nc.scalar.activation(s, s, ACT.Exp))
            dve.wait(e3)
            e3 = dve.done(V.tensor_scalar(need, need, -1.0, float(TOPK), ALU.mult, ALU.add))
            dve.wait(e1)
            e = dve.done(V.tensor_tensor_scan(flat(cnt), flat(reset), flat(eq), 0.0, ALU.mult, ALU.add))
            dve.wait(e, e3)
            e = dve.done(V.tensor_tensor(cnt, cnt, spread(need), ALU.is_le))
            dve.wait(e)
            e = dve.done(V.tensor_tensor(eq, eq, cnt, ALU.mult))
            dve.wait(e, e2)
            e = dve.done(V.tensor_tensor(gt, gt, eq, ALU.add))
            dve.wait(e, ex)
            e = dve.done(V.tensor_tensor(s, s, gt, ALU.mult))
            dve.wait(e)
            e = dve.done(V.tensor_reduce(zsum, s, AX.X, ALU.add))
            dve.wait(e)
            e = dve.done(V.reciprocal(zsum, zsum))
            dve.wait(e)
            weights_ready[b] = dve.done(V.tensor_tensor(s, s, spread(zsum), ALU.mult))

        def tile_products(b):
            halves = s_buf[b % 2].rearrange("p (h c) k -> p c k h", c=2)
            first = halves[:, 0, 0:rows_i, :][:, :, None, :].to_broadcast([P, rows_i, NKEY, QH])
            second = halves[:, 1, :, :][:, None, :, :].to_broadcast([P, rows_i, NKEY, QH])
            pool.wait(weights_ready[b], prod_read.get(b - 2))
            prod_ready[b] = used[b] = pool.done(G.tensor_tensor(
                prod[b % 2].rearrange("p (i j) h -> p i j h", i=rows_i), first, second, ALU.mult))
            dve.wait(weights_ready[b])
            rest_ready[b] = dve.done(V.tensor_reduce(restw[b % 2], halves[:, 0, rows_i:, :], AX.XY, ALU.add))

        def tile_experts(b):
            dve.wait(prod_ready[b])
            e = prod_read[b] = dve.done(V.tensor_reduce(wt, prod[b % 2], AX.X, ALU.add))
            dve.wait(e, rest_ready[b])
            e = dve.done(V.tensor_tensor(wt[:, D - 1:D], wt[:, D - 1:D], restw[b % 2], ALU.add))
            dve.wait(e, gelu_ready, wg_read.get(b - 1))
            e = dve.done(V.tensor_tensor(wg, wt, gl[:, b, :], ALU.mult))
            n, bank, freed = misc.take()
            pe.wait(e, *events_of(freed))
            for k in range(2):
                mm = self.transpose(bank[:, k * P:(k + 1) * P], wg[:, k * P:(k + 1) * P])
            wg_read[b] = pe.done(mm)
            act.wait(wg_read[b], wgT_read.get(b - 1))
            e = act.done(nc.scalar.activation(wgT, bank[:, 0:2 * P].rearrange("p (k t) -> p k t", k=2), ACT.Copy))
            misc.release(n, e)
            turned[b] = e

        def tile_out(b):
            n, bank, freed = misc.take()
            pe.wait(turned[b], *events_of(freed))
            for k in range(2):
                mm = nc.tensor.matmul(bank[:, 0:D], wgT[:, k, :], up[:, k, :], start=k == 0, stop=k == 1)
            wgT_read[b] = pe.done(mm)
            misc.release(n, self.update(b, bank[:, 0:D], 7, wgT_read[b]))

        s_banks.release(0, gelu_ready)
        s_banks.release(1, gelu_ready)
        n_bank.release(0, gelu_ready)
        n_bank.release(1, gelu_ready)
        tile_scores(0)
        tile_norms(0)
        for t in range(B + 2):
            if t + 1 < B:
                tile_scores(t + 1)
            if t < B:
                tile_choice(t)
            if t + 1 < B:
                tile_norms(t + 1)
            if t < B:
                tile_products(t)
            if t >= 2:
                tile_out(t - 2)
                self.store_out(t - 2)
            if 1 <= t <= B:
                tile_experts(t - 1)

    def update(self, b, y, gate, *after):
        self.dve.wait(self.x_ready[b], *after)
        self.x_ready[b] = self.dve.done(self.nc.vector.scalar_tensor_tensor(
            self.x[:, b, :], y, self.gates[:, gate:gate + 1], self.x[:, b, :], ALU.mult, ALU.add))
        return self.x_ready[b]

    def store_out(self, b):
        self.sp.wait(self.x_ready[b])
        self.stored = self.stores.of(self.nc.sync.dma_start(self.out[b], self.x[:, b, :]))

    def finish(self):
        if self.stored is None:
            for b in range(B):
                self.store_out(b)
        self.sp.wait(self.stored)


def program(nc, d, out, stop=8, start=0):
    core = Core(nc, d, out)
    core.constants()
    core.first_layernorm()
    layers = [
        lambda: core.attention(0, 16, 4, 0.25, True, None),
        lambda: core.moe(0, E0, I0, 1),
        lambda: core.attention(1, 16, 4, 0.25, True, "pairs"),
        lambda: core.moe(1, E1, I1, 2),
        lambda: core.attention(2, 16, 4, 0.25, True, None),
        lambda: core.soft_moe(),
        lambda: core.attention(3, 64, 2, 0.125, False, "keys"),
        lambda: core.peer(),
    ]
    for layer in layers[start:stop]:
        layer()
    core.finish()


def laid_out(x):
    a = {k: np.asarray(v) for k, v in x.items()}
    rows = lambda w: np.ascontiguousarray(w.reshape(-1, P, w.shape[-1]).transpose(1, 0, 2))
    column = lambda v: np.ascontiguousarray(v.reshape(-1, P).T)
    d = {"x": a["x"], "g_xattn": a["g_xattn"][None], "g_ffn": a["g_ffn"][None]}
    d["ctxT"] = rows(np.ascontiguousarray(a["ctx_1024"].reshape(T, D).T))
    d["mask_keys"] = a["mask_BxS2_bk0"].reshape(1, T)
    d["rel"] = a["fside_Bx1xSxS2_0"][:, 0]
    d["relT"] = np.ascontiguousarray(d["rel"].transpose(0, 2, 1))
    keep = a["mask_BxSxS2_bk0"]
    d["keep"] = keep
    d["keepT"] = np.ascontiguousarray(keep.transpose(0, 2, 1))
    for n, out_name in ((0, "o"), (1, "out"), (2, "o")):
        for name in ("q", "k", "v", out_name):
            w = a[f"L{n}_xattn_W{name}"]
            short = name[0]
            w = w if n == 0 else w.T
            b = a[f"L{n}_xattn_b{name}"]
            if short in "qk":
                w = w.reshape(D, HEADS, -1).transpose(0, 2, 1).reshape(D, D)
                b = np.ascontiguousarray(b.reshape(HEADS, -1).T).reshape(D)
            d[f"L{n}_W{short}"] = rows(np.ascontiguousarray(w))
            d[f"L{n}_b{short}"] = column(b) if short in "qk" else b[None]
    for name in "QKVO":
        d[f"L3_W{name.lower()}"] = rows(a[f"L3_xattn_W_{name}"])

    def experts(gate, up, down):
        n, inter, _ = gate.shape
        both = np.stack([gate, up], 1).reshape(n, 2, inter, KD, P).transpose(0, 4, 3, 1, 2).reshape(n, P, -1)
        chunks = -(-inter // P)
        low = np.zeros((n, chunks * P, D), down.dtype)
        low[:, :inter] = down.transpose(0, 2, 1)
        low = low.reshape(n, chunks, P, D).transpose(0, 2, 1, 3).reshape(n, P, -1)
        return np.concatenate([both, low], 2).reshape(n * P, -1)

    d["L0_experts"] = experts(a["L0_ffn_gate_w"], a["L0_ffn_up_w"], a["L0_ffn_down_w"])
    d["L1_experts"] = experts(a["L1_ffn_w1"], a["L1_ffn_w3"], a["L1_ffn_w2"])
    d["L1_shared"] = experts(a["L1_ffn_sw1"][None], a["L1_ffn_sw3"][None], a["L1_ffn_sw2"][None])
    d["L0_router"] = rows(np.ascontiguousarray(a["L0_ffn_router_w"].T))
    d["L1_router"] = rows(np.ascontiguousarray(a["L1_ffn_gate_w"].T))
    d["L1_gate_bias"] = a["L1_ffn_gate_bias"][None]
    d["phiT"] = rows(np.ascontiguousarray(a["L2_ffn_phi_w"].T))
    d["phi_b"] = a["L2_ffn_phi_b"][None]
    d["expert_w"] = np.ascontiguousarray(a["L2_ffn_expert_w"].reshape(ST, 4, KD, P, D).transpose(0, 3, 1, 2, 4))
    d["expert_b"] = np.ascontiguousarray(a["L2_ffn_expert_b"].reshape(ST, 4, D).transpose(1, 0, 2))
    d["L3f_Wq"] = rows(a["L3_ffn_Wq"])
    d["L3f_bq"] = column(a["L3_ffn_bq"])
    d["L3f_gamma"], d["L3f_beta"] = a["L3_ffn_bn_gamma"][:, None], a["L3_ffn_bn_beta"][:, None]
    d["key0"], d["key1"] = a["L3_ffn_sub_key0"], a["L3_ffn_sub_key1"]
    d["downT"] = rows(np.ascontiguousarray(a["L3_ffn_expert_down"].T))
    d["up"] = rows(a["L3_ffn_expert_up"])
    return d


def kernel(**inputs):
    import concourse.bacc as _bacc
    from concourse.bass_utils import run_bass_kernel_spmd as _run

    nc = _bacc.Bacc("TRN2", target_bir_lowering=False, num_devices=1)
    arrays = laid_out(inputs)
    d = {k: nc.dram_tensor(f"in_{k}", list(v.shape), mybir.dt.from_np(v.dtype), kind="ExternalInput").ap()
         for k, v in arrays.items()}
    out = nc.dram_tensor("out", [B, S, D], F32, kind="ExternalOutput").ap()
    program(nc, d, out)
    r = _run(nc, [{f"in_{k}": v for k, v in arrays.items()}], core_ids=[0])
    return r.results[0]["out"]
```

```python
import numpy as np
import concourse.bass as bass
from concourse import mybir

F32, BF16, I32, U8 = mybir.dt.float32, mybir.dt.bfloat16, mybir.dt.int32, mybir.dt.uint8
ALU, ACT, AX = mybir.AluOpType, mybir.ActivationFunctionType, mybir.AxisListType

P = 128
B, S, D = 16, 128, 256
T = B * S
KD = D // P
HEADS = 16
EPS = 1e-5
SBUF_END = 229344
BIG = 2.0 ** 100
E0, I0 = 8, 704
E1, I1 = 8, 512
SLOTS = 2048
NEXP, PSLOT = 64, 32
ST = SLOTS // P
QPARTS, KPARTS = (0, 0, 1, 1, 0, 2, 1, 2), (0, 1, 0, 1, 2, 0, 2, 1)
TERMS = len(QPARTS)
QH, QD, NKEY, TOPK = 8, 64, 32, 4


class Lane:

    def __init__(self, engine, semaphore):
        self.engine, self.semaphore = engine, semaphore
        self.count, self.waited = 0, {}

    def wait(self, *events):
        for event in events:
            if event is None:
                continue
            semaphore, value = event
            if self.waited.get(semaphore.num, 0) < value:
                self.engine.wait_ge(semaphore, value)
                self.waited[semaphore.num] = value

    def done(self, instruction):
        self.count += 1
        instruction.then_inc(self.semaphore, 1)
        return (self.semaphore, self.count)

    @property
    def last(self):
        return (self.semaphore, self.count) if self.count else None


class Arrivals:

    def __init__(self, semaphore):
        self.semaphore, self.count = semaphore, 0

    def of(self, dma):
        self.count += 16
        dma.then_inc(self.semaphore, 16)
        return (self.semaphore, self.count)


class Ring:

    def __init__(self, buffers):
        self.buffers, self.freed, self.at = buffers, [None] * len(buffers), -1

    def take(self):
        self.at = (self.at + 1) % len(self.buffers)
        return self.at, self.buffers[self.at], self.freed[self.at]

    def release(self, n, *events):
        self.freed[n] = events[0] if len(events) == 1 else events


def events_of(freed):
    if freed is None:
        return ()
    return freed if isinstance(freed[0], tuple) else (freed,)


class Core:
    def __init__(self, nc, d, out):
        self.nc, self.d, self.out = nc, d, out
        self.pe = Lane(nc.tensor, nc.alloc_semaphore("pe_done"))
        self.act = Lane(nc.scalar, nc.alloc_semaphore("act_done"))
        self.dve = Lane(nc.vector, nc.alloc_semaphore("dve_done"))
        self.pool = Lane(nc.gpsimd, nc.alloc_semaphore("pool_done"))
        self.sp = Lane(nc.sync, nc.alloc_semaphore("sp_done"))
        self.floor = nc.sbuf_base // 32 * 32 + 32
        self.names = 0
        self.region_free = ()
        self.limit = SBUF_END
        self.tail, self.tail_ring, self.tail_mark = [], None, ()
        self.ahead = {}
        self.stores, self.stored = Arrivals(nc.alloc_semaphore("out_store")), None
        self.x_ready = [None] * B
        self.xn_ready = [None] * B
        self.xnT_ready = [None] * B
        self.x = self.sb("x_residual", [P, B, D])
        self.xn = self.sb("x_normed", [P, B, D])
        self.xnT = self.sb("x_normed_T", [P, KD, T])
        self.ctxT = self.sb("context_T", [P, KD, T])
        self.banks = [nc.alloc_psum_tensor(f"bank{i}", [P, 512], F32).ap() for i in range(8)]

    def place(self, name, shape, dtype, offset):
        size = {F32: 4, BF16: 2, I32: 4, U8: 1}[dtype] * int(np.prod(shape[1:]))
        self.names += 1
        t = self.nc.alloc_sbuf_tensor_at(f"{name}_{self.names}", shape, dtype, offset=offset)
        return t.ap(), offset + (size + 31) // 32 * 32

    def sb(self, name, shape, dtype=F32):
        ap, self.floor = self.place(name, shape, dtype, self.floor)
        return ap

    def engines_last(self):
        return tuple(x.last for x in (self.pe, self.act, self.dve, self.pool) if x.last)

    def phase(self):
        self.region_free = self.tail_mark if self.tail else self.engines_last()
        self.at = self.floor

    def tail_step(self, count=1):
        for _ in range(count):
            if self.tail:
                self.tail.pop(0)()

    def high(self, name, shape, dtype=F32):
        size = {F32: 4, BF16: 2, I32: 4, U8: 1}[dtype] * int(np.prod(shape[1:]))
        self.limit -= (size + 31) // 32 * 32
        return self.place(name, shape, dtype, self.limit)[0]

    def tmp(self, name, shape, dtype=F32):
        ap, self.at = self.place(name, shape, dtype, self.at)
        assert self.at <= self.limit, (name, self.at, self.limit)
        return ap

    def arrivals(self, name):
        self.names += 1
        return Arrivals(self.nc.alloc_semaphore(f"{name}_{self.names}"))

    def load(self, arrivals, dst, src, *after):
        self.sp.wait(*after)
        return arrivals.of(self.nc.sync.dma_start(dst, src))

    def transpose(self, out, in_):
        return self.nc.tensor.transpose(out, in_, self.ident)

    def constants(self):
        nc, pool, dve, d = self.nc, self.pool, self.dve, self.d
        self.ident = self.sb("identity", [P, P])
        self.ones = self.sb("ones", [P, P])
        self.before = self.sb("strictly_before", [P, P])
        self.neg_ident = self.sb("minus_identity", [P, P], BF16)
        self.identb = self.sb("identity_bf16", [P, P], BF16)
        self.onesb = self.sb("ones_bf16", [P, P], BF16)
        self.par = self.sb("lower_upper_half", [P, 2])
        self.gates = self.sb("gates", [P, 8])
        self.half_power = self.sb("minus_half", [P, B])
        self.stats = self.sb("ln_stats", [P, B, 6])
        self.meanvar = self.sb("ln_mean_var", [P, B, 2])
        self.vareps = self.sb("ln_var_eps", [P, B])
        self.rstd = self.sb("ln_rstd", [P, B])
        g = nc.gpsimd
        pool.done(g.memset(self.ident, 0.0))
        pool.done(g.memset(self.identb, 0.0))
        pool.done(g.memset(self.neg_ident, 0.0))
        pool.done(g.memset(self.ones, 1.0))
        pool.done(g.memset(self.onesb, 1.0))
        zeroed = pool.done(g.memset(self.half_power, -0.5))
        pool.wait(zeroed)
        for m, value in ((self.ident, 1.0), (self.identb, 1.0), (self.neg_ident, -1.0)):
            pool.done(g.affine_select(out=m, in_=m, compare_op=ALU.not_equal, fill=value, base=0,
                                      pattern=[[-1, P]], channel_multiplier=1))
        self.const_ready = pool.done(g.affine_select(
            out=self.before, in_=self.ones, compare_op=ALU.is_gt, fill=0.0, base=0,
            pattern=[[1, P]], channel_multiplier=-1))
        dve.wait(self.const_ready)
        cols = self.ident.rearrange("p (c r) -> p c r", c=2)
        for c in range(2):
            self.par_ready = dve.done(nc.vector.tensor_reduce(
                self.par[:, c:c + 1], cols[:, c, :], AX.X, ALU.add))
        small = self.arrivals("small_loads")
        self.load(small, self.gates[:, 0:4], d["g_xattn"].to_broadcast([P, 4]))
        loaded = self.load(small, self.gates[:, 4:8], d["g_ffn"].to_broadcast([P, 4]))
        self.act.wait(loaded)
        self.gates_ready = self.act.done(nc.scalar.activation(self.gates, self.gates, ACT.Tanh))
        self.ctx_ready = [None] * (B // 4)
        for b in range(0, 4, 2):
            self.load_x(b)
        dve.wait(self.gates_ready)

    def load_x(self, b):
        self.x_ready[b] = self.x_ready[b + 1] = self.load(
            self.arrivals("x_load"), self.x[:, b:b + 2, :], self.d["x"][b:b + 2].rearrange("b s d -> s b d"))

    def load_context(self, g):
        cols = slice(g * 4 * P, (g + 1) * 4 * P)
        self.ctx_ready[g] = self.load(self.arrivals("context_load"), self.ctxT[:, :, cols], self.d["ctxT"][:, :, cols])

    def other_loads(self):
        for g in range(4):
            self.load_context(g)
            if g < 3:
                self.load_x(4 * g + 4)
                self.load_x(4 * g + 6)

    def slot_bias_parts(self):
        nc, dve, sp = self.nc, self.dve, self.sp
        self.limit = SBUF_END
        y, part = self.high("slot_bias", [ST, P]), self.high("slot_bias_parts", [ST, 3, P], BF16)
        self.phi_b_parts = nc.dram_tensor("phi_b_parts", [3, SLOTS], BF16, kind="Internal").ap()
        arrived = self.arrivals("slot_bias")
        dve.wait(self.load(arrived, y, self.d["phi_b"].rearrange("a (s p) -> (a s) p", p=P)))
        for n in range(3):
            e = dve.done(nc.vector.tensor_copy(part[:, n, :], y))
            dve.wait(e)
            if n < 2:
                e = dve.done(nc.vector.tensor_tensor(y, y, part[:, n, :], ALU.subtract))
                dve.wait(e)
        sp.wait(e)
        stored = self.arrivals("slot_bias_parts")
        self.phi_b_stored = stored.of(nc.sync.dma_start(self.phi_b_parts.rearrange("n (s p) -> s n p", p=P), part))

    def ln_stats(self, b):
        nc, dve, pool = self.nc, self.dve, self.pool
        dve.wait(self.x_ready[b])
        e = dve.done(nc.vector.bn_stats(self.stats[:, b, :], self.x[:, b, :]))
        dve.wait(e)
        aggregated = dve.done(nc.vector.bn_aggr(self.meanvar[:, b, :], self.stats[:, b, :]))
        pool.wait(aggregated)
        e = pool.done(nc.gpsimd.tensor_scalar(self.vareps[:, b:b + 1], self.meanvar[:, b, 1:2], EPS, None, ALU.add))
        pool.wait(e)
        self.rstd_ready = pool.done(nc.gpsimd.tensor_tensor(
            self.rstd[:, b:b + 1], self.vareps[:, b:b + 1], self.half_power[:, 0:1], ALU.pow))
        return self.rstd_ready

    def ln_apply(self, b, rstd_ready, *readers):
        dve = self.dve
        dve.wait(rstd_ready, *readers)
        self.xn_ready[b] = dve.done(self.nc.vector.tensor_scalar(
            self.xn[:, b, :], self.x[:, b, :], self.meanvar[:, b, 0:1], self.rstd[:, b:b + 1],
            ALU.subtract, ALU.mult))

    def ln_transpose(self, b, ring):
        pe, act = self.pe, self.act
        n, bank, freed = ring.take()
        pe.wait(self.xn_ready[b], *events_of(freed))
        for k in range(KD):
            turned = self.transpose(bank[:, k * P:(k + 1) * P], self.xn[:, b, k * P:(k + 1) * P])
        act.wait(pe.done(turned))
        self.xnT_ready[b] = act.done(self.nc.scalar.activation(
            self.xnT[:, :, b * P:(b + 1) * P], bank[:, 0:KD * P].rearrange("p (k t) -> p k t", k=KD), ACT.Copy))
        ring.release(n, self.xnT_ready[b])

    def first_layernorm(self):
        ring = Ring(self.banks[6:8])
        self.pe.wait(self.const_ready)
        self.leave_layernorms(lambda b: None, ring)

    def leave_layernorms(self, finish_tile, ring):
        pend = {}

        def step(b):
            if b < B:
                finish_tile(b)
                pend[b] = self.ln_stats(b)
            if b >= 2:
                self.ln_apply(b - 2, pend[b - 2])
                self.ln_transpose(b - 2, ring)

        self.tail_mark = self.engines_last()
        self.tail, self.tail_ring = [lambda b=b: step(b) for b in range(B + 2)], ring

    def attention(self, layer, dk, group, scale, bias, mask, load_ahead):
        nc, pe, act, dve, pool, sp, d = self.nc, self.pe, self.act, self.dve, self.pool, self.sp, self.d
        small = dk == 16
        width = HEADS * dk
        tiles = width // P
        dv1 = dk + 1
        tok = group * P
        pre = f"L{layer}_"
        self.phase()
        wq = self.tmp("wq", [P, KD, width])
        wk = self.tmp("wk", [P, KD, width])
        wv = self.tmp("wv", [P, KD, width])
        wo = self.tmp("wo", [P, tiles, D])
        if small:
            raw = [self.tmp("projected", [P, tok]) for _ in range(2)]
            parts = [self.tmp("parts", [P, 3, tiles, tok], BF16) for _ in range(2)]
            stack = {k: [self.tmp(f"{k}_stack", [TERMS * dk, HEADS, tok], BF16) for _ in range(2)] for k in "qk"}
            parts_dram = [[nc.dram_tensor(f"parts_{layer}_{k}{i}", [3, width, tok], BF16, kind="Internal").ap()
                           for i in range(2)] for k in "qk"]
            parts_sem = [[self.arrivals("parts_store") for _ in range(2)] for _ in "qk"]
            stack_sem = [[self.arrivals("stack_load") for _ in range(2)] for _ in "qk"]
            raw_ring, parts_ring = Ring(raw), Ring(parts)
        else:
            qT = [[self.tmp("qT", [P, tiles, tok]) for _ in range(2)] for _ in range(2)]
            kT = [self.tmp("kT", [P, tiles, tok]) for _ in range(2)]
            qb = [self.tmp("q_bf16", [P, tiles, tok], BF16) for _ in range(2)]
            kb = [self.tmp("k_bf16", [P, tiles, tok], BF16) for _ in range(2)]
        v1 = [self.tmp("v_and_ones", [P, group, HEADS, dv1]) for _ in range(2)]
        probs = [self.tmp("probsT", [P, 4, P]) for _ in range(4)]
        maxes = [self.tmp("row_max", [P, 2, 4], BF16) for _ in range(2)]
        recips = [self.tmp("recips", [P, HEADS]) for _ in range(2)]
        o_row = [self.tmp("attn_out", [P, HEADS, dk]) for _ in range(2)]
        o_col = [self.tmp("attn_outT", [P, tiles, P]) for _ in range(2)]
        weights = self.arrivals("attn_weights")
        for name, m in (("Wk", wk), ("Wv", wv), ("Wq", wq)):
            self.load(weights, m, d[pre + name], *self.region_free)
        w_ready = self.load(weights, wo, d[pre + "Wo"])
        if bias:
            bq = self.tmp("bq", [P, tiles])
            bk = self.tmp("bk", [P, tiles])
            bv = self.tmp("bv", [P, width])
            gbo = self.tmp("gated_bo", [P, D])
            self.load(weights, bq, d[pre + "bq"])
            self.load(weights, bk, d[pre + "bk"])
            self.load(weights, bv, d[pre + "bv"].to_broadcast([P, width]))
            w_ready = self.load(weights, gbo, d[pre + "bo"].to_broadcast([P, D]))
        if layer == 0:
            self.other_loads()
        pool.wait(*self.region_free)
        for v in v1:
            ones_ready = pool.done(nc.gpsimd.memset(v[:, :, :, dk:dv1], 1.0))
        act.wait(*self.region_free)
        dve.wait(*self.region_free)
        if mask == "keys":
            kmask = o_col[1].rearrange("p t q -> p (t q)").bitcast(U8)[0:1, 0:T]
            kneg = self.tmp("key_neg", [1, T], BF16)
            kload = self.arrivals("key_mask")
            dve.wait(self.load(kload, kmask, d["mask_keys"]))
            kneg_ready = dve.done(nc.vector.tensor_scalar(kneg, kmask, -BIG, None, ALU.mult))
        if mask == "pairs":
            rt = [[self.tmp("rel", [P, P]) for _ in range(2)] for _ in range(2)]
            mk = [[self.tmp("keep", [P, P], U8) for _ in range(2)] for _ in range(2)]
            neg, kept = self.tmp("neg", [P, P]), self.tmp("kept", [P, P])
            r_q = [self.tmp("bias_qk", [P, P], BF16) for _ in range(2)]
            r_k = [self.tmp("bias_kq", [P, P]) for _ in range(2)]
            any_kept = self.tmp("any_kept", [P, B])
            rload = [self.arrivals("rel_load") for _ in range(2)]
            r_ready, r_read, any_ready, pair_loaded = [None] * B, [None] * B, [None] * B, [None] * B

        s_bank, t_bank = self.banks[0:2], self.banks[2:4]
        o_ring, misc = Ring(self.banks[4:6]), self.tail_ring or Ring(self.banks[6:8])

        q_ready, k_ready, v_ready = {}, {}, {}
        pv_done = {}

        def project(g, kind, m):
            dst = g % 2
            before = (pv_done.get((g - 2) * group + group - 1),)
            n, bank, freed = misc.take()
            pe.wait(w_ready, *events_of(freed))
            if kind == "v":
                bi, half = m
                b = g * group + bi
                cols = min(width, 512)
                pe.wait(self.ctx_ready[b // 4])
                for k in range(KD):
                    mm = nc.tensor.matmul(bank[:, 0:cols], self.ctxT[:, k, b * P:(b + 1) * P],
                                          wv[:, k, half * cols:(half + 1) * cols], start=k == 0, stop=k == KD - 1)
                hs = cols // dk
                target = v1[dst][:, bi, half * hs:(half + 1) * hs, 0:dk]
                src = bank[:, 0:cols].rearrange("p (h d) -> p h d", d=dk)
                if bias:
                    dve.wait(pe.done(mm), *before)
                    e = dve.done(nc.vector.tensor_tensor(
                        target, src, bv[:, half * cols:(half + 1) * cols].rearrange("p (h d) -> p h d", d=dk), ALU.add))
                else:
                    act.wait(pe.done(mm), *before)
                    e = act.done(nc.scalar.activation(target, src, ACT.Copy))
                v_ready[(g, bi)] = v_ready.get((g, bi), ()) + (e,)
                misc.release(n, e)
                return
            src = self.ctxT if kind == "k" else self.xnT
            w = wk if kind == "k" else wq
            if kind == "q":
                pe.wait(*[self.xnT_ready[b] for b in range(g * group, (g + 1) * group)])
            else:
                pe.wait(self.ctx_ready[g * group // 4])
            for k in range(KD):
                mm = nc.tensor.matmul(bank[:, 0:tok], w[:, k, m * P:(m + 1) * P],
                                      src[:, k, g * tok:(g + 1) * tok], start=k == 0, stop=k == KD - 1)
            projected = pe.done(mm)
            if small:
                split(g, kind, m, n, bank, projected)
                return
            act.wait(projected, *before)
            dve.wait(*before)
            if kind == "k":
                e = act.done(nc.scalar.activation(kT[dst][:, m, :], bank[:, 0:tok], ACT.Copy))
                dve.wait(e)
                k_ready[g] = (e, dve.done(nc.vector.tensor_copy(kb[dst][:, m, :], bank[:, 0:tok])))
                misc.release(n, k_ready[g][1])
                return
            for c in range(2):
                e = act.done(nc.scalar.activation(qT[dst][c][:, m, :], bank[:, 0:tok], ACT.Copy,
                                                  scale=self.par[:, c:c + 1]))
            dve.wait(e)
            q_ready[g] = (e, dve.done(nc.vector.tensor_copy(qb[dst][:, m, :], bank[:, 0:tok])))
            misc.release(n, q_ready[g][1])

        def split(g, kind, m, n, bank, projected):
            i = "qk".index(kind)
            if m == 0:
                split.pn, split.parts, freed = parts_ring.take()
                split.before = events_of(freed)
            part = split.parts
            rn, y, rfreed = raw_ring.take()
            act.wait(projected, *split.before, *events_of(rfreed))
            bias_col = (bq if kind == "q" else bk)[:, m:m + 1]
            act.done(nc.scalar.activation(y, bank, ACT.Identity, bias=bias_col))
            e = act.done(nc.scalar.activation(part[:, 0, m, :], bank, ACT.Identity, bias=bias_col))
            misc.release(n, e)
            dve.wait(e)
            e = dve.done(nc.vector.tensor_tensor(y, y, part[:, 0, m, :], ALU.subtract))
            dve.wait(e, *split.before)
            e = dve.done(nc.vector.tensor_copy(part[:, 1, m, :], y))
            dve.wait(e)
            e = dve.done(nc.vector.tensor_tensor(part[:, 2, m, :], y, part[:, 1, m, :], ALU.subtract))
            raw_ring.release(rn, e)
            if m < tiles - 1:
                return
            c = g % 2
            sp.wait(e, *[x for x in (stack_ready.get((kind, g - 2)),) if x])
            stored = parts_sem[i][c].of(nc.sync.dma_start(
                parts_dram[i][c].rearrange("s (m p) c -> p s m c", p=P), part))
            parts_ring.release(split.pn, stored)
            if g == 0:
                load_stack(kind, g, stored)
            else:
                rest.setdefault(now[0] + 1, []).append(lambda: load_stack(kind, g, stored))

        def load_stack(kind, g, stored):
            i, c = "qk".index(kind), g % 2
            sp.wait(stored, pv_done.get((g - 2) * group + group - 1))
            for s, which in enumerate(QPARTS if kind == "q" else KPARTS):
                ready = stack_sem[i][c].of(nc.sync.dma_start(
                    stack[kind][c][s * dk:(s + 1) * dk, :, :], parts_dram[i][c][which].rearrange("(d h) c -> d h c", d=dk)))
            stack_ready[(kind, g)] = ready
            (q_ready if kind == "q" else k_ready)[g] = (ready,)

        stack_ready, now = {}, [0]

        def projections(g):
            keys, queries = ([(g, kind, m) for m in range(tiles)] for kind in "kq")
            values = [(g, "v", (bi, h)) for bi in range(group) for h in range((width + 511) // 512)]
            if g:
                return keys + queries + values
            return keys + values + queries if layer else queries + keys + values

        def pair_load(b):
            c = b % 2
            for i, (rel, keep) in enumerate((("rel", "keep"), ("relT", "keepT"))):
                self.load(rload[c], rt[c][i], d[rel][b], *(r_ready[b - 2] if b >= 2 else self.region_free))
                pair_loaded[b] = self.load(rload[c], mk[c][i], d[keep][b])

        def pair_bias(b):
            c = b % 2
            e = pair_loaded[b]
            pool.wait(e, *((r_read[b - 2],) if b >= 2 else ()))
            ends = []
            for i, dst in enumerate((r_q[c], r_k[c])):
                e1 = pool.done(nc.gpsimd.tensor_scalar(neg, mk[c][i], BIG, -BIG, ALU.mult, ALU.add))
                e2 = pool.done(nc.gpsimd.tensor_copy(kept, mk[c][i]))
                pool.wait(e2)
                e2 = pool.done(nc.gpsimd.tensor_tensor(rt[c][i], rt[c][i], kept, ALU.mult))
                pool.wait(e1, e2)
                e3 = pool.done(nc.gpsimd.tensor_tensor(dst, rt[c][i], neg, ALU.add))
                pool.wait(e3)
                ends.append(e3)
            dve.wait(e)
            any_ready[b] = dve.done(nc.vector.tensor_reduce(any_kept[:, b:b + 1], mk[c][0], AX.X, ALU.max))
            r_ready[b] = (ends[-1], any_ready[b])
            if b + 2 < B:
                pair_load(b + 2)

        if small:
            quads = [list(range(4 * r, 4 * r + 4)) for r in range(4)]
        else:
            quads = [[2 * (4 * (r // 2) + i) + r % 2 for i in range(4)] for r in range(4)]

        def operands(h, b, exact):
            g, bi = b // group, b % group
            t = slice(bi * P, (bi + 1) * P)
            if small:
                return stack["q"][g % 2][:, h, t], stack["k"][g % 2][:, h, t]
            if exact:
                return qT[g % 2][h % 2][:, h // 2, t], kT[g % 2][:, h // 2, t]
            rows = slice(dk * (h % 2), dk * (h % 2 + 1))
            return qb[g % 2][rows, h // 2, t], kb[g % 2][rows, h // 2, t]

        units = [(b, pair) for b in range(B) for pair in range(2)]
        max_done, exp_done, pv_of, st_done = {}, {}, {}, {}
        s_free = [None, None]
        t_free = [None, None]

        def scores_for_max(u):
            b, pair = units[u]
            pe.wait(*q_ready[b // group], *k_ready[b // group], *s_free)
            if mask == "pairs":
                pe.wait(*r_ready[b])
            if mask == "keys":
                pe.wait(kneg_ready)
            for j in range(2):
                if mask == "pairs":
                    nc.tensor.matmul(s_bank[j].rearrange("p (h k) -> p h k", h=4), self.identb,
                                     r_q[b % 2][:, None, :].to_broadcast([P, 4, P]), start=True, stop=False, skip_group_check=True)
                if mask == "keys":
                    nc.tensor.matmul(s_bank[j].rearrange("p (h k) -> p h k", h=4), self.onesb[0:1, 0:P],
                                     kneg[0:1, None, b * P:(b + 1) * P].to_broadcast([1, 4, P]), start=True, stop=False, skip_group_check=True)
            for i in range(4):
                for j in range(2):
                    q, k = operands(quads[2 * pair + j][i], b, False)
                    mm = nc.tensor.matmul(s_bank[j][:, i * P:(i + 1) * P], q, k, start=mask is None, stop=True, skip_group_check=True)
            e = pe.done(mm)
            dve.wait(e, st_done.get(u - 2))
            for j in range(2):
                s_free[j] = dve.done(nc.vector.tensor_reduce(
                    maxes[u % 2][:, j, :], s_bank[j].rearrange("p (h k) -> p h k", h=4), AX.X, ALU.max))
            max_done[u] = s_free[1]

        def scores_for_exp(u, products):
            b, pair = units[u]
            pe.wait(max_done[u], *t_free)
            for j in range(2):
                if mask == "pairs":
                    nc.tensor.matmul(t_bank[j].rearrange("p (h q) -> p h q", h=4), self.ident,
                                     r_k[b % 2][:, None, :].to_broadcast([P, 4, P]), start=True, stop=False, skip_group_check=True)
                if mask == "keys":
                    nc.tensor.matmul(t_bank[j].rearrange("p (h q) -> p h q", h=4), kneg[0:1, b * P:(b + 1) * P],
                                     self.onesb[0:1, None, :].to_broadcast([1, 4, P]),
                                     start=True, stop=False, skip_group_check=True)
            for j in range(2):
                for i in range(4):
                    next(products, None)
                    q, k = operands(quads[2 * pair + j][i], b, True)
                    region = t_bank[j][:, i * P:(i + 1) * P]
                    nc.tensor.matmul(region, maxes[u % 2][:, j, i:i + 1].to_broadcast([P, P]), self.neg_ident,
                                     start=mask is None, stop=False, skip_group_check=True)
                    mm = nc.tensor.matmul(region, k, q, start=False, stop=True, skip_group_check=True)
            e = st_done[u] = pe.done(mm)
            if mask == "pairs":
                r_read[b] = e
            act.wait(e, pv_of.get(u - 2))
            for j in range(2):
                t_free[j] = act.done(nc.scalar.activation(
                    probs[2 * (u % 2) + j].rearrange("p h q -> p (h q)"), t_bank[j], ACT.Exp, scale=scale))
            exp_done[u] = t_free[1]

        o_now = {}
        rest = {}

        def times_v(u):
            b, pair = units[u]
            g, bi = b // group, b % group
            pe.wait(exp_done[u], ones_ready, *v_ready[(g, bi)])
            orow = o_row[b % 2]
            for j in range(2):
                r = 2 * pair + j
                if not small or r == 0:
                    o_now[b] = o_ring.take()
                    pe.wait(*events_of(o_now[b][2]))
                n, bank, _ = o_now[b]
                for i, h in enumerate(quads[r]):
                    at = (h if small else i) * dv1
                    yield
                    mm = nc.tensor.matmul(bank[:, at:at + dv1], probs[2 * (u % 2) + j][:, i, :],
                                          v1[g % 2][:, bi, h, :], start=True, stop=True)
                if small and r < 3:
                    continue
                heads = HEADS if small else 4
                full = bank[:, 0:heads * dv1].rearrange("p (h d) -> p h d", d=dv1)
                rec = recips[b % 2][:, 0:HEADS] if small else recips[b % 2][:, 4 * r:4 * r + 4]
                pv = pe.done(mm)
                dve.wait(pv, o_read.get(b - 2))
                e = dve.done(nc.vector.reciprocal(rec[:, :, None], full[:, :, dk:dv1]))
                dve.wait(e)
                if mask == "pairs":
                    dve.wait(any_ready[b])
                    e = dve.done(nc.vector.tensor_scalar(rec, rec, any_kept[:, b:b + 1], None, ALU.mult))
                    dve.wait(e)
                target = orow if small else orow.rearrange("p (r i c) d -> p r c i d", r=2, c=2)[:, r // 2, r % 2]
                e = dve.done(nc.vector.tensor_tensor(
                    target, full[:, :, 0:dk], rec[:, :, None].to_broadcast([P, heads, dk]), ALU.mult))
                o_ring.release(n, e)
                o_done[b] = e
            pv_of[u] = pe.done(mm) if (small and 2 * pair + 1 < 3) else pv
            if pair == 1:
                pv_done[b] = pv_of[u]

        o_done, o_read = {}, {}

        def turn_out(b):
            flat = o_row[b % 2].rearrange("p h d -> p (h d)")
            col = o_col[b % 2]
            pe.wait(o_done[b])
            if bias:
                pool.wait(self.xn_ready[b], self.x_ready[b], gbo_ready)
                self.x_ready[b] = pool.done(nc.gpsimd.tensor_tensor(self.x[:, b, :], self.x[:, b, :], gbo, ALU.add))
            for t0 in range(0, tiles, 4):
                n, bank, freed = misc.take()
                pe.wait(*events_of(freed))
                some = range(t0, min(tiles, t0 + 4))
                for t in some:
                    mm = self.transpose(bank[:, (t - t0) * P:(t - t0 + 1) * P], flat[:, t * P:(t + 1) * P])
                e = o_read[b] = pe.done(mm)
                act.wait(e, proj_done.get(b - 2))
                e = act.done(nc.scalar.activation(
                    col[:, t0:t0 + len(some), :], bank[:, 0:len(some) * P].rearrange("p (t q) -> p t q", q=P), ACT.Copy))
                misc.release(n, e)
            col_ready[b] = e

        col_ready, proj_done = {}, {}

        def out_project(b):
            n, bank, freed = misc.take()
            pe.wait(col_ready[b], *events_of(freed))
            for t in range(tiles):
                mm = nc.tensor.matmul(bank[:, 0:D], o_col[b % 2][:, t, :], wo[:, t, :],
                                      start=t == 0, stop=t == tiles - 1)
            e = proj_done[b] = pe.done(mm)
            misc.release(n, self.update(b, bank[:, 0:D], layer, e))
            pend[b] = self.ln_stats(b)

        pend = {}
        if mask == "pairs":
            pair_load(0)
            pair_load(1)
        for step in projections(0):
            if step[1:] == ("q", 0):
                self.tail_step(group + 2)
            project(*step)
        if mask == "pairs":
            pair_bias(0)
        if bias:
            dve.wait(w_ready, self.gates_ready)
            gbo_ready = dve.done(nc.vector.tensor_scalar(gbo, gbo, self.gates[:, layer:layer + 1], None, ALU.mult))
        early = [step for step in projections(1) if step[1] != "q"] if small else []
        for step in early:
            project(*step)
        todo = []
        for u in range(len(units) + 9):
            now[0] = u
            for step in rest.pop(u, ()):
                step()
            self.tail_step(2)
            if u == (12 if small else len(units) - 3):
                load_ahead()
            if u < len(units):
                b, pair = units[u]
                if b % group == 0 and pair == 0 and b // group + 1 < B // group:
                    todo = [step for step in projections(b // group + 1) if step not in early]
                    pace = -(-len(todo) // (2 * group - 1))
                if mask == "pairs" and pair == 1 and b + 1 < B:
                    pair_bias(b + 1)
                scores_for_max(u)
            products = iter(times_v(u - 2) if 2 <= u <= len(units) + 1 else ())
            if 1 <= u <= len(units):
                scores_for_exp(u - 1, products)
            if u < len(units) and not (b % group == 0 and pair == 0):
                for step in todo[:pace]:
                    project(*step)
                todo = todo[pace:]
            if 2 <= u <= len(units) + 1:
                for _ in products:
                    pass
                b, pair = units[u - 2]
                if pair == 1:
                    rest.setdefault(u + 1, []).append(lambda b=b: turn_out(b))
                    rest.setdefault(u + 2, []).append(lambda b=b: out_project(b))
                    rest.setdefault(u + 4, []).append(lambda b=b: self.ln_apply(b, pend[b]))
                    rest.setdefault(u + 5, []).append(lambda b=b: self.ln_transpose(b, misc))

    def first_max(self, values, pick, top, ramp, equal):
        nc, dve = self.nc, self.dve
        spread = lambda m: m[:, :, None].to_broadcast([P, B, 8])
        e = dve.done(nc.vector.tensor_reduce(top, values, AX.X, ALU.max))
        dve.wait(e)
        e = dve.done(nc.vector.tensor_tensor(equal, values, spread(top), ALU.is_equal))
        dve.wait(e)
        e = dve.done(nc.vector.tensor_tensor(equal, equal, ramp, ALU.mult))
        dve.wait(e)
        e = dve.done(nc.vector.tensor_reduce(top, equal, AX.X, ALU.max))
        dve.wait(e)
        e = dve.done(nc.vector.tensor_tensor(pick, equal, spread(top), ALU.is_equal))
        dve.wait(e)
        return e

    def load_moe(self, layer, inter):
        a, d = self.ahead, self.d
        chunks = -(-inter // P)
        wide = KD * 2 * inter + chunks * D
        self.limit = SBUF_END - 512
        small, free = self.arrivals("router_w"), self.engines_last() + (self.phi_b_stored,)
        a["router"] = self.high("router", [P, KD, 8])
        a["router_ready"] = self.load(small, a["router"], d[f"L{layer}_router"], *free)
        if layer == 1:
            a["bias"], a["shared_w"] = self.high("gate_bias", [P, 8]), self.high("shared_w", [P, wide])
            a["router_ready"] = self.load(small, a["bias"], d["L1_gate_bias"].to_broadcast([P, 8]))
            a["shared_ready"] = self.load(self.arrivals("shared_w"), a["shared_w"], d["L1_shared"])

    def moe(self, layer, experts, inter, topk):
        nc, pe, act, dve, pool, sp, d = self.nc, self.pe, self.act, self.dve, self.pool, self.sp, self.d
        V = nc.vector
        shared = layer == 1
        gate = 4 + layer
        blocks = T * topk // P + experts - 1
        chunks = -(-inter // P)
        last_rows = inter - (chunks - 1) * P
        wide = KD * 2 * inter + chunks * D
        groups, c = [], 0
        while c < chunks:
            n = 2 if c + 2 < chunks or (c + 2 == chunks and last_rows == P) else 1
            groups.append(list(range(c, c + n)))
            c += n
        self.phase()
        free = self.region_free
        router, router_ready = self.ahead["router"], self.ahead["router_ready"]
        if shared:
            bias8, shared_w, shared_ready = (self.ahead[name] for name in ("bias", "shared_w", "shared_ready"))
        ahead_limit, self.limit = self.limit, SBUF_END
        pos_i = [self.high("pos_int", [P, B], I32) for _ in range(topk)]
        tw = [self.high("token_weight", [P, B]) for _ in range(topk)]
        nb = min(B * topk, 24)
        back = [self.high("gathered", [P, D]) for _ in range(nb)]
        attention_limit, self.limit = self.limit, min(self.limit, ahead_limit)
        nw = 4
        weights = [self.tmp("expert_w", [P, wide]) for _ in range(nw)]
        w_sems = [self.arrivals("expert_w") for _ in range(nw)]
        nr = 4
        rows = [self.tmp("block_rows", [P, D]) for _ in range(nr)]
        r_sems = [self.arrivals("block_rows") for _ in range(nr)]
        cols = [self.tmp("block_T", [P, KD, P]) for _ in range(2)]
        silu = [self.tmp("silu", [P, 2 * P]) for _ in range(2)]
        hid = [self.tmp("hidden", [P, chunks, P]) for _ in range(2)]
        youts = [self.tmp("block_out", [P, D]) for _ in range(3)]
        y_sems = [self.arrivals("block_out") for _ in range(3)]
        b_sems = [self.arrivals("gathered") for _ in range(B)]
        xs_dram = nc.dram_tensor(f"sorted_x_{layer}", [blocks * P, D], F32, kind="Internal").ap()
        ys_dram = nc.dram_tensor(f"sorted_y_{layer}", [blocks * P, D], F32, kind="Internal").ap()
        t = lambda name, shape, dtype=F32: self.tmp(name, shape, dtype)
        BE = B * 8
        zeros = t("zeros", [P, 2 * D])
        ramp, step, reset = t("ramp", [P, B, 8]), t("block_step", [P, 8, B]), t("reset", [P, 8, B])
        index = t("block_index", [P, blocks, 8])
        logits, equal, top = t("logits", [P, B, 8]), t("equal", [P, B, 8]), t("top", [P, B])
        picks = [t("pick", [P, B, 8]) for _ in range(topk)]
        both = t("either_pick", [P, B, 8])
        total, upto = t("tile_totals", [P, 8, B]), t("totals_upto", [P, 8, B])
        more, nblk, end, ones8 = t("more", [P, 8, B]), t("nblk", [P, 8]), t("end_block", [P, 8]), t("ones8", [P, 8])
        base, rank, tmp8 = t("base", [P, 8]), t("rank", [P, B, 8]), t("tmp8", [P, B, 8])
        past, eid, eid_i = t("past", [P, blocks, 8]), t("expert_row", [P, blocks]), t("expert_row_int", [P, blocks], I32)
        pos = [t("pos", [P, B]) for _ in range(topk)]

        g = nc.gpsimd
        pool.wait(*free)
        pool.done(g.iota(ramp, pattern=[[0, B], [-1, 8]], base=8, channel_multiplier=0, allow_small_or_imprecise_dtypes=True))
        pool.done(g.iota(step, pattern=[[0, 8], [P, B]], base=0, channel_multiplier=0, allow_small_or_imprecise_dtypes=True))
        pool.done(g.iota(index, pattern=[[1, blocks], [0, 8]], base=0, channel_multiplier=0, allow_small_or_imprecise_dtypes=True))
        pool.done(g.memset(zeros, 0.0))
        pool.done(g.memset(ones8, 1.0))
        e = pool.done(g.memset(reset, 1.0))
        pool.wait(e)
        tables_ready = pool.done(g.memset(reset[:, :, 0:1], 0.0))
        zero_sem = self.arrivals("zero_fill")
        sp.wait(tables_ready)
        half = blocks * P // (2 * P)
        zero_done = zero_sem.of(nc.sync.dma_start(
            xs_dram[0:half * 2 * P, :].rearrange("(p n r) d -> p n (r d)", p=P, r=2),
            zeros[:, None, :].to_broadcast([P, half, 2 * D])))
        if blocks % 2:
            zero_done = zero_sem.of(nc.sync.dma_start(xs_dram[half * 2 * P:, :], zeros[:, 0:D]))
        rb = self.banks[0]
        pe.wait(router_ready, *self.xnT_ready, *free)
        for b in range(B):
            for k in range(KD):
                mm = nc.tensor.matmul(rb[:, b * 8:(b + 1) * 8], self.xnT[:, k, b * P:(b + 1) * P], router[:, k, :],
                                      start=k == 0, stop=k == KD - 1)
        dve.wait(pe.done(mm), tables_ready, router_ready, *free)
        spread = lambda m: m[:, :, None].to_broadcast([P, B, 8])
        bank3 = rb[:, 0:BE].rearrange("p (b e) -> p b e", e=8)
        e = dve.done(V.tensor_copy(logits, bank3))
        dve.wait(e)
        if shared:
            prob = t("router_prob", [P, B, 8])
            e = dve.done(V.tensor_reduce(top, logits, AX.X, ALU.max))
            dve.wait(e)
            e = dve.done(V.tensor_tensor(logits, logits, spread(top), ALU.subtract))
            act.wait(e)
            e = act.done(nc.scalar.activation(prob, logits, ACT.Exp))
            dve.wait(e)
            e = dve.done(V.tensor_reduce(top, prob, AX.X, ALU.add))
            dve.wait(e)
            e = dve.done(V.reciprocal(top, top))
            dve.wait(e)
            e = dve.done(V.tensor_tensor(prob, prob, spread(top), ALU.mult))
            dve.wait(e)
            e = dve.done(V.tensor_tensor(logits, prob, bias8[:, None, :].to_broadcast([P, B, 8]), ALU.add))
            dve.wait(e)
        for n in range(topk):
            e = self.first_max(logits, picks[n], top, ramp, equal)
            if n + 1 < topk:
                e = dve.done(V.tensor_scalar(tmp8, picks[n], BIG, None, ALU.mult))
                dve.wait(e)
                e = dve.done(V.tensor_tensor(logits, logits, tmp8, ALU.subtract))
                dve.wait(e)
            if shared:
                e = dve.done(V.tensor_tensor(tmp8, prob, picks[n], ALU.mult))
                dve.wait(e)
                e = dve.done(V.tensor_reduce(tw[n], tmp8, AX.X, ALU.add))
                dve.wait(e)
                e = dve.done(V.tensor_scalar(tw[n], tw[n], self.gates[:, gate:gate + 1], None, ALU.mult))
                dve.wait(e)
        if topk == 2:
            e = dve.done(V.tensor_tensor(both, picks[0], picks[1], ALU.add))
        else:
            both = picks[0]
        pb = self.banks[1]
        flat = both.rearrange("p b e -> p (b e)")
        pe.wait(e)
        nc.tensor.matmul(pb[:, 0:BE], self.before, flat, start=True, stop=True)
        e = pe.done(nc.tensor.matmul(pb[:, BE:2 * BE], self.ones, flat, start=True, stop=True))
        dve.wait(e)
        e = dve.done(V.tensor_copy(total, pb[:, BE:2 * BE].rearrange("p (b e) -> p e b", e=8)))
        dve.wait(e)
        line = lambda m: m.rearrange("p e b -> p (e b)")
        e = dve.done(V.tensor_tensor_scan(line(upto), line(reset), line(total), 0.0, ALU.mult, ALU.add))
        dve.wait(e)
        e = dve.done(V.tensor_tensor(more, upto[:, :, B - 1:B].to_broadcast([P, 8, B]), step, ALU.is_gt))
        dve.wait(e)
        e = dve.done(V.tensor_reduce(nblk, more, AX.X, ALU.add))
        e2 = dve.done(V.tensor_tensor(upto, upto, total, ALU.subtract))
        dve.wait(e)
        e = dve.done(V.tensor_tensor_scan(end, ones8, nblk, 0.0, ALU.mult, ALU.add))
        dve.wait(e)
        e = dve.done(V.tensor_tensor(base, end, nblk, ALU.subtract))
        dve.wait(e)
        e = dve.done(V.tensor_scalar(base, base, float(P), None, ALU.mult))
        e1 = dve.done(V.tensor_tensor(past, index, end[:, None, :].to_broadcast([P, blocks, 8]), ALU.is_ge))
        dve.wait(e1)
        e1 = dve.done(V.tensor_reduce(eid, past, AX.X, ALU.add))
        dve.wait(e1)
        e1 = dve.done(V.tensor_scalar(eid, eid, float(experts - 1), float(P), ALU.min, ALU.mult))
        dve.wait(e1)
        ids_ready = dve.done(V.tensor_copy(eid_i, eid))
        dve.wait(e, e2)
        e = dve.done(V.tensor_tensor(rank, pb[:, 0:BE].rearrange("p (b e) -> p b e", e=8),
                                     upto.rearrange("p e b -> p b e"), ALU.add))
        dve.wait(e)
        e = dve.done(V.tensor_tensor(rank, rank, base[:, None, :].to_broadcast([P, B, 8]), ALU.add))
        dve.wait(e)
        for n in range(topk):
            e = dve.done(V.tensor_tensor(tmp8, rank, picks[n], ALU.mult))
            dve.wait(e)
            e = dve.done(V.tensor_reduce(pos[n], tmp8, AX.X, ALU.add))
            dve.wait(e)
            pos_ready = dve.done(V.tensor_copy(pos_i[n], pos[n]))

        scattered = self.arrivals("scattered")
        pool.wait(pos_ready, zero_done, *self.xn_ready)
        for b in range(B):
            for n in range(topk):
                all_scattered = scattered.of(g.indirect_dma_start(
                    xs_dram, bass.IndirectOffsetOnAxis(pos_i[n][:, b:b + 1], 0), self.xn[:, b, :], None))

        gu_ring, y_ring, t_ring = Ring(self.banks[0:4]), Ring(self.banks[4:6]), Ring(self.banks[6:8])
        gu_ring.release(0, pos_ready)
        gu_ring.release(1, pos_ready)
        silu_ring, down_done, w_read, hid_read = Ring(silu), {}, {}, {}
        col_read, y_copied, y_stored, row_read = {}, {}, {}, {}
        steps = ([("shared", b) for b in range(B)] if shared else []) + [("routed", i) for i in range(blocks)]
        w_ready, rows_ready, cols_ready, h_ready = {}, {}, {}, {}

        def load_rows(i):
            rows_ready[i] = self.load(r_sems[i % nr], rows[i % nr], xs_dram[i * P:(i + 1) * P, :], all_scattered, row_read.get(i - nr))

        def load_weights(i):
            slot = i % nw
            sp.wait(ids_ready)
            row = nc.sync.value_load(eid_i[0:1, i:i + 1], min_val=0, max_val=(experts - 1) * P)
            w_ready[i] = self.load(w_sems[slot], weights[slot], d[f"L{layer}_experts"][bass.ds(row, P), :], w_read.get(i - nw))

        def turn_block(i):
            n, bank, freed = t_ring.take()
            pe.wait(rows_ready[i], *events_of(freed))
            for k in range(KD):
                mm = self.transpose(bank[:, k * P:(k + 1) * P], rows[i % nr][:, k * P:(k + 1) * P])
            row_read[i] = pe.done(mm)
            act.wait(row_read[i], col_read.get(i - 2))
            cols_ready[i] = act.done(nc.scalar.activation(
                cols[i % 2], bank[:, 0:KD * P].rearrange("p (k t) -> p k t", k=KD), ACT.Copy))
            t_ring.release(n, cols_ready[i])

        def up(s, kind, i):
            if kind == "shared":
                w, x_in = shared_w, self.xnT[:, :, i * P:(i + 1) * P]
                pe.wait(shared_ready)
            else:
                w, x_in = weights[i % nw], cols[i % 2]
                pe.wait(w_ready[i], cols_ready[i])
            for gr in groups:
                n, bank, freed = gu_ring.take()
                pe.wait(*events_of(freed))
                m = last_rows if gr[-1] == chunks - 1 else P
                for half in range(2):
                    for j, c in enumerate(gr):
                        at = (half * len(gr) + j) * P
                        for k in range(KD):
                            col = (k * 2 + half) * inter + c * P
                            mm = nc.tensor.matmul(bank[0:m, at:at + P], w[:, col:col + m], x_in[:, k, :],
                                                  start=k == 0, stop=k == KD - 1)
                e = pe.done(mm)
                size = len(gr) * P
                sn, sbuf, sfreed = silu_ring.take()
                act.wait(e, *events_of(sfreed))
                e = act.done(nc.scalar.activation(sbuf[0:m, 0:size], bank[0:m, 0:size], ACT.Silu))
                dve.wait(e, hid_read.get(s - 2))
                h_ready[s] = dve.done(V.tensor_tensor(
                    hid[s % 2][0:m, gr[0]:gr[0] + len(gr), :], sbuf[0:m, 0:size].rearrange("p (c t) -> p c t", t=P),
                    bank[0:m, size:2 * size].rearrange("p (c t) -> p c t", t=P), ALU.mult))
                gu_ring.release(n, h_ready[s])
                silu_ring.release(sn, h_ready[s])
            if kind == "routed":
                col_read[i] = (pe.semaphore, pe.count)

        def down(s, kind, i):
            w = shared_w if kind == "shared" else weights[i % nw]
            n, bank, freed = y_ring.take()
            pe.wait(h_ready[s], *events_of(freed))
            for c in range(chunks):
                m = last_rows if c == chunks - 1 else P
                col = KD * 2 * inter + c * D
                mm = nc.tensor.matmul(bank[:, 0:D], hid[s % 2][0:m, c, :], w[0:m, col:col + D],
                                      start=c == 0, stop=c == chunks - 1)
            e = hid_read[s] = pe.done(mm)
            if kind == "shared":
                y_ring.release(n, self.update(i, bank[:, 0:D], gate, e))
                return
            w_read[i] = e
            dve.wait(e, y_stored.get(i - 3))
            e = dve.done(V.tensor_copy(youts[i % 3], bank[:, 0:D]))
            y_ring.release(n, e)
            y_copied[i] = e

        def store_block(i):
            sp.wait(y_copied[i])
            y_stored[i] = y_sems[i % 3].of(nc.sync.dma_start(ys_dram[i * P:(i + 1) * P, :], youts[i % 3]))

        for i in range(2):
            load_weights(i)
        for i in range(nr):
            load_rows(i)
        for i in range(2, nw):
            load_weights(i)
        for s in range(len(steps) + 1):
            if s < len(steps):
                kind, i = steps[s]
                if steps[s] == ("routed", 0):
                    turn_block(0)
                up(s, kind, i)
                if kind == "routed" and i + 1 < blocks:
                    turn_block(i + 1)
            if s >= 1:
                kind, i = steps[s - 1]
                down(s - 1, kind, i)
                if kind == "routed":
                    if i + nr < blocks:
                        load_rows(i + nr)
                    if i + nw < blocks:
                        load_weights(i + nw)
                    store_block(i)

        self.limit = attention_limit
        pool.wait(*[y_stored[i] for i in range(blocks - 3, blocks)])
        order = [(b, n) for b in range(B) for n in range(topk)]
        gathered, taken = {}, {}

        def gather(m):
            b, n = order[m]
            pool.wait(taken.get(m - nb))
            gathered[b] = b_sems[b].of(g.indirect_dma_start(
                back[m % nb], None, ys_dram, bass.IndirectOffsetOnAxis(pos_i[n][:, b:b + 1], 0)))

        def finish_tile(b):
            for n in range(topk):
                m = b * topk + n
                if shared:
                    dve.wait(self.x_ready[b], gathered[b])
                    self.x_ready[b] = dve.done(V.scalar_tensor_tensor(
                        self.x[:, b, :], back[m % nb], tw[n][:, b:b + 1], self.x[:, b, :], ALU.mult, ALU.add))
                else:
                    self.update(b, back[m % nb], gate, gathered[b])
                taken[m] = self.x_ready[b]
            for m in range((b + 7) * topk, min((b + 8) * topk, B * topk)):
                gather(m)

        self.leave_layernorms(finish_tile, t_ring)
        for m in range(7 * topk):
            gather(m)

    def load_phi(self):
        self.limit = SBUF_END
        a, loads = self.ahead, self.arrivals("phi")
        a["phi"], a["phi_at"] = self.high("phiT", [P, KD, SLOTS]), self.limit
        a["phib"] = self.high("phi_b_parts", [3, SLOTS], BF16)
        self.load(loads, a["phib"], self.phi_b_parts, self.phi_b_stored, *self.engines_last())
        a["phi_ready"] = self.load(loads, a["phi"], self.d["phiT"])

    def soft_moe(self):
        nc, pe, act, dve, pool, sp, d = self.nc, self.pe, self.act, self.dve, self.pool, self.sp, self.d
        V = nc.vector
        self.phase()
        free = self.region_free
        group, nd = 4, 6
        acc = self.tmp("slot_sums", [P, ST, D])
        disp_at = self.at
        disp = [self.tmp("dispatch", [P, SLOTS]) for _ in range(nd)]
        phi, phi_at, phib, phi_ready = (self.ahead[name] for name in ("phi", "phi_at", "phib", "phi_ready"))
        lg_at = self.at
        lg = [self.tmp("slot_logits", [P, SLOTS]) for _ in range(2)]
        comb_at = self.at
        comb = [self.tmp("combine", [P, SLOTS]) for _ in range(3)]
        combT = self.tmp("combineT", [P, ST, P])
        gmax, gsum = self.tmp("expert_max", [P, NEXP]), self.tmp("expert_sum", [P, NEXP])
        smax, ssum = self.tmp("slot_max", [P, PSLOT]), self.tmp("slot_sum", [P, PSLOT])
        xt = [self.tmp("slots_normed", [P, D]) for _ in range(4)]
        sst, smv = self.tmp("slot_stats", [P, ST, 6]), self.tmp("slot_mean_var", [P, ST, 2])
        sve, srs = self.tmp("slot_var_eps", [P, ST]), self.tmp("slot_rstd", [P, ST])
        ct_dram = nc.dram_tensor("combineT_rows", [B, P, ST * P], F32, kind="Internal").ap()
        lbank = self.banks[0:4]
        xt_ring, misc = Ring(self.banks[4:6]), Ring(self.banks[6:8])
        pe.wait(phi_ready, *free)
        act.wait(*free)
        dve.wait(*free)
        pool.wait(*free)
        lg_free, lb_free, d_ready, d_read, c_ready, c_read, ct_stored = {}, [None] * 4, {}, {}, {}, {}, None
        lg_ready, c_exp = {}, {}
        cts = self.arrivals("combineT_store")
        acc_ready = [None] * (ST // 2)
        by_expert = lambda m: m.rearrange("p (n s) -> p n s", s=PSLOT)
        by_slot = lambda m: m.rearrange("p (n s) -> p s n", s=PSLOT)

        def slot_logits(b):
            pe.wait(self.xnT_ready[b])
            for j in range(4):
                pe.wait(lb_free[j])
                cs = slice(j * 512, (j + 1) * 512)
                for k in range(KD):
                    nc.tensor.matmul(lbank[j], self.xnT[:, k, b * P:(b + 1) * P], phi[:, k, cs], start=k == 0, stop=False)
                e = pe.done(nc.tensor.matmul(lbank[j], self.onesb[0:3, 0:P], phib[:, cs], start=False, stop=True))
                act.wait(e, *lg_free.get(b - 2, ()))
                e = lb_free[j] = act.done(nc.scalar.activation(lg[b % 2][:, cs], lbank[j], ACT.Copy))
            lg_ready[b] = e

        def slot_weights(b):
            D_, C_, L_ = disp[b % nd], comb[b % 3], lg[b % 2]
            dve.wait(lg_ready[b], d_read.get(b - nd), lg_free.get(b - 1, (None, None))[1])
            e2 = dve.done(V.tensor_reduce(smax, by_slot(L_), AX.X, ALU.max))
            e1 = dve.done(V.tensor_reduce(gmax, by_expert(L_), AX.X, ALU.max))
            dve.wait(e1)
            e3 = dve.done(V.tensor_tensor(by_expert(D_), by_expert(L_), gmax[:, :, None].to_broadcast([P, NEXP, PSLOT]), ALU.subtract))
            pool.wait(e2, c_read.get(b - 3))
            e4 = pool.done(nc.gpsimd.tensor_tensor(by_expert(C_), by_expert(L_), smax[:, None, :].to_broadcast([P, NEXP, PSLOT]), ALU.subtract))
            lg_free[b] = (e3, e4)
            act.wait(e3)
            e3 = act.done(nc.scalar.activation(D_, D_, ACT.Exp))
            act.wait(e4)
            c_exp[b] = act.done(nc.scalar.activation(C_, C_, ACT.Exp))
            combine_weights(b - 1)
            dve.wait(e3)
            e3 = dve.done(V.tensor_reduce(gsum, by_expert(D_), AX.X, ALU.add))
            dve.wait(e3)
            e3 = dve.done(V.reciprocal(gsum, gsum))
            dve.wait(e3)
            d_ready[b] = dve.done(V.tensor_tensor(by_expert(D_), by_expert(D_), gsum[:, :, None].to_broadcast([P, NEXP, PSLOT]), ALU.mult))

        def combine_weights(b):
            if b < 0:
                return
            C_ = comb[b % 3]
            dve.wait(c_exp[b], c_ready.get(b - 1))
            e4 = dve.done(V.tensor_reduce(ssum, by_slot(C_), AX.X, ALU.add))
            dve.wait(e4)
            e4 = dve.done(V.reciprocal(ssum, ssum))
            pool.wait(e4)
            c_ready[b] = pool.done(nc.gpsimd.tensor_tensor(by_expert(C_), by_expert(C_), ssum[:, None, :].to_broadcast([P, NEXP, PSLOT]), ALU.mult))

        def turn_combine(b):
            nonlocal ct_stored
            pe.wait(c_ready[b])
            for j in range(0, ST, 4):
                n, bank, freed = misc.take()
                pe.wait(*events_of(freed))
                for i in range(4):
                    mm = self.transpose(bank[:, i * P:(i + 1) * P], comb[b % 3][:, (j + i) * P:(j + i + 1) * P])
                e = pe.done(mm)
                act.wait(e, ct_stored)
                e2 = act.done(nc.scalar.activation(combT[:, j:j + 4, :], bank.rearrange("p (s t) -> p s t", t=P), ACT.Copy))
                misc.release(n, e2)
            c_read[b] = e
            sp.wait(e2)
            ct_stored = cts.of(nc.sync.dma_start(ct_dram[b], combT.rearrange("p s t -> p (s t)")))

        def slot_sums(gp, j):
            tiles = range(gp * group, (gp + 1) * group)
            n, bank, freed = xt_ring.take()
            pe.wait(*[d_ready[b] for b in tiles], *events_of(freed))
            for i in range(2):
                for b in tiles:
                    mm = nc.tensor.matmul(bank[:, i * D:(i + 1) * D], disp[b % nd][:, (j + i) * P:(j + i + 1) * P],
                                          self.xn[:, b, :], start=b == tiles[0], stop=b == tiles[-1])
            e = pe.done(mm)
            target, src = acc[:, j:j + 2, :], bank.rearrange("p (s d) -> p s d", d=D)
            dve.wait(e, acc_ready[j // 2])
            if gp == 0:
                e2 = dve.done(V.tensor_copy(target, src))
            else:
                e2 = dve.done(V.tensor_tensor(target, target, src, ALU.add))
            acc_ready[j // 2] = e2
            xt_ring.release(n, e2)
            for b in tiles:
                d_read[b] = e

        half = ST // 2
        slot_logits(0)
        for b in range(B + 2):
            if b + 1 < B:
                slot_logits(b + 1)
            if b < B:
                slot_weights(b)
            if b == B:
                combine_weights(B - 1)
            if b >= group and b % group in (0, 1):
                at = half * (b % group)
                if b < B:
                    for j in range(at, at + half, 2):
                        slot_sums(b // group - 1, j)
            if b >= 2:
                turn_combine(b - 2)
        logits_read, logits_used = lb_free[3], lg_free[B - 1]

        self.limit = SBUF_END
        self.at = phi_at
        xtT = self.tmp("slots_normed_T", [P, KD, SLOTS])
        self.at = lg_at
        yt = self.tmp("slot_outputs", [P, ST, D])
        self.at = comb_at
        ne = 3
        ew = [self.tmp("expert_w", [P, 4, KD, D]) for _ in range(ne)]
        ews = [self.arrivals("expert_w") for _ in range(ne)]
        ebs = self.arrivals("expert_b")
        for j in range(4):
            yb_ready = self.load(ebs, yt[j * PSLOT:(j + 1) * PSLOT, :, :],
                                 d["expert_b"][j].rearrange("(a s) d -> a s d", a=1).to_broadcast([PSLOT, ST, D]), *logits_used)
        ew_read, ew_ready = {}, {}

        def load_expert(s):
            ew_ready[s] = self.load(ews[s % ne], ew[s % ne], d["expert_w"][s], ew_read.get(s - ne), c_read[B - 1], ct_stored)

        stats_ready, normed, xt_free, xtT_ready = {}, {}, {}, {}

        def slot_stats(j):
            dve.wait(acc_ready[j // 2])
            e = dve.done(V.tensor_scalar(acc[:, j:j + 2, :], acc[:, j:j + 2, :], -33000.0, 65000.0, ALU.max, ALU.min))
            dve.wait(e)
            for s in (j, j + 1):
                e = dve.done(V.bn_stats(sst[:, s, :], acc[:, s, :]))
            dve.wait(e)
            for s in (j, j + 1):
                e = dve.done(V.bn_aggr(smv[:, s, :], sst[:, s, :]))
            pool.wait(e)
            e = pool.done(nc.gpsimd.tensor_scalar(sve[:, j:j + 2, None], smv[:, j:j + 2, 1:2], EPS, None, ALU.add))
            pool.wait(e)
            stats_ready[j] = pool.done(nc.gpsimd.tensor_tensor(srs[:, j:j + 2], sve[:, j:j + 2], self.half_power[:, 0:2], ALU.pow))

        def slot_norm(j):
            dve.wait(stats_ready[j])
            for s in (j, j + 1):
                e = dve.done(V.tensor_scalar(acc[:, s, :], acc[:, s, :], smv[:, s, 0:1], srs[:, s:s + 1], ALU.subtract, ALU.mult))
                act.wait(e, xt_free.get(s - 4))
                normed[s] = act.done(nc.scalar.activation(xt[s % 4], acc[:, s, :], ACT.Tanh))

        def slot_turn(s):
            n, bank, freed = misc.take()
            pe.wait(normed[s], *events_of(freed))
            for k in range(KD):
                mm = self.transpose(bank[:, k * P:(k + 1) * P], xt[s % 4][:, k * P:(k + 1) * P])
            xt_free[s] = pe.done(mm)
            act.wait(xt_free[s], logits_read)
            xtT_ready[s] = act.done(nc.scalar.activation(xtT[:, :, s * P:(s + 1) * P], bank[:, 0:KD * P].rearrange("p (k t) -> p k t", k=KD), ACT.Copy))
            misc.release(n, xtT_ready[s])

        e_ring = Ring(self.banks[0:2])
        e_ring.release(0, logits_read)
        e_ring.release(1, logits_read)

        def slot_expert(s):
            nonlocal yt_ready
            n, bank, freed = e_ring.take()
            pe.wait(ew_ready[s], xtT_ready[s], *events_of(freed))
            for j in range(4):
                for k in range(KD):
                    mm = nc.tensor.matmul(bank[j * PSLOT:(j + 1) * PSLOT, 0:D], xtT[:, k, s * P + j * PSLOT:s * P + (j + 1) * PSLOT],
                                          ew[s % ne][:, j, k, :], start=k == 0, stop=k == KD - 1)
            ew_read[s] = pe.done(mm)
            dve.wait(ew_read[s], yb_ready)
            yt_ready = dve.done(V.tensor_tensor(yt[:, s, :], yt[:, s, :], bank[:, 0:D], ALU.add))
            e_ring.release(n, yt_ready)
            if s + ne < ST:
                load_expert(s + ne)

        yt_ready = None
        for s in range(ne):
            load_expert(s)
        for t in range(half + 4):
            if t < half:
                slot_sums(B // group - 1, 2 * t)
                slot_stats(2 * t)
            if 1 <= t <= half:
                slot_norm(2 * t - 2)
            if 2 <= t <= half + 1:
                slot_turn(2 * t - 4)
                slot_turn(2 * t - 3)
            if t >= 4:
                slot_expert(2 * t - 8)
                slot_expert(2 * t - 7)

        self.at = disp_at
        ctl = [self.tmp("combineT_load", [P, ST, P]) for _ in range(3)]
        ctls = [self.arrivals("combineT_load") for _ in range(3)]
        ct_read, ct_ready, pend = {}, {}, {}

        def load_combine(b):
            ct_ready[b] = self.load(ctls[b % 3], ctl[b % 3].rearrange("p s t -> p (s t)"), ct_dram[b], ct_stored, d_read[B - 1], ct_read.get(b - 3))

        for b in range(3):
            load_combine(b)
        pe.wait(yt_ready)
        for b in range(B + 2):
            if b >= 2:
                self.ln_transpose(b - 2, misc)
            if 1 <= b <= B:
                self.ln_apply(b - 1, pend[b - 1])
            if b < B:
                n, bank, freed = xt_ring.take()
                pe.wait(ct_ready[b], *events_of(freed))
                for s in range(ST):
                    mm = nc.tensor.matmul(bank[:, 0:D], ctl[b % 3][:, s, :], yt[:, s, :], start=s == 0, stop=s == ST - 1)
                ct_read[b] = pe.done(mm)
                if b + 3 < B:
                    load_combine(b + 3)
                xt_ring.release(n, self.update(b, bank[:, 0:D], 6, ct_read[b]))
                pend[b] = self.ln_stats(b)

    def load_peer(self):
        d, self.limit, at = self.d, SBUF_END, self.at
        free, self.at = self.engines_last(), self.floor
        wq, down, up = self.tmp("wq", [P, KD, QH * QD]), self.tmp("downT", [P, KD, D]), self.tmp("up", [P, 2, D])
        bq, gamma, beta = self.tmp("bq", [P, QH * QD // P]), self.tmp("gamma", [P, 1]), self.tmp("beta", [P, 1])
        keys = self.tmp("keys", [P, 32])
        ws = self.arrivals("peer_w")
        self.load(ws, wq, d["L3f_Wq"], *free)
        self.load(ws, bq, d["L3f_bq"])
        for i in range(2):
            for name, m in (("gamma", gamma), ("beta", beta)):
                self.load(ws, m[i * QD:(i + 1) * QD, :], d["L3f_" + name])
            for j in range(2):
                at = (2 * i + j) * NKEY
                self.load(ws, keys[at:at + NKEY, :], d[f"key{j}"])
        self.load(ws, down, d["downT"])
        w_ready = self.load(ws, up, d["up"])
        self.ahead["peer"], self.ahead["peer_end"] = (wq, down, up, bq, gamma, beta, keys, w_ready), self.at
        assert self.at - self.floor <= 3 * KD * HEADS * QD * 4
        self.at = at

    def peer(self):
        nc, pe, act, dve, pool, sp, d = self.nc, self.pe, self.act, self.dve, self.pool, self.sp, self.d
        V, G = nc.vector, nc.gpsimd
        self.phase()
        free = self.region_free
        QT = QH * QD // P
        NG = 2 * QH
        wq, down, up, bq, gamma, beta, keys, w_ready = self.ahead["peer"]
        self.at = self.ahead["peer_end"]
        keysq, kn = self.tmp("keys_sq", [P, 32]), self.tmp("key_norm", [P, 1])
        kdiag, kT = self.tmp("keys_diag", [P, P]), self.tmp("keys_diag_T", [P, P])
        blocks32, pairm = self.tmp("block_of_32", [P, 4]), self.tmp("pair_mean", [P, P])
        q = self.tmp("queries_T", [P, QT, T])
        qst, qmv, ex2 = self.tmp("q_stats", [P, QT, 4, 6]), self.tmp("q_mv", [P, QT, 2]), self.tmp("q_ex2", [P, QT, 1])
        mom, var, sc, sh = self.tmp("moments", [P, 2]), self.tmp("q_var", [P, 1]), self.tmp("q_scale", [P, 1]), self.tmp("q_shift", [P, 1])
        gl = self.tmp("gelu_T", [P, 2, T])
        reset = self.tmp("reset", [P, NG, NKEY])
        pool.wait(*free)
        pool.done(G.memset(kdiag, 0.0))
        e = pool.done(G.memset(reset, 1.0))
        pool.wait(e)
        set_ready = pool.done(G.memset(reset[:, :, 0:1], 0.0))
        dve.wait(w_ready, set_ready, *free)
        e = dve.done(V.tensor_tensor(keysq, keys, keys, ALU.mult))
        dve.wait(e)
        e = dve.done(V.tensor_reduce(kn, keysq, AX.X, ALU.add))
        dve.wait(e)
        e = dve.done(V.tensor_scalar(kn, kn, 1e-24, None, ALU.max))
        pool.wait(e)
        e = pool.done(G.tensor_tensor(kn, kn, self.half_power[:, 0:1], ALU.pow))
        dve.wait(e)
        for i in range(4):
            r = slice(i * NKEY, (i + 1) * NKEY)
            kd_ready = dve.done(V.tensor_scalar(kdiag[r, r], keys[r, :], kn[r, :], None, ALU.mult))
        b32_ready = dve.done(V.tensor_reduce(blocks32, self.ident.rearrange("p (i c) -> p i c", c=32), AX.X, ALU.add))
        ids = self.ident.rearrange("p (i c) -> p i c", i=2)
        e = dve.done(V.tensor_tensor(pairm[:, 0:QD], ids[:, 0, :], ids[:, 1, :], ALU.add))
        dve.wait(e)
        e = dve.done(V.tensor_scalar(pairm[:, 0:QD], pairm[:, 0:QD], 1.0 / QH, None, ALU.mult))
        dve.wait(e)
        pm_ready = dve.done(V.tensor_copy(pairm[:, QD:P], pairm[:, 0:QD]))
        ring, misc = Ring(self.banks[0:4]), Ring(self.banks[4:6])
        pe.wait(*free)
        act.wait(*free)
        for g in range(4):
            pe.wait(w_ready, *self.xnT_ready[4 * g:4 * g + 4])
            for m in range(QT):
                n, bank, freed = ring.take()
                pe.wait(*events_of(freed))
                for k in range(KD):
                    mm = nc.tensor.matmul(bank, wq[:, k, m * P:(m + 1) * P], self.xnT[:, k, g * 512:(g + 1) * 512],
                                          start=k == 0, stop=k == KD - 1)
                act.wait(pe.done(mm), w_ready)
                e = act.done(nc.scalar.activation(q[:, m, g * 512:(g + 1) * 512], bank, ACT.Identity, bias=bq[:, m:m + 1]))
                ring.release(n, e)
                dve.wait(e)
                st_ready = dve.done(V.bn_stats(qst[:, m, g, :], q[:, m, g * 512:(g + 1) * 512]))
        def gelu(g, m):
            n, bank, freed = ring.take()
            pe.wait(*events_of(freed))
            for k in range(KD):
                mm = nc.tensor.matmul(bank, down[:, k, m * P:(m + 1) * P], self.xnT[:, k, g * 512:(g + 1) * 512],
                                      start=k == 0, stop=k == KD - 1)
            act.wait(pe.done(mm))
            e = act.done(nc.scalar.activation(gl[:, m, g * 512:(g + 1) * 512], bank, ACT.Gelu))
            ring.release(n, e)
            return e

        n, bank, _ = misc.take()
        pe.wait(kd_ready)
        e = pe.done(self.transpose(bank[:, 0:P], kdiag))
        act.wait(e)
        kT_ready = act.done(nc.scalar.activation(kT, bank[:, 0:P], ACT.Copy))
        misc.release(n, kT_ready)
        gelus = [(g, m) for g in range(4) for m in range(2)]
        for step in gelus[:3]:
            gelu(*step)
        dve.wait(st_ready)
        for m in range(QT):
            e = dve.done(V.bn_aggr(qmv[:, m, :], qst[:, m, :, :].rearrange("p g s -> p (g s)")))
        dve.wait(e)
        e = dve.done(V.tensor_tensor(ex2, qmv[:, :, 0:1], qmv[:, :, 0:1], ALU.mult))
        dve.wait(e)
        e = dve.done(V.tensor_tensor(qmv[:, :, 1:2], qmv[:, :, 1:2], ex2, ALU.add))
        n, bank, freed = misc.take()
        pe.wait(e, pm_ready, *events_of(freed))
        for m in range(QT):
            mm = nc.tensor.matmul(bank[:, 0:2], pairm, qmv[:, m, :], start=m == 0, stop=m == QT - 1)
        dve.wait(pe.done(mm))
        for step in gelus[3:]:
            gelu_ready = gelu(*step)
        e = dve.done(V.tensor_copy(mom, bank[:, 0:2]))
        misc.release(n, e)
        dve.wait(e)
        e = dve.done(V.tensor_tensor(var, mom[:, 0:1], mom[:, 0:1], ALU.mult))
        dve.wait(e)
        e = dve.done(V.tensor_tensor(var, mom[:, 1:2], var, ALU.subtract))
        dve.wait(e)
        e = dve.done(V.tensor_scalar(var, var, EPS, None, ALU.add))
        pool.wait(e)
        e = pool.done(G.tensor_tensor(var, var, self.half_power[:, 0:1], ALU.pow))
        dve.wait(e)
        e = dve.done(V.tensor_tensor(sc, var, gamma, ALU.mult))
        dve.wait(e)
        e = dve.done(V.tensor_tensor(sh, mom[:, 0:1], sc, ALU.mult))
        dve.wait(e)
        sh_ready = dve.done(V.tensor_tensor(sh, beta, sh, ALU.subtract))

        s_buf = [self.tmp("scores", [P, NG, NKEY]) for _ in range(2)]
        qn = [self.tmp("queries_normed", [P, QT, P]) for _ in range(2)]
        sq = [self.tmp("q_squares", [P, QT, P]) for _ in range(2)]
        eq, gt = self.tmp("equals_kth", [P, NG, NKEY]), self.tmp("greater", [P, NG, NKEY])
        cnt, ex = self.tmp("equal_count", [P, NG, NKEY]), self.tmp("exponentials", [P, NG, NKEY])
        inv, v8 = [self.tmp("inv_norm", [P, NG]) for _ in range(2)], self.tmp("top8", [P, NG, 8])
        g4, need, zsum = self.tmp("greater4", [P, NG, 4]), self.tmp("need", [P, NG]), self.tmp("exp_sum", [P, NG])
        prod = [self.tmp("expert_weight_parts", [P, QH, D]) for _ in range(2)]
        restw = [self.tmp("rest_weight", [P, 1]) for _ in range(2)]
        wgT = self.tmp("weighted_T", [P, 2, P])
        spread = lambda m: m[:, :, None].to_broadcast([P, NG, NKEY])
        flat = lambda m: m.rearrange("p g k -> p (g k)")
        s_banks, n_bank = Ring(self.banks[0:2]), Ring(self.banks[2:4])
        rows_i = D // NKEY
        sq_read, inv_ready, banks, weights_ready, prod_ready, prod_read, used = {}, {}, {}, {}, {}, {}, {}
        turned, wgT_read, exp_read = {}, {}, {}

        def tile_scores(b):
            ts, c = slice(b * P, (b + 1) * P), b % 2
            act.wait(sh_ready, sq_read.get(b - 2))
            qn_ready = act.done(nc.scalar.activation(qn[c], q[:, :, ts], ACT.Identity, scale=sc, bias=sh))
            act.wait(qn_ready)
            sq_ready = act.done(nc.scalar.activation(sq[c], qn[c], ACT.Square))
            n1, sbank, f1 = s_banks.take()
            n2, nbank, f2 = n_bank.take()
            pe.wait(qn_ready, kT_ready, *events_of(f1))
            for m in range(QT):
                mm = nc.tensor.matmul(sbank[:, m * P:(m + 1) * P], qn[c][:, m, :], kT, start=True, stop=True)
            pe.wait(sq_ready, b32_ready, *events_of(f2))
            for m in range(QT):
                mm = nc.tensor.matmul(nbank[:, m * 4:(m + 1) * 4], sq[c][:, m, :], blocks32, start=True, stop=True)
            sq_read[b] = pe.done(mm)
            banks[b] = (n1, sbank, n2, nbank)

        def tile_norms(b):
            _, _, n2, nbank = banks[b]
            dve.wait(sq_read[b])
            e = dve.done(V.tensor_scalar(inv[b % 2], nbank[:, 0:NG], 1e-24, None, ALU.max))
            n_bank.release(n2, e)
            pool.wait(e)
            inv_ready[b] = pool.done(G.tensor_tensor(inv[b % 2], inv[b % 2], self.half_power[:, 0:1].to_broadcast([P, NG]), ALU.pow))

        def tile_choice(b):
            c = b % 2
            n1, sbank, _, _ = banks[b]
            s = s_buf[c]
            dve.wait(inv_ready[b], sq_read[b], used.get(b - 2))
            e = dve.done(V.tensor_tensor(s, sbank.rearrange("p (g k) -> p g k", k=NKEY), spread(inv[c]), ALU.mult))
            s_banks.release(n1, e)
            dve.wait(e)
            for g in range(NG):
                e = dve.done(V.max(v8[:, g, :], s[:, g, :]))
            dve.wait(e)
            kth = v8[:, :, TOPK - 1:TOPK]
            kth_all = kth.to_broadcast([P, NG, NKEY])
            pool.wait(e, exp_read.get(b - 1))
            e4 = pool.done(G.tensor_tensor(ex, s, v8[:, :, 0:1].to_broadcast([P, NG, NKEY]), ALU.subtract))
            act.wait(e4)
            ex_ready = act.done(nc.scalar.activation(ex, ex, ACT.Exp))
            e1 = dve.done(V.tensor_tensor(eq, s, kth_all, ALU.is_equal))
            e3 = dve.done(V.tensor_tensor(g4, v8[:, :, 0:TOPK], kth.to_broadcast([P, NG, TOPK]), ALU.is_gt))
            e2 = dve.done(V.tensor_tensor(gt, s, kth_all, ALU.is_gt))
            dve.wait(e3)
            e3 = dve.done(V.tensor_reduce(need, g4, AX.X, ALU.add))
            if b + 1 < B:
                tile_norms(b + 1)
            dve.wait(e3)
            e3 = dve.done(V.tensor_scalar(need, need, -1.0, float(TOPK), ALU.mult, ALU.add))
            dve.wait(e1)
            e = dve.done(V.tensor_tensor_scan(flat(cnt), flat(reset), flat(eq), 0.0, ALU.mult, ALU.add))
            dve.wait(e, e3)
            e = dve.done(V.tensor_tensor(cnt, cnt, spread(need), ALU.is_le))
            dve.wait(e)
            e = dve.done(V.tensor_tensor(eq, eq, cnt, ALU.mult))
            dve.wait(e, e2)
            e = dve.done(V.tensor_tensor(gt, gt, eq, ALU.add))
            dve.wait(e, ex_ready)
            e = exp_read[b] = dve.done(V.tensor_tensor(s, ex, gt, ALU.mult))
            dve.wait(e)
            e = dve.done(V.tensor_reduce(zsum, s, AX.X, ALU.add))
            dve.wait(e)
            e = dve.done(V.reciprocal(zsum, zsum))
            pool.wait(e)
            weights_ready[b] = pool.done(G.tensor_tensor(s, s, spread(zsum), ALU.mult))

        def tile_products(b):
            halves = s_buf[b % 2].rearrange("p (h c) k -> p c h k", c=2)
            first = halves[:, 0, :, 0:rows_i][:, :, :, None].to_broadcast([P, QH, rows_i, NKEY])
            second = halves[:, 1][:, :, None, :].to_broadcast([P, QH, rows_i, NKEY])
            pool.wait(weights_ready[b], prod_read.get(b - 2))
            used[b] = pool.done(G.tensor_tensor(
                prod[b % 2].rearrange("p h (i j) -> p h i j", i=rows_i), first, second, ALU.mult))

        def tile_rest(b):
            halves = s_buf[b % 2].rearrange("p (h c) k -> p c h k", c=2)
            dve.wait(weights_ready[b], prod_ready.get(b - 2))
            rest_ready = dve.done(V.tensor_reduce(restw[b % 2], halves[:, 0, :, rows_i:], AX.XY, ALU.add))
            last_row = prod[b % 2][:, 0, D - 1:D]
            pool.wait(used[b], rest_ready)
            prod_ready[b] = pool.done(G.tensor_tensor(last_row, last_row, restw[b % 2], ALU.add))

        def tile_experts(b):
            n, bank, freed = misc.take()
            pe.wait(prod_ready[b], *events_of(freed))
            for k in range(2):
                for h in range(QH):
                    mm = nc.tensor.matmul(bank[:, k * P:(k + 1) * P], prod[b % 2][:, h, k * P:(k + 1) * P], self.ident,
                                          start=h == 0, stop=h == QH - 1)
            prod_read[b] = pe.done(mm)
            dve.wait(prod_read[b], gelu_ready, wgT_read.get(b - 1))
            turned[b] = dve.done(V.tensor_tensor(wgT, bank[:, 0:2 * P].rearrange("p (k t) -> p k t", k=2),
                                                 gl[:, :, b * P:(b + 1) * P], ALU.mult))
            misc.release(n, turned[b])

        def tile_out(b):
            n, bank, freed = misc.take()
            pe.wait(turned[b], *events_of(freed))
            for k in range(2):
                mm = nc.tensor.matmul(bank[:, 0:D], wgT[:, k, :], up[:, k, :], start=k == 0, stop=k == 1)
            wgT_read[b] = pe.done(mm)
            misc.release(n, self.update(b, bank[:, 0:D], 7, wgT_read[b]))

        s_banks.release(0, gelu_ready)
        s_banks.release(1, gelu_ready)
        n_bank.release(0, gelu_ready)
        n_bank.release(1, gelu_ready)
        tile_scores(0)
        tile_norms(0)
        for t in range(B + 2):
            if t + 1 < B:
                tile_scores(t + 1)
            if t < B:
                tile_choice(t)
            if t < B:
                tile_products(t)
            if t >= 2:
                tile_out(t - 2)
                self.store_out(t - 2)
            if 1 <= t <= B:
                tile_experts(t - 1)
            if t < B:
                tile_rest(t)

    def update(self, b, y, gate, *after):
        self.dve.wait(self.x_ready[b], *after)
        self.x_ready[b] = self.dve.done(self.nc.vector.scalar_tensor_tensor(
            self.x[:, b, :], y, self.gates[:, gate:gate + 1], self.x[:, b, :], ALU.mult, ALU.add))
        return self.x_ready[b]

    def store_out(self, b):
        self.sp.wait(self.x_ready[b])
        self.stored = self.stores.of(self.nc.sync.dma_start(self.out[b], self.x[:, b, :]))

    def finish(self):
        self.sp.wait(self.stored)


def program(nc, d, out):
    core = Core(nc, d, out)
    core.constants()
    core.first_layernorm()
    core.attention(0, 16, 4, 0.25, True, None, lambda: (core.slot_bias_parts(), core.load_moe(0, I0)))
    core.moe(0, E0, I0, 1)
    core.attention(1, 16, 4, 0.25, True, "pairs", lambda: core.load_moe(1, I1))
    core.moe(1, E1, I1, 2)
    core.attention(2, 16, 4, 0.25, True, None, core.load_phi)
    core.soft_moe()
    core.attention(3, 64, 2, 0.125, False, "keys", core.load_peer)
    core.peer()
    core.finish()


def laid_out(x):
    a = {k: np.asarray(v) for k, v in x.items()}
    rows = lambda w: np.ascontiguousarray(w.reshape(-1, P, w.shape[-1]).transpose(1, 0, 2))
    column = lambda v: np.ascontiguousarray(v.reshape(-1, P).T)
    d = {"x": a["x"], "g_xattn": a["g_xattn"][None], "g_ffn": a["g_ffn"][None]}
    d["ctxT"] = rows(np.ascontiguousarray(a["ctx_1024"].reshape(T, D).T))
    d["mask_keys"] = a["mask_BxS2_bk0"].reshape(1, T)
    d["rel"] = a["fside_Bx1xSxS2_0"][:, 0]
    d["relT"] = np.ascontiguousarray(d["rel"].transpose(0, 2, 1))
    keep = a["mask_BxSxS2_bk0"]
    d["keep"] = keep
    d["keepT"] = np.ascontiguousarray(keep.transpose(0, 2, 1))
    for n, out_name in ((0, "o"), (1, "out"), (2, "o")):
        for name in ("q", "k", "v", out_name):
            w = a[f"L{n}_xattn_W{name}"]
            short = name[0]
            w = w if n == 0 else w.T
            b = a[f"L{n}_xattn_b{name}"]
            if short in "qk":
                w = w.reshape(D, HEADS, -1).transpose(0, 2, 1).reshape(D, D)
                b = np.ascontiguousarray(b.reshape(HEADS, -1).T).reshape(D)
            d[f"L{n}_W{short}"] = rows(np.ascontiguousarray(w))
            d[f"L{n}_b{short}"] = column(b) if short in "qk" else b[None]
    for name in "QKVO":
        d[f"L3_W{name.lower()}"] = rows(a[f"L3_xattn_W_{name}"])

    def experts(gate, up, down):
        n, inter, _ = gate.shape
        both = np.stack([gate, up], 1).reshape(n, 2, inter, KD, P).transpose(0, 4, 3, 1, 2).reshape(n, P, -1)
        chunks = -(-inter // P)
        low = np.zeros((n, chunks * P, D), down.dtype)
        low[:, :inter] = down.transpose(0, 2, 1)
        low = low.reshape(n, chunks, P, D).transpose(0, 2, 1, 3).reshape(n, P, -1)
        return np.concatenate([both, low], 2).reshape(n * P, -1)

    d["L0_experts"] = experts(a["L0_ffn_gate_w"], a["L0_ffn_up_w"], a["L0_ffn_down_w"])
    d["L1_experts"] = experts(a["L1_ffn_w1"], a["L1_ffn_w3"], a["L1_ffn_w2"])
    d["L1_shared"] = experts(a["L1_ffn_sw1"][None], a["L1_ffn_sw3"][None], a["L1_ffn_sw2"][None])
    d["L0_router"] = rows(np.ascontiguousarray(a["L0_ffn_router_w"].T))
    d["L1_router"] = rows(np.ascontiguousarray(a["L1_ffn_gate_w"].T))
    d["L1_gate_bias"] = a["L1_ffn_gate_bias"][None]
    d["phiT"] = rows(np.ascontiguousarray(a["L2_ffn_phi_w"].T))
    d["phi_b"] = a["L2_ffn_phi_b"][None]
    d["expert_w"] = np.ascontiguousarray(a["L2_ffn_expert_w"].reshape(ST, 4, KD, P, D).transpose(0, 3, 1, 2, 4))
    d["expert_b"] = np.ascontiguousarray(a["L2_ffn_expert_b"].reshape(ST, 4, D).transpose(1, 0, 2))
    d["L3f_Wq"] = rows(a["L3_ffn_Wq"])
    d["L3f_bq"] = column(a["L3_ffn_bq"])
    d["L3f_gamma"], d["L3f_beta"] = a["L3_ffn_bn_gamma"][:, None], a["L3_ffn_bn_beta"][:, None]
    d["key0"], d["key1"] = a["L3_ffn_sub_key0"], a["L3_ffn_sub_key1"]
    d["downT"] = rows(np.ascontiguousarray(a["L3_ffn_expert_down"].T))
    d["up"] = rows(a["L3_ffn_expert_up"])
    return d


def kernel(**inputs):
    import concourse.bacc as _bacc
    from concourse.bass_utils import run_bass_kernel_spmd as _run

    nc = _bacc.Bacc("TRN2", target_bir_lowering=False, num_devices=1)
    arrays = laid_out(inputs)
    d = {k: nc.dram_tensor(f"in_{k}", list(v.shape), mybir.dt.from_np(v.dtype), kind="ExternalInput").ap()
         for k, v in arrays.items()}
    out = nc.dram_tensor("out", [B, S, D], F32, kind="ExternalOutput").ap()
    program(nc, d, out)
    r = _run(nc, [{f"in_{k}": v for k, v in arrays.items()}], core_ids=[0])
    return r.results[0]["out"]
```
